# Optimizing a Trainium2 kernel written in Bass

```python
import numpy as np
import jax
import jax.numpy as jnp

def _softmax(x, axis=-1):
    return jax.nn.softmax(x, axis=axis)

def _gelu(x):
    return jax.nn.gelu(x, approximate=True)

def _silu(x):
    return jax.nn.silu(x)

def _sigmoid(x):
    return jax.nn.sigmoid(x)

def _layernorm(x, axis=-1, eps=1e-05):
    m = jnp.mean(x, axis=axis, keepdims=True)
    v = jnp.var(x, axis=axis, keepdims=True)
    return (x - m) / jnp.sqrt(v + eps)

def _scatter_add(tgt, idx, src, axis=0):
    return tgt.at[idx].add(src)

def _segment_sum(src, seg, n):
    return jax.ops.segment_sum(src, seg, n)
kernel_name = 'mk_recurrent_d2_jaxref_r4_b86448'

def setup_inputs(seed: int=0):
    np.random.seed(seed)
    _w = jnp.asarray

    def _L0_attn_setup():
        import jax, jax.numpy as jnp
        import numpy as np
        D_MODEL = 256
        N_HEADS = 16
        HEAD_DIM = D_MODEL // N_HEADS
        ROPE_BASE = 10000.0

        def _rope(q, k):
            S, Dh = (q.shape[1], q.shape[-1])
            inv_freq = 1.0 / ROPE_BASE ** (jnp.arange(0, Dh, 2, dtype=jnp.float32) / Dh)
            t = jnp.arange(S, dtype=jnp.float32)
            freqs = jnp.outer(t, inv_freq)
            emb = jnp.concatenate([freqs, freqs], axis=-1)
            cos = jnp.cos(emb)[None, :, None, :]
            sin = jnp.sin(emb)[None, :, None, :]

            def rotate_half(v):
                v1, v2 = (v[..., :Dh // 2], v[..., Dh // 2:])
                return jnp.concatenate([-v2, v1], axis=-1)
            return (q * cos + rotate_half(q) * sin, k * cos + rotate_half(k) * sin)
        key = jax.random.key(seed)
        ks = jax.random.split(key, 5)
        B, S = (1, 1024)
        scale = 1.0 / np.sqrt(D_MODEL)
        x = jax.random.normal(ks[0], (B, S, D_MODEL), dtype=jnp.float32)
        Wq = jax.random.normal(ks[1], (D_MODEL, D_MODEL), dtype=jnp.float32) * scale
        Wk = jax.random.normal(ks[2], (D_MODEL, D_MODEL), dtype=jnp.float32) * scale
        Wv = jax.random.normal(ks[3], (D_MODEL, D_MODEL), dtype=jnp.float32) * scale
        Wo = jax.random.normal(ks[4], (D_MODEL, D_MODEL), dtype=jnp.float32) * scale
        return {'x': x, 'Wq': Wq, 'Wk': Wk, 'Wv': Wv, 'Wo': Wo}
    _L0_attn_in = _L0_attn_setup()

    def _L0_ffn_setup():
        import jax, jax.numpy as jnp
        import numpy as np
        B, SEQ, DIM = (2, 1024, 256)
        E, S = (8, 128)
        HID = 4 * DIM
        SCALE = DIM ** 0.5

        def rmsnorm(x, gamma):
            n = jnp.linalg.norm(x, axis=-1, keepdims=True)
            return x / jnp.maximum(n, 1e-12) * SCALE * gamma
        key = jax.random.key(seed)
        ks = jax.random.split(key, 4)
        w_init = lambda k, shape: jax.random.normal(k, shape, dtype=jnp.float32) * 0.02
        return {'x': jax.random.normal(ks[0], (B, SEQ, DIM), dtype=jnp.float32), 'norm_gamma': jnp.ones((DIM,), jnp.float32), 'slot_norm_gamma': jnp.ones((DIM,), jnp.float32), 'slot_embeds': jax.random.normal(ks[1], (E, S, DIM), dtype=jnp.float32), 'w1': w_init(ks[2], (E, DIM, HID)), 'b1': jnp.zeros((E, HID), jnp.float32), 'w2': w_init(ks[3], (E, HID, DIM)), 'b2': jnp.zeros((E, DIM), jnp.float32)}
    _L0_ffn_in = _L0_ffn_setup()

    def _L1_attn_setup():
        import jax, jax.numpy as jnp
        import numpy as np
        H_HEADS = 16
        SEG = 64
        EPS = 1e-06
        key = jax.random.key(seed)
        ks = jax.random.split(key, 6)
        B, T, D = (2, 1024, 256)
        sc = 1.0 / np.sqrt(D)
        return {'x': jax.random.normal(ks[0], (B, T, D), jnp.float32), 'norm_w': jnp.ones((D,), jnp.float32), 'Wq': jax.random.normal(ks[1], (D, D), jnp.float32) * sc, 'Wk': jax.random.normal(ks[2], (D, D), jnp.float32) * sc, 'Wv': jax.random.normal(ks[3], (D, D), jnp.float32) * sc, 'Wo': jax.random.normal(ks[4], (D, D), jnp.float32) * sc, 'Wu': jax.random.normal(ks[5], (D, D), jnp.float32) * sc}
    _L1_attn_in = _L1_attn_setup()

    def _L1_ffn_setup():
        import jax, jax.numpy as jnp
        import numpy as np
        D_MODEL, D_FF, D2, DL = (256, 1024, 64, 64)
        D1 = D_FF // D2
        BATCH, SEQ = (2, 256)
        KERNEL_SCALE = D2 ** 0.5
        key = jax.random.key(seed)
        ks = jax.random.split(key, 7)
        xav = lambda k, shape, fan: jax.random.normal(k, shape, jnp.float32) * (2.0 / sum(fan)) ** 0.5
        x = jax.random.normal(ks[0], (BATCH, SEQ, D_MODEL), jnp.float32)
        m1 = xav(ks[1], (D_MODEL, DL), (D_MODEL, DL))
        m2 = xav(ks[2], (DL, D1, D2), (DL, D_FF))
        mb = jax.random.normal(ks[3], (D1, D2), jnp.float32)
        w1 = xav(ks[4], (D_MODEL, D1, D2), (D_MODEL, D_FF))
        w2 = xav(ks[5], (D2, D1, D_MODEL), (D_FF, D_MODEL)) * KERNEL_SCALE
        b2 = jax.random.normal(ks[6], (D_MODEL,), jnp.float32)
        return {'x': x, 'm1': m1, 'm2': m2, 'mb': mb, 'w1': w1, 'w2': w2, 'b2': b2}
    _L1_ffn_in = _L1_ffn_setup()
    _d = {'L0_attn_x': _L0_attn_in['x'], 'L0_attn_Wq': _L0_attn_in['Wq'], 'L0_attn_Wk': _L0_attn_in['Wk'], 'L0_attn_Wv': _L0_attn_in['Wv'], 'L0_attn_Wo': _L0_attn_in['Wo'], 'L0_ffn_norm_gamma': _L0_ffn_in['norm_gamma'], 'L0_ffn_slot_norm_gamma': _L0_ffn_in['slot_norm_gamma'], 'L0_ffn_slot_embeds': _L0_ffn_in['slot_embeds'], 'L0_ffn_w1': _L0_ffn_in['w1'], 'L0_ffn_b1': _L0_ffn_in['b1'], 'L0_ffn_w2': _L0_ffn_in['w2'], 'L0_ffn_b2': _L0_ffn_in['b2'], 'L1_attn_norm_w': _L1_attn_in['norm_w'], 'L1_attn_Wq': _L1_attn_in['Wq'], 'L1_attn_Wk': _L1_attn_in['Wk'], 'L1_attn_Wv': _L1_attn_in['Wv'], 'L1_attn_Wo': _L1_attn_in['Wo'], 'L1_attn_Wu': _L1_attn_in['Wu'], 'L1_ffn_m1': _L1_ffn_in['m1'], 'L1_ffn_m2': _L1_ffn_in['m2'], 'L1_ffn_mb': _L1_ffn_in['mb'], 'L1_ffn_w1': _L1_ffn_in['w1'], 'L1_ffn_w2': _L1_ffn_in['w2'], 'L1_ffn_b2': _L1_ffn_in['b2']}
    _x0 = _d['L0_attn_x']
    _d['L0_attn_x'] = jax.random.normal(jax.random.fold_in(jax.random.key(seed), 1), (8, 1024, 256), dtype=_x0.dtype)
    del _x0
    return _d

def reference(L0_attn_x, L0_attn_Wq, L0_attn_Wk, L0_attn_Wv, L0_attn_Wo, L0_ffn_norm_gamma, L0_ffn_slot_norm_gamma, L0_ffn_slot_embeds, L0_ffn_w1, L0_ffn_b1, L0_ffn_w2, L0_ffn_b2, L1_attn_norm_w, L1_attn_Wq, L1_attn_Wk, L1_attn_Wv, L1_attn_Wo, L1_attn_Wu, L1_ffn_m1, L1_ffn_m2, L1_ffn_mb, L1_ffn_w1, L1_ffn_w2, L1_ffn_b2):

    def _L0_attn_ref(x, Wq, Wk, Wv, Wo):
        import jax, jax.numpy as jnp
        import numpy as np
        D_MODEL = 256
        N_HEADS = 16
        HEAD_DIM = D_MODEL // N_HEADS
        ROPE_BASE = 10000.0

        def _rope(q, k):
            S, Dh = (q.shape[1], q.shape[-1])
            inv_freq = 1.0 / ROPE_BASE ** (jnp.arange(0, Dh, 2, dtype=jnp.float32) / Dh)
            t = jnp.arange(S, dtype=jnp.float32)
            freqs = jnp.outer(t, inv_freq)
            emb = jnp.concatenate([freqs, freqs], axis=-1)
            cos = jnp.cos(emb)[None, :, None, :]
            sin = jnp.sin(emb)[None, :, None, :]

            def rotate_half(v):
                v1, v2 = (v[..., :Dh // 2], v[..., Dh // 2:])
                return jnp.concatenate([-v2, v1], axis=-1)
            return (q * cos + rotate_half(q) * sin, k * cos + rotate_half(k) * sin)
        B, S, _ = x.shape
        H, Dh = (N_HEADS, HEAD_DIM)
        q = (x @ Wq.T).reshape(B, S, H, Dh)
        k = (x @ Wk.T).reshape(B, S, H, Dh)
        v = (x @ Wv.T).reshape(B, S, H, Dh)
        q, k = _rope(q, k)
        scale = 1.0 / np.sqrt(Dh)
        scores = jnp.einsum('bqhd,bkhd->bhqk', q, k) * scale
        causal = jnp.triu(jnp.ones((S, S), dtype=bool), k=1)
        scores = jnp.where(causal, -jnp.inf, scores)
        attn = jax.nn.softmax(scores, axis=-1)
        out = jnp.einsum('bhqk,bkhd->bqhd', attn, v).reshape(B, S, H * Dh)
        return out @ Wo.T

    def _L0_ffn_ref(x, norm_gamma, slot_norm_gamma, slot_embeds, w1, b1, w2, b2):
        import jax, jax.numpy as jnp
        import numpy as np
        B, SEQ, DIM = (2, 1024, 256)
        E, S = (8, 128)
        HID = 4 * DIM
        SCALE = DIM ** 0.5

        def rmsnorm(x, gamma):
            n = jnp.linalg.norm(x, axis=-1, keepdims=True)
            return x / jnp.maximum(n, 1e-12) * SCALE * gamma
        xn = rmsnorm(x, norm_gamma)
        sn = rmsnorm(slot_embeds, slot_norm_gamma)
        logits = jnp.einsum('bnd,esd->bnes', xn, sn)
        dispatch = jax.nn.softmax(logits, axis=1)
        b, n, e, s = logits.shape
        combine = jax.nn.softmax(logits.reshape(b, n, e * s), axis=-1)
        slots = jnp.einsum('bnd,bnes->besd', xn, dispatch)
        h = jnp.einsum('besd,edh->besh', slots, w1) + b1[None, :, None, :]
        h = jax.nn.gelu(h, approximate=False)
        eo = jnp.einsum('besh,ehd->besd', h, w2) + b2[None, :, None, :]
        eo = eo.reshape(b, e * s, DIM)
        out = jnp.einsum('bmd,bnm->bnd', eo, combine)
        return out

    def _L1_attn_ref(x, norm_w, Wq, Wk, Wv, Wo, Wu):
        import jax, jax.numpy as jnp
        import numpy as np
        H_HEADS = 16
        SEG = 64
        EPS = 1e-06
        B, T, D = x.shape
        H = H_HEADS
        dk = D // H
        N = T // SEG
        xn = x * jax.lax.rsqrt(jnp.mean(x * x, axis=-1, keepdims=True) + EPS) * norm_w

        def proj(W):
            return (xn @ W.T).reshape(B, T, H, dk)
        q, k, v = (proj(Wq), proj(Wk), proj(Wv))
        pq = jax.nn.elu(q) + 1.0
        pk = jax.nn.elu(k) + 1.0
        pqc = pq.reshape(B, N, SEG, H, dk)
        pkc = pk.reshape(B, N, SEG, H, dk)
        vc = v.reshape(B, N, SEG, H, dk)
        S_chunk = jnp.einsum('bnchk,bnchv->bnhkv', pkc, vc)
        S_cum = jnp.cumsum(S_chunk, axis=1)
        S_excl = S_cum - S_chunk
        boundary_states = S_cum
        inter = jnp.einsum('bnchk,bnhkv->bnchv', pqc, S_excl)
        tri = jnp.tril(jnp.ones((SEG, SEG), x.dtype))
        A = jnp.einsum('bnchk,bndhk->bnhcd', pqc, pkc) * tri
        intra = jnp.einsum('bnhcd,bndhv->bnchv', A, vc)
        zk = pkc.sum(axis=2)
        z_excl = jnp.cumsum(zk, axis=1) - zk
        z = z_excl[:, :, None] + jnp.cumsum(pkc, axis=2)
        denom = jnp.einsum('bnchk,bnchk->bnch', pqc, z) + EPS
        attn_out = ((inter + intra) / denom[..., None]).reshape(B, T, D) @ Wo.T
        x_out = x + attn_out
        xc = x.reshape(B, N, SEG, D)
        m_stack = xc.mean(axis=2)
        counts = jnp.arange(1, SEG + 1, dtype=x.dtype)[None, None, :, None]
        m_current = (jnp.cumsum(xc, axis=2) / counts).reshape(B, T, D)
        causal_mask = (jnp.arange(T) // SEG)[:, None] > jnp.arange(N)[None, :]
        u = x @ Wu.T
        scale = 1.0 / jnp.sqrt(jnp.asarray(D, x.dtype))
        sc_cached = jnp.einsum('btd,bnd->btn', u, m_stack) * scale
        sc_cached = jnp.where(causal_mask[None], sc_cached, -jnp.inf)
        sc_cur = jnp.sum(u * m_current, axis=-1, keepdims=True) * scale
        attn_w = jax.nn.softmax(jnp.concatenate([sc_cached, sc_cur], axis=-1), axis=-1)
        gates_cached = attn_w[..., :N]
        gate_current = attn_w[..., N:]
        h_retrieved = jnp.einsum('btn,bthk,bnhkv->bthv', gates_cached, pq, boundary_states).reshape(B, T, D)
        retrieval_scale = 1.0
        return gate_current * x_out + retrieval_scale * h_retrieved

    def _L1_ffn_ref(x, m1, m2, mb, w1, w2, b2):
        import jax, jax.numpy as jnp
        import numpy as np
        D_MODEL, D_FF, D2, DL = (256, 1024, 64, 64)
        D1 = D_FF // D2
        BATCH, SEQ = (2, 256)
        KERNEL_SCALE = D2 ** 0.5
        x_shape = x.shape
        xf = x.reshape(-1, x_shape[-1])
        d1 = w1.shape[1]
        lr = xf @ m1
        mask_logits = jnp.einsum('bl,lxy->bxy', lr, m2) + mb
        quant_mask = jnp.argmax(mask_logits, axis=-1)
        w1p = jnp.transpose(w1, (1, 2, 0))
        w2p = jnp.transpose(w2, (1, 0, 2))
        j = jnp.arange(d1)[None, :]
        w = w1p[j, quant_mask]
        mid = jnp.einsum('ai,aji->aj', xf, w)
        relu = jax.nn.relu(mid)
        v = w2p[j, quant_mask]
        res = jnp.einsum('ai,aij->aj', relu, v) + b2
        return res.reshape(x_shape)
    x = L0_attn_x
    xn = _layernorm(x, axis=-1)
    s = _L0_attn_ref(xn, L0_attn_Wq, L0_attn_Wk, L0_attn_Wv, L0_attn_Wo)
    g = _silu(_L0_ffn_ref(xn, L0_ffn_norm_gamma, L0_ffn_slot_norm_gamma, L0_ffn_slot_embeds, L0_ffn_w1, L0_ffn_b1, L0_ffn_w2, L0_ffn_b2))
    x = x + s * g
    xn = _layernorm(x, axis=-1)
    s = _L1_attn_ref(xn, L1_attn_norm_w, L1_attn_Wq, L1_attn_Wk, L1_attn_Wv, L1_attn_Wo, L1_attn_Wu)
    g = _silu(_L1_ffn_ref(xn, L1_ffn_m1, L1_ffn_m2, L1_ffn_mb, L1_ffn_w1, L1_ffn_w2, L1_ffn_b2))
    x = x + s * g
    return x

_drawn_inputs = setup_inputs


def setup_inputs(seed=0):
    import zlib

    import numpy as np

    out = dict(_drawn_inputs(seed))
    spreads = {'L0_ffn_norm_gamma': (1.0, 0.2),
     'L0_ffn_slot_norm_gamma': (1.0, 0.6),
     'L0_ffn_b1': (0.0, 0.462),
     'L0_ffn_b2': (0.0, 0.1),
     'L1_attn_norm_w': (1.0, 0.2)}
    factors = {'L1_attn_Wo': 200.0}
    for name, (base, spread) in spreads.items():
        noise = np.random.default_rng([zlib.crc32(name.encode()), seed]).standard_normal(out[name].shape)
        drawn = base * np.exp(spread * noise) if base else spread * noise
        out[name] = jnp.asarray(drawn.astype(out[name].dtype))
    for name, factor in factors.items():
        out[name] = (out[name] * factor).astype(out[name].dtype)
    return out
```

```python
from contextlib import ExitStack

import concourse.bass as bass
from concourse import mybir

F32 = mybir.dt.float32
BF16 = mybir.dt.bfloat16
ALU = mybir.AluOpType
ACT = mybir.ActivationFunctionType
AX = mybir.AxisListType

P = 128
B, T, D = 8, 1024, 256
TILES = T // P
ALL = B * TILES
H, DH = 16, 16
G = 4
STEPS = B * H // G
VP = 32
LN_EPS, RMS_EPS = 1e-5, 1e-6
NEG = -1e30


class Chain:

    def __init__(self, eng, sem):
        self.eng, self.sem, self.base, self.n = eng, sem, 0, 0

    def start(self, base):
        self.base, self.n = base, 0

    def link(self, ins):
        self.n += 1
        ins.then_inc(self.sem, 1)
        self.eng.wait_ge(self.sem, self.base + self.n)


class Event:

    def __init__(self, sem, unit, credit):
        self.sem, self.unit, self.credit = sem, unit, credit

    def __call__(self, n):
        return self.sem, (n + self.credit) * self.unit


class Phase:

    def __init__(self, nc, tag):
        self.nc, self.tag, self.ctx = nc, tag, ExitStack()
        self.events = []

    def __enter__(self):
        self.ctx.enter_context(self.nc.cleanup_on_exit())
        return self

    def __exit__(self, *exc):
        return self.ctx.__exit__(*exc)

    def sb(self, name, shape, dt=F32):
        return self.ctx.enter_context(self.nc.sbuf_tensor(f"{self.tag}_{name}", shape, dt))

    def ps(self, name, shape, dt=F32):
        return self.ctx.enter_context(self.nc.psum_tensor(f"{self.tag}_{name}", shape, dt))

    def sem(self, name):
        return self.nc.alloc_semaphore(name=f"{self.tag}_{name}")

    def event(self, name, unit=1, credit=2):
        e = Event(self.sem(name), unit, credit)
        self.events.append(e)
        return e

    def give_credits(self, eng):
        for e in self.events:
            if e.credit:
                eng.sem_inc(e.sem, e.unit * e.credit)

    def block(self):
        return self.ctx.enter_context(self.nc.Block())


def staggered(eng, n, stages, R=2):
    lead = -(-max(lag for lag, _ in stages) // R)

    def rounds(k):
        for u in range(R):
            for lag, fn in stages:
                kk, uu = k + (u - lag) // R, (u - lag) % R
                if isinstance(k, int) and not 0 <= kk * R + uu < n:
                    continue
                fn(kk * R + uu, kk, uu)

    for k in range(lead):
        rounds(k)
    with eng.Fori(lead, n // R) as k:
        rounds(k)
    for k in range(n // R, n // R + lead):
        rounds(k)


def project_rope(nc, x, w_qkv, gamma, cos_t, sin_t, eye, eye_bf, qk_parts, v_pad, xr, xr_t):
    with Phase(nc, "pr") as ph:
        x_n = x.rearrange("b (i p) d -> (b i) p d", p=P)
        ident = ph.sb("ident", [P, P])
        ident_bf = ph.sb("ident_bf", [P, P], BF16)
        w_t = ph.sb("w_t", [P, 2, 3 * D])
        gam = ph.sb("gam", [P, D])
        cos = ph.sb("cos", [P, TILES, DH])
        sin = ph.sb("sin", [P, TILES, DH])
        xt = ph.sb("xt", [P, 2, D])
        stat = ph.sb("stat", [P, 6])
        mv = ph.sb("mv", [P, 2])
        v2 = ph.sb("v2", [P, 2])
        sd = ph.sb("sd", [P, 2])
        rstd = ph.sb("rstd", [P, 1])
        nrm = ph.sb("nrm", [P, 1])
        rnr = ph.sb("rnr", [P, 1])
        srs = ph.sb("srs", [P, 1])
        xn = ph.sb("xn", [P, 2, D])
        xs = ph.sb("xs", [P, D])
        xrn = ph.sb("xrn", [P, 2, D])
        turn = ph.sb("turn", [P, 2, 4, P])
        qk = ph.sb("qk", [P, 2, 2 * D])
        ra = ph.sb("ra", [P, 2 * D])
        rb = ph.sb("rb", [P, 2 * D])
        roped = ph.sb("roped", [P, 2, 2 * D])
        rest = ph.sb("rest", [P, 2, 2 * D])
        parts = ph.sb("parts", [P, 2, 3, 2 * D], BF16)
        vp = ph.sb("vp", [P, 2, H, VP])
        part_t = ph.sb("part_t", [P, 1, 2, 3, 2, 2 * P], BF16)
        tr = ph.ps("tr", [P, 4, P])
        pqk = ph.ps("pqk", [P, 2 * D])
        pv = ph.ps("pv", [P, 512])
        tb = ph.ps("tb", [P, 2, 2, 4, P], BF16)

        const_in = ph.sem("const_in")
        preset = ph.sem("preset")
        loaded = [ph.event(f"loaded{u}", 16) for u in range(2)]
        x_read = ph.event("x_read")
        var_ready = ph.event("var_ready")
        sd_ready = ph.event("sd_ready")
        xn_ready = ph.event("xn_ready")
        xr_ready = ph.event("xr_ready")
        turned = ph.event("turned")
        turn_copied = ph.event("turn_copied")
        projected = ph.event("projected")
        qk_copied = ph.event("qk_copied")
        v_copied = ph.event("v_copied")
        rope_done = ph.event("rope_done")
        part0_done = ph.event("part0_done")
        rest_done = ph.event("rest_done")
        part1_done = ph.event("part1_done")
        part2_done = ph.event("part2_done")
        parts_turned = ph.event("parts_turned")
        parts_copied = ph.event("parts_copied")
        stored = [ph.event(f"stored{u}", 16 * (2 + G)) for u in range(2)]
        stored_qk = [ph.event("stored_qk", 6 * 16)]
        chain_v = ph.sem("chain_v")
        chain_g = ph.sem("chain_g")
        passed = ph.sem("passed")
        block = ph.block()
        PAIRS = ALL // 2
        VC, GC = 6, 3

        @block.sync
        def _(sp):
            for dst, src in ((ident[:, :], eye), (ident_bf[:, :], eye_bf),
                             (w_t[:, :, :], w_qkv.rearrange("(c p) n -> p c n", p=P)),
                             (gam[:, :], gamma.unsqueeze(0).broadcast_to((P, D))),
                             (cos[:, :, :], cos_t.rearrange("(i p) d -> p i d", p=P)),
                             (sin[:, :, :], sin_t.rearrange("(i p) d -> p i d", p=P))):
                sp.dma_start(dst, src).then_inc(const_in, 16)
            ph.give_credits(sp)
            for u in range(2):
                sp.dma_start(xt[:, u], x_n[u]).then_inc(loaded[u].sem, 16)

            def stores(b, j, u):
                k = b * (TILES // 2) + j
                t = k * 2 + u
                sp.wait_ge(*xr_ready(t + 1))
                sp.dma_start(xr[t], xrn[:, u]).then_inc(stored[u].sem, 16)
                sp.wait_ge(*turn_copied(t + 1))
                sp.dma_start(xr_t[t], turn[:, u, 2:4]).then_inc(stored[u].sem, 16)
                sp.wait_ge(*v_copied(t + 1))
                for g in range(G):
                    sp.dma_start(v_pad[b, j * 2 + u, g], vp[:, u, G * g:G * g + G]).then_inc(stored[u].sem, 16)

            def store_parts(b, j):
                k = b * (TILES // 2) + j
                sp.wait_ge(*parts_copied(k * 2 + 2))
                for qc in range(2):
                    for c in range(3):
                        sp.dma_start(qk_parts[b, j, qc, c].rearrange("(e p) t -> p e t", p=P),
                                     part_t[:, 0, qc, c]).then_inc(stored_qk[0].sem, 16)

            def pair(b, j, more=True):
                k = b * (TILES // 2) + j
                for u in range(2):
                    if more:
                        sp.wait_ge(*x_read(k * 2 + u + 1))
                        sp.dma_start(xt[:, u], x_n[k * 2 + u + 2]).then_inc(loaded[u].sem, 16)
                    stores(b, j, u)
                store_parts(b, j)

            with sp.Fori(0, B - 1) as b, sp.Fori(0, TILES // 2) as j:
                pair(b, j)
            with sp.Fori(0, TILES // 2 - 1) as j:
                pair(B - 1, j)
            pair(B - 1, TILES // 2 - 1, more=False)
            for u in range(2):
                sp.wait_ge(*stored[u](PAIRS))
            sp.wait_ge(*stored_qk[0](PAIRS))

        @block.gpsimd
        def _(gp):
            gp.memset(vp[:, :, :, :], 0.0).then_inc(chain_g, 1)
            gp.wait_ge(chain_g, 1)
            gp.memset(vp[:, :, :, DH:DH + 1], 1.0).then_inc(preset, 1)
            gp.wait_ge(const_in, 6 * 16)
            lo, hi = slice(0, DH // 2), slice(DH // 2, DH)
            ch = Chain(gp, chain_g)
            with gp.Fori(0, B) as b, gp.Fori(0, TILES // 2) as j:
                for u in range(2):
                    k = b * (TILES // 2) + j
                    t = k * 2 + u
                    i = j * 2 + u
                    ch.start(t * GC + 1)
                    heads = lambda a: a.rearrange("p (h d) -> p h d", d=DH)
                    qs, ah, bh = heads(qk[:, u]), heads(ra[:, :]), heads(rb[:, :])
                    gp.wait_ge(*qk_copied(t + 1))
                    gp.tensor_tensor(ah, qs, cos[:, bass.ds(i, 1), :].broadcast_to((P, 2 * H, DH)), ALU.mult) \
                        .then_inc(chain_g, 1)
                    gp.tensor_tensor(bh[:, :, lo], qs[:, :, hi],
                                     sin[:, bass.ds(i, 1), lo].broadcast_to((P, 2 * H, DH // 2)), ALU.mult) \
                        .then_inc(chain_g, 1)
                    gp.tensor_tensor(bh[:, :, hi], qs[:, :, lo],
                                     sin[:, bass.ds(i, 1), hi].broadcast_to((P, 2 * H, DH // 2)), ALU.mult) \
                        .then_inc(chain_g, 1)
                    gp.wait_ge(chain_g, t * GC + 1 + GC)
                    gp.wait_ge(*rest_done(t - 1))
                    gp.wait_ge(*part0_done(t - 1))
                    gp.tensor_tensor(roped[:, u], ra[:, :], rb[:, :], ALU.add).then_inc(rope_done.sem, 1)
                    gp.wait_ge(*rope_done(t + 1))
                    gp.wait_ge(*part1_done(t + 1))
                    gp.wait_ge(*parts_turned(t - 1))
                    gp.tensor_tensor(parts[:, u, 2], rest[:, u], parts[:, u, 1], ALU.subtract).then_inc(part2_done.sem, 1)

        @block.scalar
        def _(ac):
            ac.wait_ge(preset, 1)
            with ac.Fori(0, PAIRS) as k:
                for u in range(2):
                    t = k * 2 + u
                    ac.wait_ge(*var_ready(t + 1))
                    ac.activation(sd[:, :], v2[:, :], ACT.Sqrt).then_inc(sd_ready.sem, 1)
                    ac.wait_ge(*turned(t + 1))
                    ac.wait_ge(*stored[u](k))
                    ac.activation(turn[:, u], tr[:, :, :], ACT.Copy).then_inc(turn_copied.sem, 1)
                    ac.wait_ge(*projected(t + 1))
                    ac.wait_ge(*rope_done(t - 1))
                    ac.activation(qk[:, u], pqk[:, :], ACT.Copy).then_inc(qk_copied.sem, 1)
                    ac.activation(vp[:, u, :, 0:DH], pv[:, 0:D].rearrange("p (h d) -> p h d", d=DH),
                                  ACT.Copy).then_inc(v_copied.sem, 1)
                    ac.wait_ge(*rope_done(t + 1))
                    ac.wait_ge(*parts_turned(t - 1))
                    ac.activation(parts[:, u, 0], roped[:, u], ACT.Copy).then_inc(part0_done.sem, 1)
                    ac.wait_ge(*rest_done(t + 1))
                    ac.activation(parts[:, u, 1], rest[:, u], ACT.Copy).then_inc(part1_done.sem, 1)

        @block.tensor
        def _(pe):
            pe.wait_ge(const_in, 6 * 16)
            with pe.Fori(0, PAIRS) as k:
                for u in range(2):
                    t = k * 2 + u
                    pe.wait_ge(*xn_ready(t + 1))
                    pe.wait_ge(*turn_copied(t))
                    for c in range(2):
                        pe.transpose(tr[:, c], xn[:, u, c * P:c * P + P], ident[:, :])
                    pe.wait_ge(*xr_ready(t + 1))
                    for c in range(2):
                        mm = pe.transpose(tr[:, 2 + c], xrn[:, u, c * P:c * P + P], ident[:, :])
                    mm.then_inc(turned.sem, 1)
                    pe.wait_ge(*turn_copied(t + 1))
                    pe.wait_ge(*v_copied(t))
                    for c in range(2):
                        pe.matmul(pqk[:, :], turn[:, u, c], w_t[:, c, 0:2 * D], start=c == 0, stop=c == 1)
                    for c in range(2):
                        mm = pe.matmul(pv[:, 0:D], turn[:, u, c], w_t[:, c, 2 * D:3 * D], start=c == 0, stop=c == 1)
                    mm.then_inc(projected.sem, 1)
                    pe.wait_ge(*part2_done(t + 1))
                    pe.wait_ge(*parts_copied(t))
                    for qc in range(2):
                        for c in range(3):
                            for e in range(2):
                                at = qc * D + e * P
                                ce = c * 2 + e
                                mm = pe.transpose(tb[:, qc, ce // 4, ce % 4], parts[:, u, c, at:at + P], ident_bf[:, :])
                    mm.then_inc(parts_turned.sem, 1)

        @block.vector
        def _(ve):
            ch = Chain(ve, chain_v)
            with ve.Fori(0, PAIRS) as k:
                for u in range(2):
                    t = k * 2 + u
                    ch.start(t * VC)
                    ve.wait_ge(*loaded[u](k + 1))
                    ch.link(ve.bn_stats(stat[:, :], xt[:, u]))
                    ve.sem_inc(passed, 1)
                    ch.link(ve.bn_aggr(mv[:, :], stat[:, :]))
                    ve.tensor_scalar(v2[:, 0:1], mv[:, 1:2], LN_EPS, None, ALU.add)
                    ve.tensor_scalar(v2[:, 1:2], mv[:, 1:2], float(D), 1e-30, ALU.mult, ALU.max).then_inc(var_ready.sem, 1)
                    ve.wait_ge(*sd_ready(t + 1))
                    ch.link(ve.reciprocal(rstd[:, :], sd[:, 0:1]))
                    ch.link(ve.tensor_scalar(nrm[:, :], sd[:, 1:2], rstd[:, :], 1e-12, ALU.mult, ALU.max))
                    ch.link(ve.reciprocal(rnr[:, :], nrm[:, :]))
                    ch.link(ve.tensor_scalar(srs[:, :], rnr[:, :], rstd[:, :], float(D) ** 0.5, ALU.mult, ALU.mult))
                    ve.wait_ge(*turned(t - 1))
                    ve.tensor_scalar(xn[:, u], xt[:, u], mv[:, 0:1], rstd[:, :], ALU.subtract, ALU.mult) \
                        .then_inc(xn_ready.sem, 1)
                    ve.tensor_scalar(xs[:, :], xt[:, u], mv[:, 0:1], srs[:, :], ALU.subtract, ALU.mult) \
                        .then_inc(x_read.sem, 1)
                    ve.wait_ge(*x_read(t + 1))
                    ve.wait_ge(*stored[u](k))
                    ve.tensor_tensor(xrn[:, u], xs[:, :], gam[:, :], ALU.mult).then_inc(xr_ready.sem, 1)
                    ve.wait_ge(*part0_done(t + 1))
                    ve.wait_ge(*part2_done(t - 1))
                    ve.tensor_tensor(rest[:, u], roped[:, u], parts[:, u, 0], ALU.subtract).then_inc(rest_done.sem, 1)
                    ve.wait_ge(*parts_turned(t + 1))
                    ve.wait_ge(*stored_qk[0](k))
                    for qc in range(2):
                        src = tb[:, qc].rearrange("p a b t -> p (a b) t")[:, 0:6]
                        ins = ve.tensor_copy(part_t[:, 0, qc, :, :, u * P:u * P + P].rearrange("p c e t -> p (c e) t"), src)
                    ins.then_inc(parts_copied.sem, 1)


NPART = 6
QPART = (0, 0, 0, 1, 1, 2)
KPART = (0, 1, 2, 0, 1, 0)
ROWS = NPART * DH
NMAX = 3


def attend_units():
    units, quads = [], []
    for c in range(2):
        for j in range(4 * c + 4):
            q0 = max(P * j, 512 * c)
            n = 512 * (c + 1) - q0
            per = 2 if n > 256 else 4
            for h in range(0, G, per):
                units.append((len(quads), c, j, h, per, q0, n))
            quads.append((c, j, q0, n, len(units)))
    return units, quads


def max_units():
    out = []
    for i in range(TILES):
        for part in range(1 + i // 4):
            n = min(P * (i + 1) - 512 * part, 512)
            per = min(G, 512 // n)
            for h in range(0, G, per):
                out.append((i, part, h, per, n, part == i // 4))
    return out


def attend(nc, qk_parts, v_pad, eye_bf, mask_q, mask_k, o_t):
    UNITS, QUADS = attend_units()
    MAXU = max_units()
    NU, NQ, NM = len(UNITS), len(QUADS), len(MAXU)
    NB = 4
    with Phase(nc, "at") as ph:
        ident = ph.sb("ident", [P, P], BF16)
        causal_q = ph.sb("causal_q", [P, P], BF16)
        causal_k = ph.sb("causal_k", [P, P], BF16)
        qs = [ph.sb(f"qs{u}", [P, G, T], BF16) for u in range(NB)]
        ks = [ph.sb(f"ks{u}", [P, G, T], BF16) for u in range(NB)]
        vs = [ph.sb(f"vs{u}", [P, TILES, G * VP]) for u in range(NB)]
        pt = [ph.sb(f"pt{r}", [P, G, 512]) for r in range(3)]
        mx = ph.sb("mx", [P, 2, TILES, G])
        mm_ = ph.sb("mxall", [P, TILES, G])
        r1 = ph.sb("r1", [P, TILES, G])
        nm3 = ph.sb("nm3", [P, TILES, NMAX * G], BF16)
        nmt = ph.sb("nmt", [NMAX * G, T], BF16)
        ot = ph.sb("ot", [P, 2, 512])
        st = [ph.ps(f"st{r}", [P, 1024]) for r in range(2)]
        sm = [ph.ps(f"sm{r}", [P, 512]) for r in range(2)]
        o = [ph.ps(f"o{c}", [P, 512]) for c in range(2)]
        tr = o[0][:, :].bitcast(BF16)

        const_in = ph.sem("const_in")
        preset = ph.sem("preset")
        loaded = [ph.event(f"loaded{u}", 16 * 2 * NPART) for u in range(NB)]
        v_loaded = [ph.event(f"v_loaded{u}", 16) for u in range(NB)]
        st_done = ph.event("st_done")
        exp_done = ph.event("exp_done")
        pv_done = ph.event("pv_done", credit=NQ + 1)
        sm_done = ph.event("sm_done")
        sm_read = ph.event("sm_read")
        nm_ready = ph.event("nm_ready")
        nm_turned = ph.event("nm_turned")
        nm_copied = ph.event("nm_copied")
        nm_in = ph.event("nm_in", 16 * NMAX)
        o_copied = ph.event("o_copied")
        stored = [ph.event(f"stored{c}", 16) for c in range(2)]
        chain_v = ph.sem("chain_v")
        split = ph.sem("split")
        block = ph.block()
        VC = 3

        def steps(eng, step):
            with eng.Fori(0, B - 1) as b:
                for g in range(NB):
                    step(b * NB + g, g, True)
            for g in range(NB):
                step((B - 1) * NB + g, g, g + 1 < NB)

        def interleave(more):
            seq, m = [], 0
            first, last = 6, NU - 4
            if more:
                seq += [("sm", n) for n in range(first)]
                m = first
            for n in range(NU):
                seq.append(("st", n))
                if more:
                    upto = min(NM, first + -(-(NM - first) * (n + 1) // last))
                    seq += [("sm", x) for x in range(m, upto)]
                    m = upto
                    if n == NU - 2:
                        seq.append(("turn", 0))
                for k, quad in enumerate(QUADS):
                    if quad[4] + 2 == n + 1:
                        seq.append(("pv", k))
            seq += [("pv", k) for k in range(NQ) if QUADS[k][4] + 2 > NU]
            return seq

        @block.sync
        def _(sp):
            sp.dma_start(ident[:, :], eye_bf).then_inc(const_in, 16)
            sp.dma_start(causal_q[:, :], mask_q).then_inc(const_in, 16)
            sp.dma_start(causal_k[:, :], mask_k).then_inc(const_in, 16)
            ph.give_credits(sp)

            def load(s, u):
                for dst, part, qc in ((qs[u], QPART, 0), (ks[u], KPART, 1)):
                    for n, c in enumerate(part):
                        src = qk_parts[qc, c, bass.ds(s * G * DH, G * DH)].rearrange("(h d) t -> d h t", d=DH)
                        sp.dma_start(dst[n * DH:n * DH + DH], src).then_inc(loaded[u].sem, 16)
                sp.dma_start(vs[u][:, :, :], v_pad[s].rearrange("(i p) n -> p i n", p=P)) \
                    .then_inc(v_loaded[u].sem, 16)

            load(0, 0)
            load(1, 1)

            def put_max(s, u):
                sp.wait_ge(*nm_copied(s + 1))
                for c in range(NMAX):
                    sp.dma_start(qs[u][ROWS + c:ROWS + c + 1], nmt[c * G:c * G + G, :]).then_inc(nm_in.sem, 16)

            def store(s, c):
                sp.wait_ge(*o_copied(s * 2 + c + 1))
                sp.dma_start(o_t[s, :, c * 512:c * 512 + 512], ot[:, c]).then_inc(stored[c].sem, 16)

            put_max(0, 0)

            def step(s, u, more, more2=True):
                if more2:
                    sp.wait_ge(*pv_done(s * NQ - NQ))
                    load(s + 2, (u + 2) % NB)
                store(s, 0)
                if more:
                    put_max(s + 1, (u + 1) % NB)
                store(s, 1)

            with sp.Fori(0, B - 1) as b:
                for g in range(NB):
                    step(b * NB + g, g, True)
            for g in range(NB):
                step((B - 1) * NB + g, g, g + 1 < NB, g + 2 < NB)
            for c in range(2):
                sp.wait_ge(*stored[c](STEPS))

        @block.gpsimd
        def _(gp):
            for u in range(NB):
                gp.memset(ks[u][ROWS:ROWS + NMAX], 1.0).then_inc(preset, 1)

        @block.tensor
        def _(pe):
            pe.wait_ge(const_in, 3 * 16)
            pe.wait_ge(preset, NB)

            def max_scores(s, u, m):
                i, part, h0, per, n, diag = MAXU[m]
                bank = sm[m % 2]
                pe.wait_ge(*sm_read(s * NM + m - 1))
                for h in range(h0, h0 + per):
                    at = (h - h0) * n
                    mm = pe.matmul(bank[:, at:at + n], qs[u][0:ROWS, h, i * P:i * P + P],
                                   ks[u][0:ROWS, h, part * 512:part * 512 + n], start=True, stop=not diag,
                                   skip_group_check=True)
                    if diag:
                        mm = pe.matmul(bank[:, at + n - P:at + n], ident[:, :], causal_q[:, :],
                                       start=False, stop=True, skip_group_check=True)
                mm.then_inc(sm_done.sem, 1)

            def turn_max(s):
                pe.wait_ge(*nm_ready(s + 1))
                pe.wait_ge(*o_copied(s * 2 - 1))
                for i in range(TILES):
                    mm = pe.transpose(tr[0:NMAX * G, i * P:i * P + P], nm3[:, i, :], ident[:, :])
                mm.then_inc(nm_turned.sem, 1)

            def scores(s, u, n):
                _, c, j, h0, per, q0, nq = UNITS[n]
                if n == 0:
                    pe.wait_ge(*nm_in(s + 1))
                pe.wait_ge(*exp_done(s * NU + n - 1))
                w = max(nq, 512) if nq > 256 else nq
                tile = st[n % 2]
                for h in range(h0, h0 + per):
                    at = (h - h0) * w
                    diag = q0 == P * j
                    mm = pe.matmul(tile[:, at:at + nq], ks[u][0:ROWS + NMAX, h, j * P:j * P + P],
                                   qs[u][0:ROWS + NMAX, h, q0:q0 + nq], start=True, stop=not diag,
                                   skip_group_check=True)
                    if diag:
                        mm = pe.matmul(tile[:, at:at + P], ident[:, :], causal_k[:, :],
                                       start=False, stop=True, skip_group_check=True)
                mm.then_inc(st_done.sem, 1)

            def values(s, u, k):
                c, j, q0, n, units_end = QUADS[k]
                pe.wait_ge(*exp_done(s * NU + units_end))
                if j == 0:
                    pe.wait_ge(*o_copied(s * 2 + c - 1))
                    if c == 0:
                        pe.wait_ge(*nm_copied(s + 1))
                for h in range(G):
                    mm = pe.matmul(o[c][h * VP:h * VP + VP, q0 - 512 * c:q0 - 512 * c + n],
                                   vs[u][:, j, h * VP:h * VP + VP], pt[k % 3][:, h, 0:n],
                                   start=j == 0, stop=j == 4 * c + 3, skip_group_check=True)
                mm.then_inc(pv_done.sem, 1)

            def step(b, s, u, more):
                for kind, n in interleave(more):
                    if kind == "sm":
                        if n == 0:
                            nb = b if u + 1 < NB else b + 1
                            pe.wait_ge(*loaded[(u + 1) % NB](nb + 1))
                        max_scores(s + 1, (u + 1) % NB, n)
                    elif kind == "turn":
                        turn_max(s + 1)
                    elif kind == "st":
                        scores(s, u, n)
                    else:
                        if n == 0:
                            pe.wait_ge(*v_loaded[u](b + 1))
                        values(s, u, n)

            pe.wait_ge(*loaded[0](1))
            for m in range(NM):
                max_scores(0, 0, m)
            turn_max(0)
            with pe.Fori(0, B - 1) as b:
                for g in range(NB):
                    step(b, b * NB + g, g, True)
            for g in range(NB):
                step(B - 1, (B - 1) * NB + g, g, g + 1 < NB)

        @block.scalar
        def _(ac):
            def copy_max(s):
                ac.wait_ge(*nm_turned(s + 1))
                ac.wait_ge(*nm_in(s))
                ac.activation(nmt[:, :], tr[0:NMAX * G, 0:T], ACT.Copy).then_inc(nm_copied.sem, 1)

            def copy_out(s, c):
                ac.wait_ge(*pv_done(s * NQ + (4 if c == 0 else NQ)))
                ac.wait_ge(*stored[c](s))
                ac.activation(ot[:, c], o[c][:, :], ACT.Copy).then_inc(o_copied.sem, 1)

            def step(s, u, more):
                for n, (k, c, j, h0, per, q0, nq) in enumerate(UNITS):
                    w = 512 if nq > 256 else nq
                    ac.wait_ge(*st_done(s * NU + n + 1))
                    ac.wait_ge(*pv_done(s * NQ + k - 2))
                    src = st[n % 2][:, 0:per * w].rearrange("p (h n) -> p h n", h=per)[:, :, 0:nq]
                    ac.activation(pt[k % 3][:, h0:h0 + per, 0:nq], src, ACT.Exp, scale=DH ** -0.5) \
                        .then_inc(exp_done.sem, 1)
                    if n == 9:
                        copy_out(s, 0)
                if more:
                    copy_max(s + 1)
                copy_out(s, 1)

            copy_max(0)
            steps(ac, step)

        @block.vector
        def _(ve):
            ch = Chain(ve, chain_v)
            ve.memset(mx[:, :, :, :], NEG * 10).then_inc(chain_v, 1)
            ve.wait_ge(chain_v, 1)

            def max_of(s, u):
                ch.start(s * VC + 1)
                for m, (i, part, h0, per, n, diag) in enumerate(MAXU):
                    ve.wait_ge(*sm_done(s * NM + m + 1))
                    ve.tensor_reduce(mx[:, part, i, h0:h0 + per],
                                     sm[m % 2][:, 0:per * n].rearrange("p (h n) -> p h n", h=per),
                                     AX.X, ALU.max).then_inc(sm_read.sem, 1)
                ve.wait_ge(*sm_read(s * NM + NM))
                ch.link(ve.tensor_tensor(mm_[:, :, :], mx[:, 0], mx[:, 1], ALU.max))
                ve.wait_ge(*nm_turned(s))
                part = [nm3[:, :, c * G:c * G + G] for c in range(NMAX)]
                ch.link(ve.tensor_scalar(part[0], mm_[:, :, :], -1.0, None, ALU.mult))
                ve.scalar_tensor_tensor(out=r1[:, :, :], in0=mm_[:, :, :], scalar=-1.0, in1=part[0],
                                        op0=ALU.mult, op1=ALU.subtract).then_inc(chain_v, 1)
                ve.wait_ge(chain_v, s * VC + 1 + 3)
                ve.tensor_copy(part[1], r1[:, :, :]).then_inc(split, 1)
                ve.wait_ge(split, s + 1)
                ve.tensor_tensor(part[2], r1[:, :, :], part[1], ALU.subtract).then_inc(nm_ready.sem, 1)

            max_of(0, 0)
            steps(ve, lambda s, u, more: max_of(s + 1, (u + 1) % NB) if more else None)


def dispatch(nc, xr, xr_t, slot_embeds, gamma, eye, ec_t, slots_t):
    E = 8
    with Phase(nc, "di") as ph:
        ident = ph.sb("ident", [P, P])
        ones = ph.sb("ones", [P, P])
        gam = ph.sb("gam", [P, D])
        emb = ph.sb("emb", [P, E, D])
        sq = ph.sb("sq", [P, D])
        ss = ph.sb("ss", [P, E])
        sn_t = ph.sb("sn_t", [P, 2, E * P])
        xs = [ph.sb(f"xs{u}", [P, TILES, D + 1]) for u in range(2)]
        xt = [ph.sb(f"xt{u}", [P, TILES, 2, P]) for u in range(2)]
        lg = [ph.sb(f"lg{u}", [P, TILES, E * P]) for u in range(2)]
        ec = ph.sb("ec", [P, 2, E, P])
        ect = ph.sb("ect", [P, 2, E, P])
        nmc = ph.sb("nmc", [P, 2])
        run = ph.sb("run", [P, E, P])
        maxd = ph.sb("maxd", [P, E])
        diag = ph.sb("diag", [P, E, P])
        mb = ph.sb("mb", [P, E * P])
        rec = ph.sb("rec", [P, 2])
        nat = ph.sb("nat", [P, 2, D])
        slt = ph.sb("slt", [P, 2, 2, P])
        pl = [ph.ps(f"pl{r}", [P, E, P]) for r in range(2)]
        tp = ph.ps("tp", [P, E, P])
        sl = ph.ps("sl", [P, 2, 512])

        const_in = ph.sem("const_in")
        ones_set = ph.sem("ones_set")
        slots_in = ph.sem("slots_in")
        prep_v = ph.sem("prep_v")
        prep_a = ph.sem("prep_a")
        prep_p = ph.sem("prep_p")
        xt_in = [ph.event(f"xt_in{u}", 16) for u in range(2)]
        xs_in = [ph.event(f"xs_in{u}", 16) for u in range(2)]
        l_done = ph.event("l_done")
        l_copied = ph.event("l_copied")
        nmc_ready = ph.event("nmc_ready")
        run_done = ph.event("run_done")
        ec_done = ph.event("ec_done")
        ec_turned = ph.event("ec_turned")
        ect_copied = ph.event("ect_copied")
        ect_stored = [ph.event(f"ect_stored{r}", 16) for r in range(2)]
        run_turned = ph.event("run_turned")
        maxd_done = ph.event("maxd_done")
        diag_ready = ph.event("diag_ready")
        mb_done = ph.event("mb_done")
        mb_copied = ph.event("mb_copied")
        ld_done = ph.event("ld_done")
        ed_done = ph.event("ed_done")
        slot_done = ph.event("slot_done", credit=E + 1)
        rec_done = ph.event("rec_done")
        nat_done = ph.event("nat_done")
        slt_turned = ph.event("slt_turned")
        slt_copied = ph.event("slt_copied")
        slt_stored = [ph.event(f"slt_stored{r}", 16) for r in range(2)]
        block = ph.block()
        N = TILES

        def steps(eng, step):
            with eng.Fori(0, B // 2 - 1) as k:
                for u in range(2):
                    step(k * 2 + u, k, u, True)
            for u in range(2):
                step(B - 2 + u, B // 2 - 1, u, u == 0)

        @block.sync
        def _(sp):
            sp.dma_start(ident[:, :], eye).then_inc(const_in, 16)
            sp.dma_start(gam[:, :], gamma.unsqueeze(0).broadcast_to((P, D))).then_inc(const_in, 16)
            sp.dma_start(emb[:, :, :], slot_embeds.rearrange("e s d -> s e d")).then_inc(slots_in, 16)
            ph.give_credits(sp)

            def load(b, u):
                sp.dma_start(xt[u][:, :, :, :], xr_t[bass.ds(b * N, N)].rearrange("i p c t -> p i c t")) \
                    .then_inc(xt_in[u].sem, 16)
                sp.dma_start(xs[u][:, :, 0:D], xr[bass.ds(b * N, N)].rearrange("i p d -> p i d")) \
                    .then_inc(xs_in[u].sem, 16)

            def store_ec(b, n):
                sp.wait_ge(*ect_copied(b * N + n + 1))
                sp.dma_start(ec_t[b * N + n], ect[:, n % 2]).then_inc(ect_stored[n % 2].sem, 16)

            load(0, 0)
            load(1, 1)
            for n in range(N):
                store_ec(0, n)

            def step(b, k, u, more):
                if more:
                    for n in range(N):
                        store_ec(b + 1, n)
                for m in range(E):
                    sp.wait_ge(*slt_copied(b * E + m + 1))
                    sp.dma_start(slots_t[m, :, :, b], slt[:, m % 2]).then_inc(slt_stored[m % 2].sem, 16)
                if not isinstance(b, int) or b + 2 < B:
                    load(b + 2, u)

            steps(sp, step)
            for r in range(2):
                sp.wait_ge(*ect_stored[r](B * N // 2))
                sp.wait_ge(*slt_stored[r](B * E // 2))

        @block.gpsimd
        def _(gp):
            gp.memset(ones[:, :], 1.0).then_inc(ones_set, 1)
            for u in range(2):
                gp.memset(xs[u][:, :, D:D + 1], 1.0).then_inc(ones_set, 1)

            def step(b, k, u, more):
                gp.wait_ge(*mb_copied(b + 1))
                for n in range(N):
                    gp.wait_ge(*l_copied(b * N + n + 1))
                    gp.tensor_tensor(lg[u][:, n], lg[u][:, n], mb[:, :], ALU.subtract).then_inc(ld_done.sem, 1)

            steps(gp, step)

        @block.tensor
        def _(pe):
            pe.wait_ge(const_in, 32)
            pe.wait_ge(ones_set, 3)
            for e in range(E):
                pe.wait_ge(prep_v, 2 * E + 3 + e)
                if e:
                    pe.wait_ge(prep_a, e + 1)
                for c in range(2):
                    mm = pe.transpose(tp[:, c], emb[:, e, c * P:c * P + P], ident[:, :])
                mm.then_inc(prep_p, 1)
            pe.wait_ge(prep_a, E + 1)

            def turn_ec(b, n):
                pe.wait_ge(*ec_done(b * N + n + 1))
                pe.wait_ge(*ect_copied(b * N + n))
                for c in range(E):
                    mm = pe.transpose(tp[:, c], ec[:, n % 2, c], ident[:, :])
                mm.then_inc(ec_turned.sem, 1)

            def logits(b, k, u):
                pe.wait_ge(*xt_in[u](k + 1))
                for n in range(N):
                    pe.wait_ge(*l_copied(b * N + n - 1))
                    for c2 in range(2):
                        for c in range(2):
                            mm = pe.matmul(pl[n % 2][:, 4 * c2:4 * c2 + 4], xt[u][:, n, c],
                                           sn_t[:, c, c2 * 512:c2 * 512 + 512], start=c == 0, stop=c == 1)
                    mm.then_inc(l_done.sem, 1)
                    if n:
                        turn_ec(b, n - 1)
                turn_ec(b, N - 1)

            logits(0, 0, 0)

            def step(b, k, u, more):
                pe.wait_ge(*run_done(b * N + N))
                pe.wait_ge(*ect_copied(b * N + N))
                pe.wait_ge(*slt_copied(b * E))
                for c in range(E):
                    mm = pe.transpose(tp[:, c], run[:, c], ident[:, :])
                mm.then_inc(run_turned.sem, 1)
                pe.wait_ge(*diag_ready(b + 1))
                pe.wait_ge(*nat_done(b * E))
                for c in range(2):
                    mm = pe.matmul(sl[:, c, :], ones[:, :], diag[:, 4 * c:4 * c + 4], start=True, stop=True)
                mm.then_inc(mb_done.sem, 1)
                if more:
                    logits(b + 1, k + u, 1 - u)
                pe.wait_ge(*xs_in[u](k + 1))
                pe.wait_ge(*mb_copied(b + 1))
                for m in range(E + 1):
                    if m < E:
                        pe.wait_ge(*nat_done(b * E + m - 1))
                        for n in range(N):
                            if m == 0:
                                pe.wait_ge(*ed_done(b * N + n + 1))
                            mm = pe.matmul(sl[:, m % 2, 0:D + 1], lg[u][:, n, m * P:m * P + P], xs[u][:, n],
                                           start=n == 0, stop=n == N - 1)
                        mm.then_inc(slot_done.sem, 1)
                    if m:
                        pe.wait_ge(*nat_done(b * E + m))
                        pe.wait_ge(*slt_copied(b * E + m - 2))
                        if m == 1:
                            pe.wait_ge(*maxd_done(b + 1))
                            pe.wait_ge(*ect_copied(b * N + N + (N if more else 0)))
                        for c in range(2):
                            at = 4 * ((m - 1) % 2) + c
                            mm = pe.transpose(tp[:, at], nat[:, (m - 1) % 2, c * P:c * P + P], ident[:, :])
                        mm.then_inc(slt_turned.sem, 1)

            steps(pe, step)

        @block.scalar
        def _(ac):
            ac.wait_ge(prep_v, E)
            ac.activation(ss[:, :], ss[:, :], ACT.Sqrt).then_inc(prep_a, 1)
            for e in range(E):
                ac.wait_ge(prep_p, e + 1)
                ac.activation(sn_t[:, :, e * P:e * P + P], tp[:, 0:2], ACT.Copy).then_inc(prep_a, 1)

            def logit_tile(b, u, n):
                ac.wait_ge(*l_done(b * N + n + 1))
                ac.wait_ge(*slot_done(b * E - E))
                ac.activation(lg[u][:, n], pl[n % 2][:, :, :].rearrange("p e s -> p (e s)"), ACT.Copy) \
                    .then_inc(l_copied.sem, 1)
                ac.wait_ge(*nmc_ready(b * N + n + 1))
                ac.wait_ge(*ec_turned(b * N + n - 1))
                ac.activation(ec[:, n % 2], lg[u][:, n].rearrange("p (e s) -> p e s", s=P), ACT.Exp, bias=nmc[:, n % 2:n % 2 + 1]) \
                    .then_inc(ec_done.sem, 1)

            for n in range(N):
                logit_tile(0, 0, n)

            def step(b, k, u, more):
                ac.wait_ge(*mb_done(b + 1))
                ac.wait_ge(*ld_done(b * N))
                ac.activation(mb[:, :], sl[:, :, :].rearrange("p c n -> p (c n)"), ACT.Copy).then_inc(mb_copied.sem, 1)
                for n in range(N):
                    if more:
                        logit_tile(b + 1, 1 - u, n)
                    ac.wait_ge(*ld_done(b * N + n + 1))
                    ac.activation(lg[u][:, n], lg[u][:, n], ACT.Exp).then_inc(ed_done.sem, 1)
                for m in range(E):
                    ac.wait_ge(*slt_turned(b * E + m + 1))
                    ac.wait_ge(*slt_stored[m % 2](b * (E // 2) + m // 2))
                    ac.activation(slt[:, m % 2], tp[:, 4 * (m % 2):4 * (m % 2) + 2], ACT.Copy).then_inc(slt_copied.sem, 1)

            steps(ac, step)

        @block.vector
        def _(ve):
            ve.wait_ge(slots_in, 16)
            ve.wait_ge(const_in, 32)
            for e in range(E):
                if e:
                    ve.wait_ge(prep_v, e)
                ve.tensor_tensor_reduce(sq[:, :], emb[:, e], emb[:, e], 1.0, 0.0, ALU.mult, ALU.add,
                                        ss[:, e:e + 1]).then_inc(prep_v, 1)
            ve.wait_ge(prep_a, 1)
            ve.tensor_scalar(ss[:, :], ss[:, :], 1e-12, None, ALU.max).then_inc(prep_v, 1)
            ve.wait_ge(prep_v, E + 1)
            ve.reciprocal(ss[:, :], ss[:, :]).then_inc(prep_v, 1)
            ve.wait_ge(prep_v, E + 2)
            for e in range(E):
                ve.tensor_scalar(emb[:, e], emb[:, e], ss[:, e:e + 1], float(D) ** 0.5, ALU.mult, ALU.mult) \
                    .then_inc(prep_v, 1)
            for e in range(E):
                ve.wait_ge(prep_v, E + 3 + e)
                ve.tensor_tensor(emb[:, e], emb[:, e], gam[:, :], ALU.mult).then_inc(prep_v, 1)

            def copy_ect(b, n):
                ve.wait_ge(*ec_turned(b * N + n + 1))
                ve.wait_ge(*ect_stored[n % 2](b * (N // 2) + n // 2))
                ve.tensor_copy(ect[:, n % 2], tp[:, :, :]).then_inc(ect_copied.sem, 1)

            def logit_tiles(b, u):
                for n in range(N):
                    ve.wait_ge(*l_copied(b * N + n + 1))
                    tile = lg[u][:, n].rearrange("p (e s) -> p e s", s=P)
                    ve.wait_ge(*ec_done(b * N + n - 1))
                    ve.tensor_reduce(nmc[:, n % 2:n % 2 + 1], lg[u][:, n],
                                     AX.X, ALU.max, negate=True).then_inc(nmc_ready.sem, 1)
                    if n == 0:
                        ve.wait_ge(*run_turned(b))
                        ve.tensor_copy(run[:, :, :], tile).then_inc(run_done.sem, 1)
                    else:
                        ve.wait_ge(*run_done(b * N + n))
                        ve.tensor_tensor(run[:, :, :], tile, run[:, :, :], ALU.max) \
                            .then_inc(run_done.sem, 1)
                        copy_ect(b, n - 1)
                copy_ect(b, N - 1)

            logit_tiles(0, 0)

            def step(b, k, u, more):
                ve.wait_ge(*run_turned(b + 1))
                ve.tensor_reduce(maxd[:, :], tp[:, :, :], AX.X, ALU.max).then_inc(maxd_done.sem, 1)
                ve.wait_ge(*maxd_done(b + 1))
                ve.wait_ge(*mb_done(b))
                ve.tensor_tensor(diag[:, :, :], ident[:, :].unsqueeze(1).broadcast_to((P, E, P)),
                                 maxd[:, :].unsqueeze(2).broadcast_to((P, E, P)), ALU.mult).then_inc(diag_ready.sem, 1)
                if more:
                    logit_tiles(b + 1, 1 - u)
                for m in range(E):
                    ve.wait_ge(*slot_done(b * E + m + 1))
                    ve.reciprocal(rec[:, m % 2:m % 2 + 1], sl[:, m % 2, D:D + 1]).then_inc(rec_done.sem, 1)
                    ve.wait_ge(*rec_done(b * E + m + 1))
                    ve.wait_ge(*slt_turned(b * E + m - 1))
                    ve.tensor_scalar(nat[:, m % 2], sl[:, m % 2, 0:D], rec[:, m % 2:m % 2 + 1], None, ALU.mult) \
                        .then_inc(nat_done.sem, 1)

            steps(ve, step)
def experts(nc, slots_t, w1, b1_t, w2, b2, eo):
    E, HID = 8, 4 * D
    F, BH = HID // P, B // 2
    with Phase(nc, "ex") as ph:
        xt = ph.sb("xt", [P, 2, 2, B * P])
        w1s = ph.sb("w1s", [P, 2, 2, HID])
        w2s = ph.sb("w2s", [P, 2, F, D])
        b1s = ph.sb("b1s", [P, 2, F])
        b2s = ph.sb("b2s", [P, 2, D])
        ht = ph.sb("ht", [P, 2, F, 512])
        eos = ph.sb("eos", [P, 2, D])
        pht = [ph.ps(f"pht{r}", [P, 512]) for r in range(4)]
        peo = [ph.ps(f"peo{r}", [P, 512]) for r in range(2)]
        loaded = [ph.event(f"loaded{u}", 16 * 5) for u in range(2)]
        h_done = ph.event("h_done", credit=4)
        gelu_done = ph.event("gelu_done", credit=4)
        eo_done = ph.event("eo_done", credit=2 * BH)
        eo_ready = ph.event("eo_ready")
        stored = [ph.event(f"stored{r}", 16) for r in range(2)]
        block = ph.block()

        @block.sync
        def _(sp):
            ph.give_credits(sp)

            def load(e, k, u):
                sp.wait_ge(*eo_done(e * B - 2 * B) if not isinstance(e, int) or e >= 2 else eo_done(0))
                for dst, src in ((xt[:, u], slots_t[e].rearrange("p c b s -> p c (b s)")),
                                 (w1s[:, u], w1[e].rearrange("(c p) h -> p c h", p=P)),
                                 (w2s[:, u], w2[e].rearrange("(f p) d -> p f d", p=P)),
                                 (b1s[:, u], b1_t[e]),
                                 (b2s[:, u], b2[bass.ds(e, 1)].broadcast_to((P, D)))):
                    sp.dma_start(dst, src).then_inc(loaded[u].sem, 16)

            def store(e, k, u):
                for n in range(B):
                    sp.wait_ge(*eo_ready(e * B + n + 1))
                    sp.dma_start(eo[n, e], eos[:, n % 2]).then_inc(stored[n % 2].sem, 16)

            staggered(sp, E, [(0, load), (1, store)])
            for r in range(2):
                sp.wait_ge(*stored[r](E * B // 2))

        @block.tensor
        def _(pe):
            def hidden(e, k, u):
                pe.wait_ge(*loaded[u](k + 1))
                for c in range(2):
                    for f in range(F):
                        i = e * 2 * F + c * F + f
                        pe.wait_ge(*gelu_done(i - 3))
                        for d in range(2):
                            mm = pe.matmul(pht[f % 4][:, :], w1s[:, u, d, f * P:f * P + P],
                                           xt[:, u, d, c * 512:c * 512 + 512], start=d == 0, stop=d == 1)
                        mm.then_inc(h_done.sem, 1)

            def out(e, k, u):
                for n in range(B):
                    c = n // BH
                    pe.wait_ge(*gelu_done(e * 2 * F + (c + 1) * F))
                    pe.wait_ge(*eo_ready(e * B + n - 1))
                    for f in range(F):
                        at = (n % BH) * P
                        mm = pe.matmul(peo[n % 2][:, 0:D], ht[:, c, f, at:at + P], w2s[:, u, f],
                                       start=f == 0, stop=f == F - 1)
                    mm.then_inc(eo_done.sem, 1)

            staggered(pe, E, [(0, lambda e, k, u: (hidden(e, k, u), out(e, k, u)))])

        @block.scalar
        def _(ac):
            def gelus(e, k, u):
                for c in range(2):
                    for f in range(F):
                        i = e * 2 * F + c * F + f
                        ac.wait_ge(*h_done(i + 1))
                        if f == 0:
                            ac.wait_ge(*eo_done(e * B - B + (c + 1) * BH))
                        ac.activation(ht[:, c, f], pht[f % 4][:, :], ACT.Gelu,
                                      bias=b1s[:, u, f:f + 1]).then_inc(gelu_done.sem, 1)

            staggered(ac, E, [(0, gelus)])

        @block.vector
        def _(ve):
            def add_bias(e, k, u):
                for n in range(B):
                    ve.wait_ge(*eo_done(e * B + n + 1))
                    ve.wait_ge(*stored[n % 2](e * (B // 2) + n // 2))
                    ve.tensor_tensor(eos[:, n % 2], peo[n % 2][:, 0:D], b2s[:, u], ALU.add).then_inc(eo_ready.sem, 1)

            staggered(ve, E, [(0, add_bias)])


def mix_and_gate(nc, x, ec_t, eo, o_t, wo_t, eye, x1):
    E = 8
    with Phase(nc, "mx") as ph:
        x_n = x.rearrange("b (i p) d -> (b i) p d", p=P)
        ident = ph.sb("ident", [P, P])
        wo = ph.sb("wo", [P, 2, D])
        eos = ph.sb("eos", [P, 2 * E, D + 1])
        ect = ph.sb("ect", [P, 2, E, P])
        ot = ph.sb("ot", [P, 2, G, P])
        xt = ph.sb("xt", [P, 2, D])
        rden = ph.sb("rden", [P, 2, H])
        on = ph.sb("on", [P, 2, H, DH])
        ont = ph.sb("ont", [P, 2, 2, P])
        rc = ph.sb("rc", [P, 2])
        ff = ph.sb("ff", [P, 2, D])
        ex = ph.sb("ex", [P, 2, D])
        e1 = ph.sb("e1", [P, D])
        r1 = ph.sb("r1", [P, D])
        gate = ph.sb("gate", [P, D])
        sg = ph.sb("sg", [P, D])
        xo = ph.sb("xo", [P, 2, D])
        pc = [ph.ps(f"pc{r}", [P, 512]) for r in range(2)]
        pt = [ph.ps(f"pt{r}", [P, H, VP]) for r in range(2)]
        pn = [ph.ps(f"pn{r}", [P, 2, P]) for r in range(2)]
        pw = [ph.ps(f"pw{r}", [P, 512]) for r in range(2)]
        const_in = ph.sem("const_in")
        ones_set = ph.sem("ones_set")
        passed = ph.sem("passed")
        eo_in = ph.event("eo_in", 16, credit=0)
        tile_in = [ph.event(f"tile_in{u}", 16 * 3) for u in range(2)]
        mixed = ph.event("mixed", credit=TILES + 1)
        o_turned = ph.event("o_turned")
        o_rec = ph.event("o_rec")
        o_ready = ph.event("o_ready")
        on_turned = ph.event("on_turned")
        on_copied = ph.event("on_copied")
        projected = ph.event("projected")
        rc_done = ph.event("rc_done")
        ff_done = ph.event("ff_done")
        exp_done = ph.event("exp_done")
        one_added = ph.event("one_added")
        inverted = ph.event("inverted")
        gate_done = ph.event("gate_done")
        s_done = ph.event("s_done")
        x_done = ph.event("x_done")
        stored = [ph.event(f"stored{u}", 16) for u in range(2)]
        block = ph.block()

        @block.sync
        def _(sp):
            sp.dma_start(ident[:, :], eye).then_inc(const_in, 16)
            sp.dma_start(wo[:, :, :], wo_t.rearrange("(c p) n -> p c n", p=P)).then_inc(const_in, 16)
            ph.give_credits(sp)

            def load(t, k, u):
                sp.wait_ge(*mixed(t - 1))
                sp.dma_start(ect[:, u], ec_t[t]).then_inc(tile_in[u].sem, 16)
                sp.wait_ge(*o_turned(t - 1))
                o_tile = o_t[k // (TILES // 2), :, :, (k % (TILES // 2)) * 2 + u]
                sp.dma_start(ot[:, u], o_tile.rearrange("g p t -> p g t")).then_inc(tile_in[u].sem, 16)
                sp.wait_ge(*x_done(t - 1))
                sp.dma_start(xt[:, u], x_n[t]).then_inc(tile_in[u].sem, 16)

            def store(t, k, u):
                sp.wait_ge(*x_done(t + 1))
                sp.dma_start(x1[t], xo[:, u]).then_inc(stored[u].sem, 16)

            staggered(sp, ALL, [(2, store), (0, load)])
            for u in range(2):
                sp.wait_ge(*stored[u](ALL // 2))

        @block.gpsimd
        def _(gp):
            gp.memset(eos[:, :, D:D + 1], 1.0).then_inc(ones_set, 1)
            for v in range(2):
                gp.dma_start(eos[:, v * E:v * E + E, 0:D], eo[v].rearrange("e p d -> p e d")).then_inc(eo_in.sem, 16)
                gp.wait_ge(*eo_in(v + 1))
            with gp.Fori(0, B // 2 - 1) as pair:
                b = pair * 2
                for v in range(2):
                    gp.wait_ge(*mixed(b * TILES + (v + 1) * TILES))
                    gp.sem_inc(passed, 1)
                    gp.dma_start(eos[:, v * E:v * E + E, 0:D], eo[b + v + 2].rearrange("e p d -> p e d")) \
                        .then_inc(eo_in.sem, 16)
                    gp.wait_ge(*eo_in(b + v + 3))
                    gp.sem_inc(passed, 1)

        @block.tensor
        def _(pe):
            pe.wait_ge(const_in, 32)
            pe.wait_ge(ones_set, 1)

            def turn_and_mix(t, k, u):
                pe.wait_ge(*tile_in[u](k + 1))
                pe.wait_ge(*o_ready(t - 1))
                for g in range(G):
                    mm = pe.transpose(pt[u][:, g * G:g * G + G].rearrange("p h d -> p (h d)"), ot[:, u, g], ident[:, :])
                mm.then_inc(o_turned.sem, 1)
                pe.wait_ge(*eo_in(k // (TILES // 2) + 1))
                pe.wait_ge(*ff_done(t - 1))
                first = ((k // (TILES // 2)) % 2) * E
                for m in range(E):
                    mm = pe.matmul(pc[u][:, 0:D + 1], ect[:, u, m], eos[:, bass.ds(first + m, 1)].rearrange("p a d -> p (a d)"),
                                   start=m == 0, stop=m == E - 1)
                mm.then_inc(mixed.sem, 1)

            def turn_back(t, k, u):
                pe.wait_ge(*o_ready(t + 1))
                pe.wait_ge(*on_copied(t - 1))
                for c in range(2):
                    mm = pe.transpose(pn[u][:, c], on[:, u, 8 * c:8 * c + 8].rearrange("p h d -> p (h d)"), ident[:, :])
                mm.then_inc(on_turned.sem, 1)

            def project(t, k, u):
                pe.wait_ge(*on_copied(t + 1))
                pe.wait_ge(*s_done(t - 1))
                for c in range(2):
                    mm = pe.matmul(pw[u][:, 0:D], ont[:, u, c], wo[:, c], start=c == 0, stop=c == 1)
                mm.then_inc(projected.sem, 1)

            staggered(pe, ALL, [(2, project), (1, turn_back), (0, turn_and_mix)])

        @block.scalar
        def _(ac):
            def copies(t, k, u):
                ac.wait_ge(*ff_done(t + 1))
                ac.wait_ge(*one_added(t - 1))
                ac.activation(ex[:, u], ff[:, u], ACT.Exp, scale=-1.0).then_inc(exp_done.sem, 1)
                ac.wait_ge(*on_turned(t + 1))
                ac.wait_ge(*projected(t - 1))
                ac.activation(ont[:, u], pn[u][:, :, :], ACT.Copy).then_inc(on_copied.sem, 1)

            staggered(ac, ALL, [(1, copies)])

        @block.vector
        def _(ve):
            def divide(t, k, u):
                ve.wait_ge(*o_turned(t + 1))
                ve.reciprocal(rden[:, u], pt[u][:, :, DH]).then_inc(o_rec.sem, 1)
                ve.wait_ge(*o_rec(t + 1))
                ve.wait_ge(*on_turned(t - 1))
                ve.tensor_tensor(on[:, u], pt[u][:, :, 0:DH], rden[:, u].unsqueeze(2).broadcast_to((P, H, DH)), ALU.mult) \
                    .then_inc(o_ready.sem, 1)
                ve.wait_ge(*mixed(t + 1))
                ve.reciprocal(rc[:, u:u + 1], pc[u][:, D:D + 1]).then_inc(rc_done.sem, 1)
                ve.wait_ge(*rc_done(t + 1))
                ve.wait_ge(*exp_done(t - 1))
                ve.tensor_scalar(ff[:, u], pc[u][:, 0:D], rc[:, u:u + 1], None, ALU.mult).then_inc(ff_done.sem, 1)

            def gate_step(t, k, u):
                ve.wait_ge(*exp_done(t + 1))
                ve.tensor_scalar(e1[:, :], ex[:, u], 1.0, None, ALU.add).then_inc(one_added.sem, 1)
                ve.wait_ge(*one_added(t + 1))
                ve.reciprocal(r1[:, :], e1[:, :]).then_inc(inverted.sem, 1)
                ve.wait_ge(*inverted(t + 1))
                ve.tensor_tensor(gate[:, :], ff[:, u], r1[:, :], ALU.mult).then_inc(gate_done.sem, 1)
                ve.wait_ge(*gate_done(t + 1))
                ve.wait_ge(*projected(t + 1))
                ve.tensor_tensor(sg[:, :], pw[u][:, 0:D], gate[:, :], ALU.mult).then_inc(s_done.sem, 1)
                ve.wait_ge(*s_done(t + 1))
                ve.wait_ge(*stored[u](k))
                ve.tensor_tensor(xo[:, u], sg[:, :], xt[:, u], ALU.add).then_inc(x_done.sem, 1)

            staggered(ve, ALL, [(2, gate_step), (0, divide)])


SEG = 64
W1 = H + 1
ONE = DH + 1


def project_memory(nc, x1, w_qkv, wu_t, wu, wo_norm, seg_avg, run_avg, seg_mask, eye, xn_d, qk_t, pk_d, v_d, gates_d):
    with Phase(nc, "pm") as ph:
        ident = ph.sb("ident", [P, P])
        w_s = ph.sb("w_s", [P, 2, 3 * D])
        wut_s = ph.sb("wut_s", [P, 2, D])
        wu_s = ph.sb("wu_s", [P, 2, D])
        nw = ph.sb("nw", [P, D])
        savg = ph.sb("savg", [P, 2])
        ravg = ph.sb("ravg", [P, P])
        smask = ph.sb("smask", [P, 1])
        half = ph.sb("half", [P, 2])
        xt = ph.sb("xt", [P, 2, D])
        stat = ph.sb("stat", [P, 6])
        mv = ph.sb("mv", [P, 2, 2])
        v2 = ph.sb("v2", [P, 2, 2])
        rs = ph.sb("rs", [P, 2, 2])
        xn = ph.sb("xn", [P, 4, D])
        xm = ph.sb("xm", [P, D])
        xr = ph.sb("xr", [P, 2, D])
        xT = ph.sb("xT", [P, 2, 4, P])
        mt = ph.sb("mt", [P, 2, 2, 2])
        neg = ph.sb("neg", [P, 2 * D])
        eq = ph.sb("eq", [P, 2 * D])
        pqk = ph.sb("pqk", [P, 2, 2 * D])
        qkT = ph.sb("qkT", [P, 2, 4, P])
        vp = ph.sb("vp", [P, 2, H, VP])
        mc = ph.sb("mc", [P, D])
        junk = ph.sb("junk", [P, D])
        gcol = ph.sb("gcol", [P, 2, H])
        gs = ph.sb("gs", [P, 4, W1])
        nm = ph.sb("nm", [P, 1])
        nms = ph.sb("nms", [P, 1])
        ge = ph.sb("ge", [P, W1])
        gsum = ph.sb("gsum", [P, 1])
        grec = ph.sb("grec", [P, 1])
        gate = ph.sb("gate", [P, 2, W1])
        p_t = ph.ps("p_t", [P, 4, P])
        p_m = ph.ps("p_m", [P, 2, 2])
        p_qk = ph.ps("p_qk", [P, 2 * D])
        p_vu = ph.ps("p_vu", [P, 2 * D])
        p_mc = ph.ps("p_mc", [P, D])
        p_g = ph.ps("p_g", [P, 2, 2])
        p_sc = ph.ps("p_sc", [P, H])
        p_tq = ph.ps("p_tq", [P, 4, P])

        const_in = ph.sem("const_in")
        preset = ph.sem("preset")
        passed = ph.sem("passed")
        carried = ph.sem("carried")
        sig = lambda name, unit=1: ph.event(name, unit, credit=5)
        loaded = [sig(f"loaded{u}", 16) for u in range(2)]
        stat_done = sig("stat_done")
        mv_done = sig("mv_done")
        v2_done = sig("v2_done")
        rs_done = sig("rs_done")
        xn_done = sig("xn_done")
        xm_done = sig("xm_done")
        xr_done = sig("xr_done")
        turned = sig("turned")
        turn_copied = sig("turn_copied")
        mt_copied = sig("mt_copied")
        projected = sig("projected")
        g_made = sig("g_made")
        g_copied = sig("g_copied")
        neg_done = sig("neg_done")
        eq_done = sig("eq_done")
        pqk_done = sig("pqk_done")
        v_copied = sig("v_copied")
        mc_copied = sig("mc_copied")
        cur_done = sig("cur_done")
        qk_turned = sig("qk_turned")
        qk_copied = sig("qk_copied")
        sc_done = sig("sc_done")
        gs_copied = sig("gs_copied")
        gs_masked = sig("gs_masked")
        nm_done = sig("nm_done")
        nms_done = sig("nms_done")
        ge_done = sig("ge_done")
        grec_done = sig("grec_done")
        gate_done = sig("gate_done")
        xn_stored = [sig(f"xn_stored{u}", 16) for u in range(4)]
        stored = [sig(f"stored{u}", 16 * 3) for u in range(2)]
        gate_stored = [sig(f"gate_stored{u}", 16) for u in range(2)]
        block = ph.block()
        R = TILES
        half_round = lambda k, i: k * (R // 2) + i // 2
        quarter = lambda k, i: k * (R // 4) + i // 4

        @block.sync
        def _(sp):
            for dst, src in ((ident[:, :], eye), (w_s[:, :, :], w_qkv.rearrange("(c p) n -> p c n", p=P)),
                             (wut_s[:, :, :], wu_t.rearrange("(c p) n -> p c n", p=P)),
                             (wu_s[:, :, :], wu.rearrange("(c p) n -> p c n", p=P)),
                             (nw[:, :], wo_norm.unsqueeze(0).broadcast_to((P, D))),
                             (savg[:, :], seg_avg), (ravg[:, :], run_avg), (smask[:, :], seg_mask)):
                sp.dma_start(dst, src).then_inc(const_in, 16)
            ph.give_credits(sp)

            def load(t, k, i):
                sp.wait_ge(*xm_done(t - 1))
                sp.dma_start(xt[:, i % 2], x1[t]).then_inc(loaded[i % 2].sem, 16)

            def store_xn(t, k, i):
                sp.wait_ge(*xn_done(t + 1))
                sp.dma_start(xn_d[t], xn[:, i % 4]).then_inc(xn_stored[i % 4].sem, 16)

            def store(t, k, i):
                u = i % 2
                sp.wait_ge(*pqk_done(t + 1))
                sp.dma_start(pk_d[t], pqk[:, u, D:2 * D]).then_inc(stored[u].sem, 16)
                sp.wait_ge(*v_copied(t + 1))
                sp.dma_start(v_d[t], vp[:, u].rearrange("p h d -> p (h d)")).then_inc(stored[u].sem, 16)
                sp.wait_ge(*qk_copied(t + 1))
                sp.dma_start(qk_t[t], qkT[:, u].rearrange("p c t -> p (c t)")).then_inc(stored[u].sem, 16)
                sp.wait_ge(*gate_done(t + 1))
                sp.dma_start(gates_d[t], gate[:, u]).then_inc(gate_stored[u].sem, 16)

            staggered(sp, ALL, [(3, store), (1, store_xn), (0, load)], R)
            for u in range(4):
                sp.wait_ge(*xn_stored[u](ALL // 4))
            for u in range(2):
                sp.wait_ge(*stored[u](ALL // 2))
                sp.wait_ge(*gate_stored[u](ALL // 2))

        @block.gpsimd
        def _(gp):
            gp.memset(half[:, :], -0.5).then_inc(preset, 1)
            gp.memset(gate[:, :, :], 0.0).then_inc(preset, 1)
            gp.memset(vp[:, :, :, :], 0.0).then_inc(passed, 1)
            gp.wait_ge(passed, 1)
            gp.memset(vp[:, :, :, DH:DH + 1], 1.0).then_inc(preset, 1)
            gp.wait_ge(preset, 3)
            gp.wait_ge(const_in, 8 * 16)

            def roots(t, k, i):
                u = i % 2
                gp.wait_ge(*v2_done(t + 1))
                gp.wait_ge(*xm_done(t - 1))
                gp.tensor_tensor(rs[:, u], v2[:, u], half[:, :], ALU.pow).then_inc(rs_done.sem, 1)

            def scale(t, k, i):
                u = i % 2
                gp.wait_ge(*xm_done(t + 1))
                gp.wait_ge(*turned(t - 1))
                gp.tensor_tensor(xr[:, u], xm[:, :], nw[:, :], ALU.mult).then_inc(xr_done.sem, 1)

            staggered(gp, ALL, [(1, scale), (0, roots)], R)

        @block.vector
        def _(ve):
            ve.wait_ge(preset, 3)
            ve.wait_ge(const_in, 8 * 16)

            def stats(t, k, i):
                u = i % 2
                ve.wait_ge(*loaded[u](half_round(k, i) + 1))
                ve.bn_stats(stat[:, :], xt[:, u]).then_inc(stat_done.sem, 1)
                ve.wait_ge(*stat_done(t + 1))
                ve.sem_inc(carried, 1)
                ve.bn_aggr(mv[:, u], stat[:, :]).then_inc(mv_done.sem, 1)
                ve.wait_ge(*mv_done(t + 1))
                ve.wait_ge(*rs_done(t - 1))
                ve.tensor_scalar(v2[:, u, 0:1], mv[:, u, 1:2], LN_EPS, None, ALU.add)
                ve.tensor_scalar(v2[:, u, 1:2], mv[:, u, 1:2], 1 + RMS_EPS, RMS_EPS * LN_EPS, ALU.mult, ALU.add) \
                    .then_inc(v2_done.sem, 1)

            def norms(t, k, i):
                u = i % 2
                ve.wait_ge(*rs_done(t + 1))
                ve.wait_ge(*xn_stored[i % 4](quarter(k, i)))
                ve.wait_ge(*projected(t - 3))
                ve.tensor_scalar(xn[:, i % 4], xt[:, u], mv[:, u, 0:1], rs[:, u, 0:1], ALU.subtract, ALU.mult) \
                    .then_inc(xn_done.sem, 1)
                ve.wait_ge(*xr_done(t))
                ve.tensor_scalar(xm[:, :], xt[:, u], mv[:, u, 0:1], rs[:, u, 1:2], ALU.subtract, ALU.mult) \
                    .then_inc(xm_done.sem, 1)

            def elu(t, k, i):
                u = i % 2
                ve.wait_ge(*projected(t + 1))
                ve.wait_ge(*eq_done(t))
                ve.tensor_scalar(neg[:, :], p_qk[:, :], 0.0, None, ALU.min).then_inc(neg_done.sem, 1)
                ve.wait_ge(*mc_copied(t + 1))
                ve.wait_ge(*v_copied(t + 1))
                ve.wait_ge(*gate_done(t - 3))
                ve.tensor_tensor_reduce(junk[:, :], p_vu[:, D:2 * D], mc[:, :], 1.0, 0.0, ALU.mult, ALU.add,
                                        gs[:, i % 4, 2 * i + 1:2 * i + 2]).then_inc(cur_done.sem, 1)
                ve.wait_ge(*eq_done(t + 1))
                ve.wait_ge(*qk_turned(t - 1))
                ve.wait_ge(*stored[u](half_round(k, i)))
                ve.scalar_tensor_tensor(out=pqk[:, u], in0=p_qk[:, :], scalar=0.0, in1=eq[:, :],
                                        op0=ALU.max, op1=ALU.add).then_inc(pqk_done.sem, 1)

            def gates(t, k, i):
                u, n = i % 2, 2 * i + 1
                g = gs[:, i % 4]
                ve.wait_ge(*sc_done(t + 1))
                if i:
                    ve.tensor_copy(g[:, 0:n - 1], p_sc[:, 0:n - 1])
                ve.tensor_scalar(g[:, n - 1:n], p_sc[:, n - 1:n], smask[:, :], None, ALU.add).then_inc(gs_copied.sem, 1)
                ve.wait_ge(*gs_copied(t + 1))
                ve.wait_ge(*cur_done(t + 1))
                ve.tensor_reduce(nm[:, :], g[:, 0:n + 1], AX.X, ALU.max, negate=True).then_inc(nm_done.sem, 1)
                ve.wait_ge(*nm_done(t + 1))
                ve.wait_ge(*ge_done(t))
                ve.tensor_scalar(nms[:, :], nm[:, :], float(D) ** -0.5, None, ALU.mult).then_inc(nms_done.sem, 1)

            def gates_end(t, k, i):
                u, n = i % 2, 2 * i + 1
                ve.wait_ge(*ge_done(t + 1))
                ve.reciprocal(grec[:, :], gsum[:, :]).then_inc(grec_done.sem, 1)
                ve.wait_ge(*grec_done(t + 1))
                ve.wait_ge(*gate_stored[u](half_round(k, i)))
                ve.tensor_scalar(gate[:, u, 1:n + 1], ge[:, 0:n], grec[:, :], None, ALU.mult)
                ve.tensor_scalar(gate[:, u, 0:1], ge[:, n:n + 1], grec[:, :], None, ALU.mult).then_inc(gate_done.sem, 1)

            staggered(ve, ALL, [(3, gates), (2, elu), (3, gates_end), (1, norms), (0, stats)], R)

        @block.scalar
        def _(ac):
            ac.wait_ge(preset, 3)

            def turn(t, k, i):
                u = i % 2
                ac.wait_ge(*turned(t + 1))
                ac.wait_ge(*sc_done(t - 1))
                ac.activation(xT[:, u], p_t[:, :, :], ACT.Copy).then_inc(turn_copied.sem, 1)
                ac.wait_ge(*g_made(t - 1))
                ac.activation(mt[:, u], p_m[:, :, :], ACT.Copy).then_inc(mt_copied.sem, 1)

            def values(t, k, i):
                u = i % 2
                ac.wait_ge(*g_made(t + 1))
                ac.activation(gcol[:, :, 2 * i:2 * i + 2], p_g[:, :, :], ACT.Copy).then_inc(g_copied.sem, 1)
                ac.wait_ge(*projected(t + 1))
                ac.wait_ge(*cur_done(t))
                ac.activation(mc[:, :], p_mc[:, :], ACT.Copy).then_inc(mc_copied.sem, 1)
                ac.wait_ge(*stored[u](half_round(k, i)))
                ac.activation(vp[:, u, :, 0:DH], p_vu[:, 0:D].rearrange("p (h d) -> p h d", d=DH), ACT.Copy) \
                    .then_inc(v_copied.sem, 1)
                ac.wait_ge(*neg_done(t + 1))
                ac.wait_ge(*pqk_done(t))
                ac.activation(eq[:, :], neg[:, :], ACT.Exp).then_inc(eq_done.sem, 1)

            def gates(t, k, i):
                n = 2 * i + 1
                ac.wait_ge(*nms_done(t + 1))
                ac.wait_ge(*gate_done(t))
                ac.activation(ge[:, 0:n + 1], gs[:, i % 4, 0:n + 1], ACT.Exp, bias=nms[:, :], scale=float(D) ** -0.5,
                              accum_out=gsum[:, :]).then_inc(ge_done.sem, 1)

            def qk(t, k, i):
                u = i % 2
                ac.wait_ge(*qk_turned(t + 1))
                ac.wait_ge(*stored[u](half_round(k, i)))
                ac.activation(qkT[:, u], p_tq[:, :, :], ACT.Copy).then_inc(qk_copied.sem, 1)

            staggered(ac, ALL, [(3, gates), (2, values), (3, qk), (1, turn)], R)

        @block.tensor
        def _(pe):
            pe.wait_ge(const_in, 8 * 16)

            def turn(t, k, i):
                u = i % 2
                pe.wait_ge(*xn_done(t + 1))
                pe.wait_ge(*xr_done(t + 1))
                pe.wait_ge(*turn_copied(t))
                for c in range(2):
                    pe.transpose(p_t[:, c], xn[:, i % 4, c * P:c * P + P], ident[:, :])
                for c in range(2):
                    pe.transpose(p_t[:, 2 + c], xr[:, u, c * P:c * P + P], ident[:, :])
                pe.wait_ge(*mt_copied(t))
                for c in range(2):
                    mm = pe.matmul(p_m[:, c], xn[:, i % 4, c * P:c * P + P], savg[:, :], start=True, stop=True)
                mm.then_inc(turned.sem, 1)

            def project(t, k, i):
                u = i % 2
                pe.wait_ge(*mt_copied(t + 1))
                pe.wait_ge(*g_copied(t))
                for ci in range(2):
                    for co in range(2):
                        mm = pe.matmul(p_g[:, ci], wu_s[:, co, ci * P:ci * P + P], mt[:, u, co],
                                       start=co == 0, stop=co == 1)
                mm.then_inc(g_made.sem, 1)
                pe.wait_ge(*turn_copied(t + 1))
                pe.wait_ge(*pqk_done(t))
                for c in range(2):
                    pe.matmul(p_qk[:, :], xT[:, u, 2 + c], w_s[:, c, 0:2 * D], start=c == 0, stop=c == 1)
                pe.wait_ge(*cur_done(t))
                for c in range(2):
                    pe.matmul(p_vu[:, 0:D], xT[:, u, 2 + c], w_s[:, c, 2 * D:3 * D], start=c == 0, stop=c == 1)
                for c in range(2):
                    pe.matmul(p_vu[:, D:2 * D], xT[:, u, c], wut_s[:, c], start=c == 0, stop=c == 1)
                mm = pe.matmul(p_mc[:, :], ravg[:, :], xn[:, i % 4], start=True, stop=True)
                mm.then_inc(projected.sem, 1)

            def scores(t, k, i):
                u = i % 2
                pe.wait_ge(*g_copied(t + 1))
                pe.wait_ge(*gs_copied(t))
                for c in range(2):
                    mm = pe.matmul(p_sc[:, 0:2 * i + 1], xT[:, u, c], gcol[:, c, 0:2 * i + 1], start=c == 0, stop=c == 1)
                mm.then_inc(sc_done.sem, 1)
                pe.wait_ge(*pqk_done(t + 1))
                pe.wait_ge(*qk_copied(t))
                for c in range(4):
                    mm = pe.transpose(p_tq[:, c], pqk[:, u, c * P:c * P + P], ident[:, :])
                mm.then_inc(qk_turned.sem, 1)

            staggered(pe, ALL, [(3, scores), (2, project), (1, turn)], R)


RETRIEVED = [2 * -(-(2 * i + 1) // 4) for i in range(TILES)]
R_BEFORE = [sum(RETRIEVED[:i]) for i in range(TILES)]
R_BATCH = sum(RETRIEVED)
LINKS = sum(2 * i + 1 for i in range(TILES))
LINKS_BEFORE = [sum(2 * j + 1 for j in range(i)) for i in range(TILES)]


def rounds_of(eng, body, lag):
    for i in range(TILES):
        body(0, i)
    with eng.Fori(1, B) as k:
        for i in range(TILES):
            body(k, i)
    for i in range(lag):
        body(B, i)


def behind(k, i, lag):
    i -= lag
    if i < 0:
        k, i = k - 1, i + TILES
    t = k * TILES + i
    if isinstance(k, int) and not 0 <= t < ALL:
        return None
    return t, k, i


def retrieve(nc, xn_d, qk_t, pk_d, v_d, gates_d, wo_t, causal, head_mask, eye, s1):
    with Phase(nc, "rt") as ph:
        ident = ph.sb("ident", [P, P])
        wo = ph.sb("wo", [P, 2, D])
        tri = ph.sb("tri", [P, P])
        hm = ph.sb("hm", [P, H // 2])
        qkT = ph.sb("qkT", [P, 4, 4, P])
        pkz = ph.sb("pkz", [P, 4, 2, D])
        vp = ph.sb("vp", [P, 4, H, VP])
        gt = ph.sb("gt", [P, 4, W1])
        xn = ph.sb("xn", [P, 4, D])
        qx = ph.sb("qx", [P, 2, H, P])
        asb = ph.sb("asb", [P, 2, H, P])
        st = ph.sb("st", [P, 2 * 2 * TILES, 2, H // 2, DH])
        last = ph.sb("last", [P, 2, 2, H // 2, VP])
        oT = ph.sb("oT", [P, 4, P])
        rden = ph.sb("rden", [P, H])
        dn = ph.sb("dn", [P, H])
        on = ph.sb("on", [P, H, DH])
        onT = ph.sb("onT", [P, 2, P])
        acc = ph.sb("acc", [P, 2, 2, P])
        sx = ph.sb("sx", [P, D])
        so = ph.sb("so", [P, 2, D])
        p_a = [ph.ps(f"p_a{r}", [P, 4, P]) for r in range(2)]
        p_r = [ph.ps(f"p_r{r}", [P, 4, P]) for r in range(2)]
        p_o = ph.ps("p_o", [P, 4, P])
        p_on = ph.ps("p_on", [P, H, VP])
        p_s = ph.ps("p_s", [P, 512])
        p_w = ph.ps("p_w", [P, 2, D])

        const_in = ph.sem("const_in")
        preset = ph.sem("preset")
        sig = lambda name, unit=1: ph.event(name, unit, credit=5)
        loaded = [sig(f"loaded{u}", 16 * 6) for u in range(4)]
        stored = [sig(f"stored{u}", 16) for u in range(2)]
        q_spread = sig("q_spread")
        a_made = ph.event("a_made", credit=9)
        a_masked = sig("a_masked")
        s_made = sig("s_made")
        s_copied = sig("s_copied")
        o_made = sig("o_made")
        o_copied = sig("o_copied")
        o_turned = sig("o_turned")
        dn_done = sig("dn_done")
        rden_done = sig("rden_done")
        on_done = sig("on_done")
        on_turned = sig("on_turned")
        on_copied = sig("on_copied")
        projected = sig("projected")
        r_made = sig("r_made")
        acc_link = [sig(f"acc_link{c}") for c in range(2)]
        sx_done = sig("sx_done")
        s_done = sig("s_done")
        block = ph.block()
        quarter = lambda k, i: k * (TILES // 4) + i // 4
        half = lambda k, i: k * (TILES // 2) + i // 2
        state = lambda k, n: st[:, bass.ds((k % 2) * (2 * TILES) + n, 1)].rearrange("p a c h d -> p (a c) h d")

        @block.sync
        def _(sp):
            for dst, src in ((ident[:, :], eye), (wo[:, :, :], wo_t.rearrange("(c p) n -> p c n", p=P)),
                             (tri[:, :], causal), (hm[:, :], head_mask)):
                sp.dma_start(dst, src).then_inc(const_in, 16)
            ph.give_credits(sp)
            sp.wait_ge(preset, 2)

            def body(k, i):
                if at := behind(k, i, 4):
                    t, _, j = at
                    sp.wait_ge(*s_done(t + 1))
                    sp.dma_start(s1[t], so[:, j % 2]).then_inc(stored[j % 2].sem, 16)
                if at := behind(k, i, 0):
                    t, _, j = at
                    u = j % 4
                    sp.wait_ge(*s_done(t - 3))
                    for dst, src in ((qkT[:, u], qk_t[t].rearrange("p (c t) -> p c t", t=P)),
                                     (pkz[0:SEG, u, 0], pk_d[t, 0:SEG]), (pkz[SEG:P, u, 1], pk_d[t, SEG:P]),
                                     (vp[:, u], v_d[t].rearrange("p (h d) -> p h d", d=VP)),
                                     (gt[:, u], gates_d[t]), (xn[:, u], xn_d[t])):
                        sp.dma_start(dst, src).then_inc(loaded[u].sem, 16)

            rounds_of(sp, body, 4)
            for u in range(2):
                sp.wait_ge(*stored[u](ALL // 2))

        @block.gpsimd
        def _(gp):
            gp.memset(pkz[:, :, :, :], 0.0).then_inc(preset, 1)
            gp.memset(last[:, :, :, :, :], 0.0).then_inc(preset, 1)
            gp.wait_ge(const_in, 4 * 16)

            def body(k, i):
                t = k * TILES + i
                gp.wait_ge(*loaded[i % 4](quarter(k, i) + 1))
                gp.wait_ge(*a_made(4 * t - 4))
                for c in range(2):
                    ins = gp.tensor_tensor(qx[:, i % 2, 8 * c:8 * c + 8],
                                           qkT[:, i % 4, c].unsqueeze(1).broadcast_to((P, 8, P)),
                                           hm[:, :].unsqueeze(2).broadcast_to((P, 8, P)), ALU.mult)
                ins.then_inc(q_spread.sem, 1)

            rounds_of(gp, body, 0)

        @block.tensor
        def _(pe):
            pe.wait_ge(const_in, 4 * 16)
            pe.wait_ge(preset, 2)

            def add_state(t, k, i, seg):
                pe.wait_ge(*s_copied(2 * t + seg))
                for c in range(2):
                    mm = pe.matmul(p_s[:, c * 8 * ONE:(c + 1) * 8 * ONE], pkz[:, i % 4, seg, c * P:c * P + P],
                                   vp[:, i % 4, 8 * c:8 * c + 8, 0:ONE], start=i == 0 and seg == 0 and c == 0,
                                   stop=i == TILES - 1 and seg == 1, skip_group_check=True)
                mm.then_inc(s_made.sem, 1)

            def products(t, k, i, m):
                pe.wait_ge(*a_masked(4 * t + m - 1))
                pe.matmul(p_a[m % 2][:, :, :], qkT[:, i % 4, 2 + m // 2], qx[:, i % 2, 4 * m:4 * m + 4],
                          start=True, stop=True).then_inc(a_made.sem, 1)

            def read_states(t, k, i, r):
                jb, c = r // 2, r % 2
                n = min(4, 2 * i + 1 - 4 * jb)
                pe.wait_ge(*acc_link[c](k * LINKS + LINKS_BEFORE[i] + 4 * jb))
                src = st[:, bass.ds((k % 2) * (2 * TILES) + 4 * jb, n), c]
                pe.matmul(p_r[c][:, 0:n], qkT[:, i % 4, c], src, start=True, stop=True).then_inc(r_made.sem, 1)

            def attend_tile(t, k, i):
                pe.wait_ge(*a_masked(4 * t + 4))
                pe.wait_ge(*o_copied(t))
                for g in range(4):
                    if i:
                        pe.matmul(p_o[:, g], last[:, (i - 1) % 2, g // 2, 4 * (g % 2):4 * (g % 2) + 4],
                                  qkT[:, i % 4, g // 2], start=True, stop=False, skip_group_check=True)
                    for h in range(4):
                        mm = pe.matmul(p_o[h * VP:h * VP + VP, g], vp[:, i % 4, 4 * g + h], asb[:, i % 2, 4 * g + h],
                                       start=i == 0, stop=True, skip_group_check=True)
                mm.then_inc(o_made.sem, 1)

            def body(k, i):
                if at := behind(k, i, 3):
                    t, _, j = at
                    pe.wait_ge(*on_copied(t + 1))
                    for c in range(2):
                        mm = pe.matmul(p_w[:, 1], onT[:, c], wo[:, c], start=c == 0, stop=c == 1)
                    mm.then_inc(projected.sem, 1)
                new, old = behind(k, i, 1), behind(k, i, 2)
                if old:
                    attend_tile(*old)
                if new:
                    pe.wait_ge(*q_spread(new[0] + 1))
                for m in range(4):
                    if new:
                        if m == 0:
                            pe.wait_ge(*loaded[new[2] % 4](quarter(*new[1:]) + 1))
                            add_state(*new, 0)
                        products(*new, m)
                        if m == 1:
                            add_state(*new, 1)
                    if old:
                        if m == 0:
                            pe.wait_ge(*o_copied(old[0] + 1))
                            pe.wait_ge(*on_done(old[0]))
                            for g in range(4):
                                mm = pe.transpose(p_on[:, 4 * g:4 * g + 4].rearrange("p h d -> p (h d)"),
                                                  oT[:, g], ident[:, :])
                            mm.then_inc(o_turned.sem, 1)
                        for r in range(2 * m, min(2 * m + 2, RETRIEVED[old[2]])):
                            read_states(*old, r)
                if old:
                    pe.wait_ge(*on_done(old[0] + 1))
                    pe.wait_ge(*sx_done(old[0]))
                    for c in range(2):
                        mm = pe.transpose(p_w[:, 0, c * P:c * P + P],
                                          on[:, 8 * c:8 * c + 8].rearrange("p h d -> p (h d)"), ident[:, :])
                    mm.then_inc(on_turned.sem, 1)

            rounds_of(pe, body, 3)

        @block.scalar
        def _(ac):
            def body(k, i):
                if at := behind(k, i, 2):
                    t, _, j = at
                    ac.wait_ge(*o_made(t + 1))
                    ac.wait_ge(*o_turned(t))
                    ac.activation(oT[:, :, :], p_o[:, :, :], ACT.Copy).then_inc(o_copied.sem, 1)
                    ac.wait_ge(*on_turned(t + 1))
                    ac.wait_ge(*projected(t))
                    ac.activation(onT[:, :, :], p_w[:, 0].rearrange("p (c t) -> p c t", t=P), ACT.Copy) \
                        .then_inc(on_copied.sem, 1)

            rounds_of(ac, body, 2)

        @block.vector
        def _(ve):
            ve.wait_ge(const_in, 4 * 16)
            ve.wait_ge(preset, 2)

            def keep_state(t, k, i, seg):
                ve.wait_ge(*s_made(2 * t + seg + 1))
                sums = p_s[:, 0:2 * 8 * ONE].rearrange("p (c h d) -> p c h d", c=2, d=ONE)
                same = hm[:, :].unsqueeze(1).unsqueeze(3).broadcast_to((P, 2, 8, ONE))
                if seg:
                    ve.wait_ge(*o_made(t))
                    ve.tensor_tensor(last[:, i % 2, :, :, 0:ONE], sums, same, ALU.mult)
                ve.tensor_tensor(state(k, 2 * i + seg), sums[:, :, :, 0:DH], same[:, :, :, 0:DH], ALU.mult) \
                    .then_inc(s_copied.sem, 1)

            def mask(t, k, i, m):
                ve.wait_ge(*a_made(4 * t + m + 1))
                ve.wait_ge(*o_made(t - 1))
                ve.tensor_tensor(asb[:, i % 2, 4 * m:4 * m + 4], p_a[m % 2][:, :, :],
                                 tri[:, :].unsqueeze(1).broadcast_to((P, 4, P)), ALU.mult).then_inc(a_masked.sem, 1)

            def divide(t, k, i):
                ve.wait_ge(*o_turned(t + 1))
                ve.tensor_scalar(dn[:, :], p_on[:, :, DH], RMS_EPS, None, ALU.add).then_inc(dn_done.sem, 1)
                ve.wait_ge(*dn_done(t + 1))
                ve.reciprocal(rden[:, :], dn[:, :]).then_inc(rden_done.sem, 1)
                ve.wait_ge(*rden_done(t + 1))
                ve.wait_ge(*on_turned(t))
                ve.tensor_tensor(on[:, :, :], p_on[:, :, 0:DH], rden[:, :].unsqueeze(2).broadcast_to((P, H, DH)), ALU.mult) \
                    .then_inc(on_done.sem, 1)

            def weigh(t, k, i, r):
                jb, c = r // 2, r % 2
                ve.wait_ge(*r_made(k * R_BATCH + R_BEFORE[i] + r + 1))
                for n in range(4 * jb, min(4 * jb + 4, 2 * i + 1)):
                    src, g = p_r[c][:, n - 4 * jb], gt[:, i % 4, 1 + n:2 + n]
                    if n == 0:
                        ins = ve.tensor_scalar(acc[:, i % 2, c], src, g, None, ALU.mult)
                    else:
                        ve.wait_ge(*acc_link[c](k * LINKS + LINKS_BEFORE[i] + n))
                        ins = ve.scalar_tensor_tensor(out=acc[:, i % 2, c], in0=src, scalar=g, in1=acc[:, i % 2, c],
                                                      op0=ALU.mult, op1=ALU.add)
                    ins.then_inc(acc_link[c].sem, 1)

            def finish(t, k, i):
                ve.wait_ge(*projected(t + 1))
                ve.wait_ge(*s_done(t))
                ve.tensor_tensor(sx[:, :], p_w[:, 1], xn[:, i % 4], ALU.add).then_inc(sx_done.sem, 1)
                ve.wait_ge(*sx_done(t + 1))
                ve.wait_ge(*stored[i % 2](half(k, i)))
                ve.scalar_tensor_tensor(out=so[:, i % 2], in0=sx[:, :], scalar=gt[:, i % 4, 0:1],
                                        in1=acc[:, i % 2].rearrange("p c d -> p (c d)"), op0=ALU.mult, op1=ALU.add) \
                    .then_inc(s_done.sem, 1)

            def body(k, i):
                if at := behind(k, i, 3):
                    finish(*at)
                new, old = behind(k, i, 1), behind(k, i, 2)
                for m in range(4):
                    if new:
                        if m == 0:
                            keep_state(*new, 0)
                        mask(*new, m)
                        if m == 1:
                            keep_state(*new, 1)
                    if old:
                        if m == 0:
                            divide(*old)
                        for r in range(2 * m, min(2 * m + 2, RETRIEVED[old[2]])):
                            weigh(*old, r)

            rounds_of(ve, body, 3)


def switch(nc, x1, xn_d, s1, m1, m2, mb, w1, w2, b2, ramp, eye, out):
    BLK, Y = 16, 64
    F = BLK * Y
    with Phase(nc, "sw") as ph:
        out_n = out.rearrange("b (i p) d -> (b i) p d", p=P)
        ident = ph.sb("ident", [P, P])
        m1s = ph.sb("m1s", [P, 2, Y])
        m2s = ph.sb("m2s", [Y + 1, F])
        w1s = ph.sb("w1s", [P, 2, F])
        w2s = ph.sb("w2s", [P, F // P, D])
        b2s = ph.sb("b2s", [P, D])
        rank = ph.sb("rank", [P, F])
        xn = ph.sb("xn", [P, 2, D])
        xs = ph.sb("xs", [P, 2, D])
        ss = ph.sb("ss", [P, 2, D])
        xnT = ph.sb("xnT", [P, 2, 2, P])
        lrT = ph.sb("lrT", [Y + 1, 2, P])
        mx = ph.sb("mx", [P, BLK])
        top = ph.sb("top", [P, F])
        cand = ph.sb("cand", [P, F])
        mx2 = ph.sb("mx2", [P, BLK])
        pick = ph.sb("pick", [P, F])
        h = ph.sb("h", [P, F])
        hT = ph.sb("hT", [P, 2, F // P, P])
        f = ph.sb("f", [P, 2, D])
        ef = ph.sb("ef", [P, D])
        e1 = ph.sb("e1", [P, D])
        rec = ph.sb("rec", [P, D])
        sf = ph.sb("sf", [P, D])
        sg = ph.sb("sg", [P, D])
        xo = ph.sb("xo", [P, 2, D])
        p_x = ph.ps("p_x", [P, 4, P])
        p_l = ph.ps("p_l", [P, F])
        p_m = ph.ps("p_m", [P, F])
        p_h = [ph.ps(f"p_h{r}", [P, 4, P]) for r in range(2)]
        p_r = ph.ps("p_r", [P, 512])

        const_in = ph.sem("const_in")
        preset = ph.sem("preset")
        sig = lambda name, unit=1: ph.event(name, unit, credit=6)
        xn_in = [sig(f"xn_in{u}", 16) for u in range(2)]
        xs_in = [sig(f"xs_in{u}", 32) for u in range(2)]
        stored = [sig(f"stored{u}", 16) for u in range(2)]
        turned = sig("turned")
        turn_copied = sig("turn_copied")
        lr_made = sig("lr_made")
        lr_copied = sig("lr_copied")
        logits_made = sig("logits_made")
        mid_made = sig("mid_made")
        mx_done = sig("mx_done")
        top_done = sig("top_done")
        cand_done = sig("cand_done")
        mx2_done = sig("mx2_done")
        pick_done = sig("pick_done")
        h_done = sig("h_done")
        h_turned = sig("h_turned")
        h_copied = sig("h_copied")
        res_made = sig("res_made")
        f_done = sig("f_done")
        exp_done = sig("exp_done")
        e1_done = sig("e1_done")
        rec_done = sig("rec_done")
        sf_done = sig("sf_done")
        sg_done = sig("sg_done")
        x_done = sig("x_done")
        block = ph.block()
        blocks = lambda a: a.rearrange("p (j y) -> p j y", y=Y)
        spread = lambda a: a.unsqueeze(2).broadcast_to((P, BLK, Y))
        CONSTS = 8

        @block.sync
        def _(sp):
            for dst, src in ((ident[:, :], eye), (m1s[:, :, :], m1.rearrange("(c p) n -> p c n", p=P)),
                             (m2s[0:Y, :], m2), (m2s[Y:Y + 1, :], mb),
                             (w1s[:, :, :], w1.rearrange("(c p) n -> p c n", p=P)),
                             (w2s[:, :, :], w2.rearrange("(c p) n -> p c n", p=P)),
                             (b2s[:, :], b2.unsqueeze(0).broadcast_to((P, D))),
                             (rank[:, :], ramp.broadcast_to((P, F)))):
                sp.dma_start(dst, src).then_inc(const_in, 16)
            ph.give_credits(sp)

            def load_xn(t, k, u):
                sp.wait_ge(*turned(t - 1))
                sp.dma_start(xn[:, u], xn_d[t]).then_inc(xn_in[u].sem, 16)

            def load_xs(t, k, u):
                sp.wait_ge(*x_done(t - 1))
                sp.dma_start(xs[:, u], x1[t]).then_inc(xs_in[u].sem, 16)
                sp.dma_start(ss[:, u], s1[t]).then_inc(xs_in[u].sem, 16)

            def store(t, k, u):
                sp.wait_ge(*x_done(t + 1))
                sp.dma_start(out_n[t], xo[:, u]).then_inc(stored[u].sem, 16)

            staggered(sp, ALL, [(6, store), (4, load_xs), (0, load_xn)])
            for u in range(2):
                sp.wait_ge(*stored[u](ALL // 2))

        @block.gpsimd
        def _(gp):
            gp.memset(lrT[Y:Y + 1, :, :], 1.0).then_inc(preset, 1)
            gp.wait_ge(const_in, CONSTS * 16)

            def scale(t, k, u):
                gp.wait_ge(*f_done(t + 1))
                gp.wait_ge(*xs_in[u](k + 1))
                gp.wait_ge(*sg_done(t))
                gp.tensor_tensor(sf[:, :], f[:, u], ss[:, u], ALU.mult).then_inc(sf_done.sem, 1)

            def rank_top(t, k, u):
                gp.wait_ge(*top_done(t + 1))
                gp.wait_ge(*pick_done(t))
                gp.tensor_tensor(cand[:, :], top[:, :], rank[:, :], ALU.mult).then_inc(cand_done.sem, 1)

            def add_x(t, k, u):
                gp.wait_ge(*sg_done(t + 1))
                gp.wait_ge(*stored[u](k))
                gp.tensor_tensor(xo[:, u], sg[:, :], xs[:, u], ALU.add).then_inc(x_done.sem, 1)

            staggered(gp, ALL, [(5, scale), (2, rank_top), (5, add_x)])

        @block.tensor
        def _(pe):
            pe.wait_ge(const_in, CONSTS * 16)
            pe.wait_ge(preset, 1)

            def turn(t, k, u):
                pe.wait_ge(*xn_in[u](k + 1))
                pe.wait_ge(*lr_copied(t))
                for c in range(2):
                    mm = pe.transpose(p_x[:, c], xn[:, u, c * P:c * P + P], ident[:, :])
                mm.then_inc(turned.sem, 1)

            def low_rank(t, k, u):
                pe.wait_ge(*turn_copied(t + 1))
                for c in range(2):
                    mm = pe.matmul(p_x[0:Y, 2], m1s[:, c], xnT[:, u, c], start=c == 0, stop=c == 1)
                mm.then_inc(lr_made.sem, 1)

            def hidden(t, k, u):
                pe.wait_ge(*lr_copied(t + 1))
                pe.wait_ge(*top_done(t))
                for n in range(0, F, 512):
                    mm = pe.matmul(p_l[:, n:n + 512], lrT[:, u], m2s[:, n:n + 512], start=True, stop=True)
                mm.then_inc(logits_made.sem, 1)
                pe.wait_ge(*h_done(t))
                for n in range(0, F, 512):
                    for c in range(2):
                        mm = pe.matmul(p_m[:, n:n + 512], xnT[:, u, c], w1s[:, c, n:n + 512], start=c == 0, stop=c == 1)
                mm.then_inc(mid_made.sem, 1)

            def turn_hidden(t, k, u):
                pe.wait_ge(*h_done(t + 1))
                for r in range(2):
                    pe.wait_ge(*h_copied(2 * t + r - 1))
                    for c in range(4):
                        mm = pe.transpose(p_h[r][:, c], h[:, (4 * r + c) * P:(4 * r + c + 1) * P], ident[:, :])
                    mm.then_inc(h_turned.sem, 1)

            def result(t, k, u):
                pe.wait_ge(*h_copied(2 * t + 2))
                pe.wait_ge(*f_done(t))
                for c in range(F // P):
                    mm = pe.matmul(p_r[:, 0:D], hT[:, u, c], w2s[:, c], start=c == 0, stop=c == F // P - 1)
                mm.then_inc(res_made.sem, 1)

            staggered(pe, ALL, [(1, turn), (2, hidden), (1, low_rank), (4, result), (3, turn_hidden)])

        @block.scalar
        def _(ac):
            ac.wait_ge(preset, 1)

            def exp(t, k, u):
                ac.wait_ge(*f_done(t + 1))
                ac.wait_ge(*e1_done(t))
                ac.activation(ef[:, :], f[:, u], ACT.Exp, scale=-1.0).then_inc(exp_done.sem, 1)

            def copy_turned(t, k, u):
                ac.wait_ge(*turned(t + 1))
                ac.wait_ge(*mid_made(t - 1))
                ac.activation(xnT[:, u], p_x[:, 0:2], ACT.Copy).then_inc(turn_copied.sem, 1)

            def copy_low_rank(t, k, u):
                ac.wait_ge(*lr_made(t + 1))
                ac.activation(lrT[0:Y, u], p_x[0:Y, 2], ACT.Copy).then_inc(lr_copied.sem, 1)

            def copy_hidden(t, k, u):
                ac.wait_ge(*res_made(t - 1))
                for r in range(2):
                    ac.wait_ge(*h_turned(2 * t + r + 1))
                    ac.activation(hT[:, u, 4 * r:4 * r + 4], p_h[r][:, :, :], ACT.Copy).then_inc(h_copied.sem, 1)

            staggered(ac, ALL, [(5, exp), (1, copy_turned), (1, copy_low_rank), (3, copy_hidden)])

        @block.vector
        def _(ve):
            ve.wait_ge(const_in, CONSTS * 16)

            def tops(t, k, u):
                ve.wait_ge(*logits_made(t + 1))
                ve.tensor_reduce(mx[:, :], blocks(p_l[:, :]), AX.X, ALU.max).then_inc(mx_done.sem, 1)
                ve.wait_ge(*mx_done(t + 1))
                ve.wait_ge(*cand_done(t))
                ve.tensor_tensor(blocks(top[:, :]), blocks(p_l[:, :]), spread(mx[:, :]), ALU.is_equal) \
                    .then_inc(top_done.sem, 1)

            def pass_chosen(t, k, u):
                ve.wait_ge(*cand_done(t + 1))
                ve.tensor_reduce(mx2[:, :], blocks(cand[:, :]), AX.X, ALU.max).then_inc(mx2_done.sem, 1)
                ve.wait_ge(*mx2_done(t + 1))
                ve.wait_ge(*h_done(t))
                ve.tensor_tensor(blocks(pick[:, :]), blocks(cand[:, :]), spread(mx2[:, :]), ALU.is_equal) \
                    .then_inc(pick_done.sem, 1)
                ve.wait_ge(*pick_done(t + 1))
                ve.wait_ge(*mid_made(t + 1))
                ve.wait_ge(*h_turned(2 * t))
                ve.scalar_tensor_tensor(out=h[:, :], in0=p_m[:, :], scalar=0.0, in1=pick[:, :],
                                        op0=ALU.max, op1=ALU.mult).then_inc(h_done.sem, 1)

            def add_bias(t, k, u):
                ve.wait_ge(*res_made(t + 1))
                ve.wait_ge(*sf_done(t - 1))
                ve.tensor_tensor(f[:, u], p_r[:, 0:D], b2s[:, :], ALU.add).then_inc(f_done.sem, 1)

            def gate(t, k, u):
                ve.wait_ge(*exp_done(t + 1))
                ve.tensor_scalar(e1[:, :], ef[:, :], 1.0, None, ALU.add).then_inc(e1_done.sem, 1)
                ve.wait_ge(*e1_done(t + 1))
                ve.reciprocal(rec[:, :], e1[:, :]).then_inc(rec_done.sem, 1)
                ve.wait_ge(*rec_done(t + 1))
                ve.wait_ge(*sf_done(t + 1))
                ve.wait_ge(*x_done(t))
                ve.tensor_tensor(sg[:, :], sf[:, :], rec[:, :], ALU.mult).then_inc(sg_done.sem, 1)

            staggered(ve, ALL, [(2, tops), (5, gate), (2, pass_chosen), (4, add_bias)])


def program(nc, w, out):
    def scratch(name, shape, dt=F32):
        return nc.dram_tensor(f"s_{name}", shape, dt).ap()

    qk_parts = scratch("qk_parts", (2, 3, STEPS * G * DH, T), BF16)
    v_pad = scratch("v_pad", (STEPS, T, G * VP))
    xr = scratch("xr", (ALL, P, D))
    xr_t = scratch("xr_t", (ALL, P, 2, P))
    qk_pairs = qk_parts.rearrange("q c (b r) (j t) -> b j q c r t", b=B, j=TILES // 2)
    v_tiles = v_pad.rearrange("(b g) (i p) n -> b i g p n", g=G, p=P)
    project_rope(nc, w["x"], w["w_qkv"], w["gamma"], w["cos_t"], w["sin_t"], w["eye"], w["eye_bf"],
                 qk_pairs, v_tiles, xr, xr_t)
    o_t = scratch("o_t", (STEPS, P, T))
    attend(nc, qk_parts, v_pad, w["eye_bf"], w["mask_q"], w["mask_k"], o_t)
    ec_t = scratch("ec_t", (ALL, P, 8, P))
    slots_t = scratch("slots_t", (8, P, 2, B, P))
    dispatch(nc, xr, xr_t, w["slots"], w["slot_gamma"], w["eye"], ec_t, slots_t)
    eo = scratch("eo", (B, 8, P, D))
    experts(nc, slots_t, w["w1"], w["b1_t"], w["w2"], w["b2"], eo)
    x1 = scratch("x1", (ALL, P, D))
    o_tiles = o_t.rearrange("(b g) p (i t) -> b g p i t", g=G, t=P)
    mix_and_gate(nc, w["x"], ec_t, eo, o_tiles, w["wo_t"], w["eye"], x1)

    xn1 = scratch("xn1", (ALL, P, D))
    qk1 = scratch("qk1", (ALL, P, 2 * D))
    pk1 = scratch("pk1", (ALL, P, D))
    v1 = scratch("v1", (ALL, P, H * VP))
    gates1 = scratch("gates1", (ALL, P, W1))
    s1 = scratch("s1", (ALL, P, D))
    project_memory(nc, x1, w["w_qkv1"], w["wu_t"], w["wu"], w["norm_w"], w["seg_avg"], w["run_avg"],
                   w["seg_mask"], w["eye"], xn1, qk1, pk1, v1, gates1)
    retrieve(nc, xn1, qk1, pk1, v1, gates1, w["wo1_t"], w["causal"], w["head_mask"], w["eye"], s1)
    switch(nc, x1, xn1, s1, w["m1"], w["m2"], w["mb"], w["f_w1"], w["f_w2"], w["f_b2"], w["ramp"], w["eye"], out)


def constants():
    import numpy as np
    inv = 1.0 / (np.float32(10000.0) ** (np.arange(0, DH, 2, dtype=np.float32) / np.float32(DH)))
    ang = np.outer(np.arange(T, dtype=np.float32), inv.astype(np.float32)).astype(np.float32)
    cos = np.concatenate([np.cos(ang), np.cos(ang)], 1).astype(np.float32)
    sin = np.concatenate([-np.sin(ang), np.sin(ang)], 1).astype(np.float32)
    eye = np.eye(P, dtype=np.float32)
    later = np.triu(np.ones((P, P), np.float32), 1) * np.float32(NEG)
    bf = mybir.dt.np(BF16)
    p = np.arange(P)
    same = p[:, None] // 64 == p[None, :] // 64
    causal = (p[:, None] <= p[None, :]).astype(np.float32)
    seg_avg = np.zeros((P, 2), np.float32)
    seg_avg[p, p // 64] = 1.0 / 64
    run_avg = np.where(same, causal / (p[None, :] % 64 + 1), 0).astype(np.float32)
    more = {"causal": causal, "seg_avg": seg_avg, "run_avg": run_avg,
            "seg_mask": np.where(p < 64, np.float32(NEG), np.float32(0))[:, None].astype(np.float32),
            "head_mask": (p[:, None] // DH == np.arange(8)[None, :]).astype(np.float32),
            "ramp": np.tile(64 - np.arange(64, dtype=np.float32), 16)[None, :]}
    return {**more, "mask_q": later.astype(bf), "mask_k": np.ascontiguousarray(later.T).astype(bf),
            "cos_t": cos, "sin_t": sin, "eye": eye, "eye_bf": eye.astype(bf)}


def kernel(**inputs):
    import numpy as np
    import concourse.bacc as bacc
    from concourse.bass_utils import run_bass_kernel_spmd

    nc = bacc.Bacc("TRN2", target_bir_lowering=False, num_devices=1)
    laid = {"x": inputs["L0_attn_x"],
            "w_qkv": np.concatenate([inputs[f"L0_attn_W{m}"].T for m in "qkv"], 1),
            "gamma": inputs["L0_ffn_norm_gamma"],
            "slots": inputs["L0_ffn_slot_embeds"], "slot_gamma": inputs["L0_ffn_slot_norm_gamma"]}
    laid.update({"w1": inputs["L0_ffn_w1"], "w2": inputs["L0_ffn_w2"], "b2": inputs["L0_ffn_b2"],
                 "b1_t": np.asarray(inputs["L0_ffn_b1"]).reshape(8, -1, P).transpose(0, 2, 1), "wo_t": inputs["L0_attn_Wo"].T})
    laid.update({"w_qkv1": np.concatenate([inputs[f"L1_attn_W{m}"].T for m in "qkv"], 1),
                 "wu_t": inputs["L1_attn_Wu"].T, "wu": inputs["L1_attn_Wu"], "wo1_t": inputs["L1_attn_Wo"].T,
                 "norm_w": inputs["L1_attn_norm_w"], "m1": inputs["L1_ffn_m1"],
                 "m2": inputs["L1_ffn_m2"].reshape(64, -1), "mb": inputs["L1_ffn_mb"].reshape(1, -1),
                 "f_w1": inputs["L1_ffn_w1"].reshape(D, -1),
                 "f_w2": inputs["L1_ffn_w2"].transpose(1, 0, 2).reshape(-1, D), "f_b2": inputs["L1_ffn_b2"]})
    laid = {n: np.ascontiguousarray(a) for n, a in laid.items()}
    laid.update(constants())
    ins = {n: nc.dram_tensor(f"in_{n}", a.shape, mybir.dt.from_np(a.dtype), kind="ExternalInput").ap()
           for n, a in laid.items()}
    out = nc.dram_tensor("out", (B, T, D), F32, kind="ExternalOutput").ap()
    program(nc, ins, out)
    r = run_bass_kernel_spmd(nc, [{f"in_{n}": a for n, a in laid.items()}], core_ids=[0])
    return r.results[0]["out"]
```

```python
from contextlib import ExitStack

import concourse.bass as bass
from concourse import mybir

F32 = mybir.dt.float32
BF16 = mybir.dt.bfloat16
F32R = mybir.dt.float32r
ALU = mybir.AluOpType
ACT = mybir.ActivationFunctionType
AX = mybir.AxisListType

P = 128
B, T, D = 8, 1024, 256
TILES = T // P
ALL = B * TILES
H, DH = 16, 16
G = 4
STEPS = B * H // G
VP = 32
LN_EPS, RMS_EPS = 1e-5, 1e-6
NEG = -1e30


class Chain:

    def __init__(self, eng, sem):
        self.eng, self.sem, self.base, self.n = eng, sem, 0, 0

    def start(self, base):
        self.base, self.n = base, 0

    def link(self, ins):
        self.n += 1
        ins.then_inc(self.sem, 1)
        self.eng.wait_ge(self.sem, self.base + self.n)


class Event:

    def __init__(self, sem, unit, credit):
        self.sem, self.unit, self.credit = sem, unit, credit

    def __call__(self, n):
        return self.sem, (n + self.credit) * self.unit


class Phase:

    def __init__(self, nc, tag):
        self.nc, self.tag, self.ctx = nc, tag, ExitStack()
        self.events = []

    def __enter__(self):
        self.ctx.enter_context(self.nc.cleanup_on_exit())
        return self

    def __exit__(self, *exc):
        return self.ctx.__exit__(*exc)

    def sb(self, name, shape, dt=F32):
        return self.ctx.enter_context(self.nc.sbuf_tensor(f"{self.tag}_{name}", shape, dt))

    def ps(self, name, shape, dt=F32):
        return self.ctx.enter_context(self.nc.psum_tensor(f"{self.tag}_{name}", shape, dt))

    def sem(self, name):
        return self.nc.alloc_semaphore(name=f"{self.tag}_{name}")

    def event(self, name, unit=1, credit=2):
        e = Event(self.sem(name), unit, credit)
        self.events.append(e)
        return e

    def give_credits(self, eng):
        for e in self.events:
            if e.credit:
                eng.sem_inc(e.sem, e.unit * e.credit)

    def block(self):
        return self.ctx.enter_context(self.nc.Block())


def staggered(eng, n, stages, R=2):
    lead = -(-max(lag for lag, _ in stages) // R)

    def rounds(k):
        for u in range(R):
            for lag, fn in stages:
                kk, uu = k + (u - lag) // R, (u - lag) % R
                if isinstance(k, int) and not 0 <= kk * R + uu < n:
                    continue
                fn(kk * R + uu, kk, uu)

    for k in range(lead):
        rounds(k)
    with eng.Fori(lead, n // R) as k:
        rounds(k)
    for k in range(n // R, n // R + lead):
        rounds(k)


def project_rope(nc, x, w_qkv, gamma, cos_t, sin_t, eye, eye_bf, qk_parts, v_pad, xr, xr_t):
    QT = 4
    with Phase(nc, "pr") as ph:
        x_n = x.rearrange("b (i p) d -> (b i) p d", p=P)
        ident = ph.sb("ident", [P, P])
        ident_bf = ph.sb("ident_bf", [P, P], BF16)
        w_t = ph.sb("w_t", [P, 2, 3 * D])
        gam = ph.sb("gam", [P, D])
        cos = ph.sb("cos", [P, TILES, DH])
        sin = ph.sb("sin", [P, TILES, DH])
        half = ph.sb("half", [P, 2])
        xt = ph.sb("xt", [P, 4, D])
        stat = ph.sb("stat", [P, 6])
        mv = ph.sb("mv", [P, 2, 2])
        v2 = ph.sb("v2", [P, 2, 2])
        rs = ph.sb("rs", [P, 2, 2])
        xn = ph.sb("xn", [P, 2, D])
        xs = ph.sb("xs", [P, 2, D])
        xrn = ph.sb("xrn", [P, 4, D])
        turn = ph.sb("turn", [P, 4, 4, P])
        qk = ph.sb("qk", [P, 2, 2 * D])
        ra = ph.sb("ra", [P, 2, 2 * D])
        rb = ph.sb("rb", [P, 2 * D])
        roped = ph.sb("roped", [P, 2, 2 * D])
        rest = ph.sb("rest", [P, 2, 2 * D])
        parts = ph.sb("parts", [P, 2, 3, 2 * D], BF16)
        vp = ph.sb("vp", [P, 4, H, VP])
        part_t = ph.sb("part_t", [P, 2, 2, 3, 2, QT * P], BF16)
        tr = [ph.ps(f"tr{u}", [P, 4, P]) for u in range(2)]
        pqk = [ph.ps(f"pqk{u}", [P, 2 * D]) for u in range(2)]
        pv = [ph.ps(f"pv{u}", [P, 512]) for u in range(2)]
        tb = ph.ps("tb", [P, 2, 2, 4, P], BF16)

        const_in = ph.sem("const_in")
        preset = ph.sem("preset")
        passed = ph.sem("passed")
        carried = ph.sem("carried")
        sig = lambda name, unit=1: ph.event(name, unit, credit=9)
        loaded = [sig(f"loaded{u}", 16) for u in range(4)]
        stat_done = sig("stat_done")
        mv_done = sig("mv_done")
        v2_done = sig("v2_done")
        rs_done = sig("rs_done")
        xn_done = sig("xn_done")
        xs_done = sig("xs_done")
        xr_done = sig("xr_done")
        turned = sig("turned")
        turn_copied = sig("turn_copied")
        projected = sig("projected")
        qk_copied = sig("qk_copied")
        v_copied = sig("v_copied")
        cos_done = sig("cos_done")
        sin_done = sig("sin_done")
        rope_done = sig("rope_done")
        part0_done = sig("part0_done")
        rest_done = sig("rest_done")
        part1_done = sig("part1_done")
        part2_done = sig("part2_done")
        parts_turned = sig("parts_turned")
        q_copied = sig("q_copied")
        k_copied = sig("k_copied")
        stored = [sig(f"stored{u}", 16 * 3) for u in range(4)]
        parts_stored = [sig(f"parts_stored{u}", 16 * 4) for u in range(2)]
        block = ph.block()
        R = TILES
        lo, hi = slice(0, DH // 2), slice(DH // 2, DH)
        heads = lambda a: a.rearrange("p (h d) -> p h d", d=DH)
        quarter = lambda b, i: b * (TILES // 4) + i // 4

        @block.sync
        def _(sp):
            for dst, src in ((ident[:, :], eye), (ident_bf[:, :], eye_bf),
                             (w_t[:, :, :], w_qkv.rearrange("(c p) n -> p c n", p=P)),
                             (gam[:, :], gamma.unsqueeze(0).broadcast_to((P, D))),
                             (cos[:, :, :], cos_t.rearrange("(i p) d -> p i d", p=P)),
                             (sin[:, :, :], sin_t.rearrange("(i p) d -> p i d", p=P))):
                sp.dma_start(dst, src).then_inc(const_in, 16)
            ph.give_credits(sp)

            def load(t, b, i):
                sp.wait_ge(*xs_done(t - 3))
                sp.dma_start(xt[:, i % 4], x_n[t]).then_inc(loaded[i % 4].sem, 16)

            def store(t, b, i):
                u = i % 4
                sp.wait_ge(*xr_done(t + 1))
                sp.dma_start(xr[t], xrn[:, u]).then_inc(stored[u].sem, 16)
                sp.wait_ge(*turn_copied(t + 1))
                sp.dma_start(xr_t[t], turn[:, u, 2:4]).then_inc(stored[u].sem, 16)
                sp.wait_ge(*v_copied(t + 1))
                sp.dma_start(v_pad[b, i].rearrange("g p n -> p g n"),
                             vp[:, u].rearrange("p (g h) d -> p g (h d)", g=G)).then_inc(stored[u].sem, 16)

            def store_parts(t, b, i):
                if i % QT != QT - 1:
                    return
                sp.wait_ge(*q_copied(t + 1))
                sp.wait_ge(*k_copied(t + 1))
                v = i // QT
                for qc in range(2):
                    for e in range(2):
                        sp.dma_start(qk_parts[b, v, qc, :, e * P:e * P + P].rearrange("c p t -> p c t"),
                                     part_t[:, v, qc, :, e]).then_inc(parts_stored[v].sem, 16)

            staggered(sp, ALL, [(0, load), (5, store), (8, store_parts)], R)
            for u in range(4):
                sp.wait_ge(*stored[u](ALL // 4))
            for v in range(2):
                sp.wait_ge(*parts_stored[v](B))

        @block.gpsimd
        def _(gp):
            gp.memset(half[:, :], -0.5).then_inc(preset, 1)
            gp.memset(vp[:, :, :, :], 0.0).then_inc(passed, 1)
            gp.wait_ge(passed, 1)
            gp.memset(vp[:, :, :, DH:DH + 1], 1.0).then_inc(preset, 1)
            gp.wait_ge(preset, 2)
            gp.wait_ge(const_in, 6 * 16)

            def roots(t, b, i):
                u = i % 2
                gp.wait_ge(*v2_done(t + 1))
                gp.wait_ge(*xs_done(t - 1))
                gp.tensor_tensor(rs[:, u], v2[:, u], half[:, :], ALU.pow).then_inc(rs_done.sem, 1)

            def rope(t, b, i):
                u = i % 2
                qs, bh = heads(qk[:, u]), heads(rb[:, :])
                gp.wait_ge(*qk_copied(t + 1))
                gp.wait_ge(*rope_done(t))
                table = lambda a, part, n: a[:, i:i + 1, part].broadcast_to((P, 2 * H, n))
                gp.tensor_tensor(bh[:, :, lo], qs[:, :, hi], table(sin, lo, DH // 2), ALU.mult)
                gp.tensor_tensor(bh[:, :, hi], qs[:, :, lo], table(sin, hi, DH // 2), ALU.mult).then_inc(sin_done.sem, 1)
                gp.wait_ge(*sin_done(t + 1))
                gp.wait_ge(*cos_done(t + 1))
                gp.wait_ge(*rest_done(t - 1))
                gp.wait_ge(*part0_done(t - 1))
                gp.tensor_tensor(roped[:, u], ra[:, u], rb[:, :], ALU.add).then_inc(rope_done.sem, 1)

            staggered(gp, ALL, [(5, rope), (1, roots)], R)

        @block.scalar
        def _(ac):
            ac.wait_ge(preset, 2)

            def middle_part(t, b, i):
                ac.wait_ge(*rest_done(t + 1))
                ac.wait_ge(*parts_turned(t - 1))
                ac.activation(parts[:, i % 2, 1], rest[:, i % 2], ACT.Copy).then_inc(part1_done.sem, 1)

            def copy_turned(t, b, i):
                ac.wait_ge(*turned(t + 1))
                ac.wait_ge(*stored[i % 4](quarter(b, i)))
                ac.wait_ge(*projected(t - 3))
                ac.activation(turn[:, i % 4], tr[i % 2][:, :, :], ACT.Copy).then_inc(turn_copied.sem, 1)

            def copy_qkv(t, b, i):
                u = i % 2
                ac.wait_ge(*projected(t + 1))
                ac.wait_ge(*rope_done(t - 1))
                ac.activation(qk[:, u], pqk[u][:, :], ACT.Copy).then_inc(qk_copied.sem, 1)
                ac.wait_ge(*stored[i % 4](quarter(b, i)))
                ac.activation(vp[:, i % 4, :, 0:DH], pv[u][:, 0:D].rearrange("p (h d) -> p h d", d=DH),
                              ACT.Copy).then_inc(v_copied.sem, 1)

            def first_part(t, b, i):
                ac.wait_ge(*rope_done(t + 1))
                ac.wait_ge(*parts_turned(t - 1))
                ac.activation(parts[:, i % 2, 0], roped[:, i % 2], ACT.Copy).then_inc(part0_done.sem, 1)

            def copy_k(t, b, i):
                ac.wait_ge(*parts_turned(t + 1))
                ac.wait_ge(*parts_stored[i // QT](b))
                ac.activation(part_t[:, i // QT, 1, :, :, (i % QT) * P:(i % QT + 1) * P].rearrange("p c e t -> p (c e) t"),
                              tb[:, 1].rearrange("p a b t -> p (a b) t")[:, 0:6], ACT.Copy).then_inc(k_copied.sem, 1)

            staggered(ac, ALL, [(6, middle_part), (3, copy_turned), (7, copy_k), (5, first_part), (4, copy_qkv)], R)

        @block.tensor
        def _(pe):
            pe.wait_ge(const_in, 6 * 16)

            def transpose(t, b, i):
                pe.wait_ge(*xn_done(t + 1))
                pe.wait_ge(*turn_copied(t - 1))
                for c in range(2):
                    pe.transpose(tr[i % 2][:, c], xn[:, i % 2, c * P:c * P + P], ident[:, :])
                pe.wait_ge(*xr_done(t + 1))
                for c in range(2):
                    mm = pe.transpose(tr[i % 2][:, 2 + c], xrn[:, i % 4, c * P:c * P + P], ident[:, :])
                mm.then_inc(turned.sem, 1)

            def project(t, b, i):
                u = i % 2
                pe.wait_ge(*turn_copied(t + 1))
                pe.wait_ge(*v_copied(t - 1))
                for c in range(2):
                    pe.matmul(pqk[u][:, :], turn[:, i % 4, c], w_t[:, c, 0:2 * D], start=c == 0, stop=c == 1)
                for c in range(2):
                    mm = pe.matmul(pv[u][:, 0:D], turn[:, i % 4, c], w_t[:, c, 2 * D:3 * D], start=c == 0, stop=c == 1)
                mm.then_inc(projected.sem, 1)

            def turn_parts(t, b, i):
                pe.wait_ge(*part2_done(t + 1))
                pe.wait_ge(*q_copied(t))
                pe.wait_ge(*k_copied(t))
                for qc in range(2):
                    for c in range(3):
                        for e in range(2):
                            at = qc * D + e * P
                            ce = c * 2 + e
                            mm = pe.transpose(tb[:, qc, ce // 4, ce % 4], parts[:, i % 2, c, at:at + P], ident_bf[:, :])
                mm.then_inc(parts_turned.sem, 1)

            staggered(pe, ALL, [(7, turn_parts), (3, transpose), (4, project)], R)

        @block.vector
        def _(ve):
            ve.wait_ge(const_in, 6 * 16)

            def stats(t, b, i):
                u = i % 2
                ve.wait_ge(*loaded[i % 4](quarter(b, i) + 1))
                ve.wait_ge(*mv_done(t))
                ve.bn_stats(stat[:, :], xt[:, i % 4]).then_inc(stat_done.sem, 1)
                ve.wait_ge(*stat_done(t + 1))
                ve.sem_inc(carried, 1)
                ve.bn_aggr(mv[:, u], stat[:, :]).then_inc(mv_done.sem, 1)
                ve.wait_ge(*mv_done(t + 1))
                ve.wait_ge(*rs_done(t - 1))
                ve.tensor_scalar(v2[:, u, 0:1], mv[:, u, 1:2], LN_EPS, None, ALU.add)
                ve.tensor_scalar(v2[:, u, 1:2], mv[:, u, 1:2], LN_EPS * 1e-24 / D, None, ALU.max).then_inc(v2_done.sem, 1)

            def norms(t, b, i):
                u = i % 2
                ve.wait_ge(*rs_done(t + 1))
                ve.wait_ge(*turned(t - 1))
                ve.tensor_scalar(xn[:, u], xt[:, i % 4], mv[:, u, 0:1], rs[:, u, 0:1], ALU.subtract, ALU.mult) \
                    .then_inc(xn_done.sem, 1)
                ve.wait_ge(*xr_done(t - 1))
                ve.tensor_scalar(xs[:, u], xt[:, i % 4], mv[:, u, 0:1], rs[:, u, 1:2], ALU.subtract, ALU.mult) \
                    .then_inc(xs_done.sem, 1)

            def scale(t, b, i):
                ve.wait_ge(*xs_done(t + 1))
                ve.wait_ge(*stored[i % 4](quarter(b, i)))
                ve.tensor_tensor(xrn[:, i % 4], xs[:, i % 2], gam[:, :], ALU.mult).then_inc(xr_done.sem, 1)

            def times_cos(t, b, i):
                u = i % 2
                ve.wait_ge(*qk_copied(t + 1))
                ve.wait_ge(*rope_done(t - 1))
                ve.tensor_tensor(heads(ra[:, u]), heads(qk[:, u]), cos[:, i:i + 1, :].broadcast_to((P, 2 * H, DH)), ALU.mult) \
                    .then_inc(cos_done.sem, 1)

            def last_part(t, b, i):
                u = i % 2
                ve.wait_ge(*part1_done(t + 1))
                ve.wait_ge(*parts_turned(t - 1))
                ve.tensor_tensor(parts[:, u, 2], rest[:, u], parts[:, u, 1], ALU.subtract).then_inc(part2_done.sem, 1)

            def what_is_left(t, b, i):
                u = i % 2
                ve.wait_ge(*part0_done(t + 1))
                ve.wait_ge(*part2_done(t - 1))
                ve.tensor_tensor(rest[:, u], roped[:, u], parts[:, u, 0], ALU.subtract).then_inc(rest_done.sem, 1)

            def copy_q(t, b, i):
                ve.wait_ge(*parts_turned(t + 1))
                ve.wait_ge(*parts_stored[i // QT](b))
                ve.tensor_copy(part_t[:, i // QT, 0, :, :, (i % QT) * P:(i % QT + 1) * P].rearrange("p c e t -> p (c e) t"),
                               tb[:, 0].rearrange("p a b t -> p (a b) t")[:, 0:6]).then_inc(q_copied.sem, 1)

            staggered(ve, ALL, [(5, times_cos), (6, what_is_left), (2, norms), (2, scale), (1, stats), (6, last_part), (7, copy_q)], R)


NPART = 6
QPART = (0, 0, 0, 1, 1, 2)
KPART = (0, 1, 2, 0, 1, 0)
ROWS = NPART * DH
NMAX = 3


def attend_units():
    units, quads = [], []
    for c in range(2):
        for j in range(4 * c + 4):
            q0 = max(P * j, 512 * c)
            n = 512 * (c + 1) - q0
            per = 2 if n > 256 else 4
            for h in range(0, G, per):
                units.append((len(quads), c, j, h, per, q0, n))
            quads.append((c, j, q0, n, len(units)))
    return units, quads


def max_units():
    out = []
    for i in range(TILES):
        for part in range(1 + i // 4):
            n = min(P * (i + 1) - 512 * part, 512)
            per = min(G, 512 // n)
            for h in range(0, G, per):
                out.append((i, part, h, per, n, part == i // 4))
    return out


def attend(nc, qk_parts, v_pad, eye_bf, mask_q, mask_k, o_t):
    UNITS, QUADS = attend_units()
    MAXU = max_units()
    NU, NQ, NM = len(UNITS), len(QUADS), len(MAXU)
    NB = 4
    with Phase(nc, "at") as ph:
        ident = ph.sb("ident", [P, P], BF16)
        causal_q = ph.sb("causal_q", [P, P], BF16)
        causal_k = ph.sb("causal_k", [P, P], BF16)
        qs = [ph.sb(f"qs{u}", [P, G, T], BF16) for u in range(NB)]
        ks = [ph.sb(f"ks{u}", [P, G, T], BF16) for u in range(NB)]
        vs = [ph.sb(f"vs{u}", [P, TILES, G * VP]) for u in range(NB)]
        pt = [ph.sb(f"pt{r}", [P, G, 512]) for r in range(3)]
        mx = ph.sb("mx", [P, 2, TILES, G])
        mm_ = ph.sb("mxall", [P, TILES, G])
        r1 = ph.sb("r1", [P, TILES, G])
        nm3 = ph.sb("nm3", [P, TILES, NMAX * G], BF16)
        nmt = ph.sb("nmt", [NMAX * G, T], BF16)
        ot = ph.sb("ot", [P, 2, 512])
        st = [ph.ps(f"st{r}", [P, 1024]) for r in range(2)]
        sm = [ph.ps(f"sm{r}", [P, 512]) for r in range(2)]
        o = [ph.ps(f"o{c}", [P, 512]) for c in range(2)]
        tr = o[0][:, :].bitcast(BF16)

        const_in = ph.sem("const_in")
        preset = ph.sem("preset")
        loaded = [ph.event(f"loaded{u}", 16 * 2 * NPART) for u in range(NB)]
        v_loaded = [ph.event(f"v_loaded{u}", 16) for u in range(NB)]
        st_done = ph.event("st_done")
        exp_done = ph.event("exp_done")
        pv_done = ph.event("pv_done", credit=NQ + 1)
        sm_done = ph.event("sm_done")
        sm_read = ph.event("sm_read")
        nm_ready = ph.event("nm_ready")
        nm_turned = ph.event("nm_turned")
        nm_copied = ph.event("nm_copied")
        nm_in = ph.event("nm_in", 16 * NMAX)
        o_copied = ph.event("o_copied")
        stored = [ph.event(f"stored{c}", 16) for c in range(2)]
        chain_v = ph.sem("chain_v")
        split = ph.sem("split")
        block = ph.block()
        VC = 3

        def steps(eng, step):
            with eng.Fori(0, B - 1) as b:
                for g in range(NB):
                    step(b * NB + g, g, True)
            for g in range(NB):
                step((B - 1) * NB + g, g, g + 1 < NB)

        def interleave(more):
            seq, m = [], 0
            first, last = 6, NU - 4
            if more:
                seq += [("sm", n) for n in range(first)]
                m = first
            for n in range(NU):
                seq.append(("st", n))
                if more:
                    upto = min(NM, first + -(-(NM - first) * (n + 1) // last))
                    seq += [("sm", x) for x in range(m, upto)]
                    m = upto
                    if n == NU - 2:
                        seq.append(("turn", 0))
                for k, quad in enumerate(QUADS):
                    if quad[4] + 2 == n + 1:
                        seq.append(("pv", k))
            seq += [("pv", k) for k in range(NQ) if QUADS[k][4] + 2 > NU]
            return seq

        @block.sync
        def _(sp):
            sp.dma_start(ident[:, :], eye_bf).then_inc(const_in, 16)
            sp.dma_start(causal_q[:, :], mask_q).then_inc(const_in, 16)
            sp.dma_start(causal_k[:, :], mask_k).then_inc(const_in, 16)
            ph.give_credits(sp)

            def load(s, u):
                for dst, part, qc in ((qs[u], QPART, 0), (ks[u], KPART, 1)):
                    for n, c in enumerate(part):
                        src = qk_parts[qc, c, bass.ds(s * G * DH, G * DH)].rearrange("(h d) t -> d h t", d=DH)
                        sp.dma_start(dst[n * DH:n * DH + DH], src).then_inc(loaded[u].sem, 16)
                sp.dma_start(vs[u][:, :, :], v_pad[s].rearrange("(i p) n -> p i n", p=P)) \
                    .then_inc(v_loaded[u].sem, 16)

            load(0, 0)
            load(1, 1)

            def put_max(s, u):
                sp.wait_ge(*nm_copied(s + 1))
                for c in range(NMAX):
                    sp.dma_start(qs[u][ROWS + c:ROWS + c + 1], nmt[c * G:c * G + G, :]).then_inc(nm_in.sem, 16)

            def store(s, c):
                sp.wait_ge(*o_copied(s * 2 + c + 1))
                sp.dma_start(o_t[s, :, c * 512:c * 512 + 512], ot[:, c]).then_inc(stored[c].sem, 16)

            put_max(0, 0)

            def step(s, u, more, more2=True):
                if more2:
                    sp.wait_ge(*pv_done(s * NQ - NQ))
                    load(s + 2, (u + 2) % NB)
                store(s, 0)
                if more:
                    put_max(s + 1, (u + 1) % NB)
                store(s, 1)

            with sp.Fori(0, B - 1) as b:
                for g in range(NB):
                    step(b * NB + g, g, True)
            for g in range(NB):
                step((B - 1) * NB + g, g, g + 1 < NB, g + 2 < NB)
            for c in range(2):
                sp.wait_ge(*stored[c](STEPS))

        @block.gpsimd
        def _(gp):
            for u in range(NB):
                gp.memset(ks[u][ROWS:ROWS + NMAX], 1.0).then_inc(preset, 1)

        @block.tensor
        def _(pe):
            pe.wait_ge(const_in, 3 * 16)
            pe.wait_ge(preset, NB)

            def max_scores(s, u, m):
                i, part, h0, per, n, diag = MAXU[m]
                bank = sm[m % 2]
                pe.wait_ge(*sm_read(s * NM + m - 1))
                for h in range(h0, h0 + per):
                    at = (h - h0) * n
                    mm = pe.matmul(bank[:, at:at + n], qs[u][0:ROWS, h, i * P:i * P + P],
                                   ks[u][0:ROWS, h, part * 512:part * 512 + n], start=True, stop=not diag,
                                   skip_group_check=True)
                    if diag:
                        mm = pe.matmul(bank[:, at + n - P:at + n], ident[:, :], causal_q[:, :],
                                       start=False, stop=True, skip_group_check=True)
                mm.then_inc(sm_done.sem, 1)

            def turn_max(s):
                pe.wait_ge(*nm_ready(s + 1))
                pe.wait_ge(*o_copied(s * 2 - 1))
                for i in range(TILES):
                    mm = pe.transpose(tr[0:NMAX * G, i * P:i * P + P], nm3[:, i, :], ident[:, :])
                mm.then_inc(nm_turned.sem, 1)

            def scores(s, u, n):
                _, c, j, h0, per, q0, nq = UNITS[n]
                if n == 0:
                    pe.wait_ge(*nm_in(s + 1))
                pe.wait_ge(*exp_done(s * NU + n - 1))
                w = max(nq, 512) if nq > 256 else nq
                tile = st[n % 2]
                for h in range(h0, h0 + per):
                    at = (h - h0) * w
                    diag = q0 == P * j
                    mm = pe.matmul(tile[:, at:at + nq], ks[u][0:ROWS + NMAX, h, j * P:j * P + P],
                                   qs[u][0:ROWS + NMAX, h, q0:q0 + nq], start=True, stop=not diag,
                                   skip_group_check=True)
                    if diag:
                        mm = pe.matmul(tile[:, at:at + P], ident[:, :], causal_k[:, :],
                                       start=False, stop=True, skip_group_check=True)
                mm.then_inc(st_done.sem, 1)

            def values(s, u, k):
                c, j, q0, n, units_end = QUADS[k]
                pe.wait_ge(*exp_done(s * NU + units_end))
                if j == 0:
                    pe.wait_ge(*o_copied(s * 2 + c - 1))
                    if c == 0:
                        pe.wait_ge(*nm_copied(s + 1))
                for h in range(G):
                    mm = pe.matmul(o[c][h * VP:h * VP + VP, q0 - 512 * c:q0 - 512 * c + n],
                                   vs[u][:, j, h * VP:h * VP + VP], pt[k % 3][:, h, 0:n],
                                   start=j == 0, stop=j == 4 * c + 3, skip_group_check=True)
                mm.then_inc(pv_done.sem, 1)

            def step(b, s, u, more):
                for kind, n in interleave(more):
                    if kind == "sm":
                        if n == 0:
                            nb = b if u + 1 < NB else b + 1
                            pe.wait_ge(*loaded[(u + 1) % NB](nb + 1))
                        max_scores(s + 1, (u + 1) % NB, n)
                    elif kind == "turn":
                        turn_max(s + 1)
                    elif kind == "st":
                        scores(s, u, n)
                    else:
                        if n == 0:
                            pe.wait_ge(*v_loaded[u](b + 1))
                        values(s, u, n)

            pe.wait_ge(*loaded[0](1))
            for m in range(NM):
                max_scores(0, 0, m)
            turn_max(0)
            with pe.Fori(0, B - 1) as b:
                for g in range(NB):
                    step(b, b * NB + g, g, True)
            for g in range(NB):
                step(B - 1, (B - 1) * NB + g, g, g + 1 < NB)

        @block.scalar
        def _(ac):
            def copy_max(s):
                ac.wait_ge(*nm_turned(s + 1))
                ac.wait_ge(*nm_in(s))
                ac.activation(nmt[:, :], tr[0:NMAX * G, 0:T], ACT.Copy).then_inc(nm_copied.sem, 1)

            def copy_out(s, c):
                ac.wait_ge(*pv_done(s * NQ + (4 if c == 0 else NQ)))
                ac.wait_ge(*stored[c](s))
                ac.activation(ot[:, c], o[c][:, :], ACT.Copy).then_inc(o_copied.sem, 1)

            def step(s, u, more):
                for n, (k, c, j, h0, per, q0, nq) in enumerate(UNITS):
                    w = 512 if nq > 256 else nq
                    ac.wait_ge(*st_done(s * NU + n + 1))
                    ac.wait_ge(*pv_done(s * NQ + k - 2))
                    src = st[n % 2][:, 0:per * w].rearrange("p (h n) -> p h n", h=per)[:, :, 0:nq]
                    ac.activation(pt[k % 3][:, h0:h0 + per, 0:nq], src, ACT.Exp, scale=DH ** -0.5) \
                        .then_inc(exp_done.sem, 1)
                    if n == 9:
                        copy_out(s, 0)
                if more:
                    copy_max(s + 1)
                copy_out(s, 1)

            copy_max(0)
            steps(ac, step)

        @block.vector
        def _(ve):
            ch = Chain(ve, chain_v)
            ve.memset(mx[:, :, :, :], NEG * 10).then_inc(chain_v, 1)
            ve.wait_ge(chain_v, 1)

            def max_of(s, u):
                ch.start(s * VC + 1)
                for m, (i, part, h0, per, n, diag) in enumerate(MAXU):
                    ve.wait_ge(*sm_done(s * NM + m + 1))
                    ve.tensor_reduce(mx[:, part, i, h0:h0 + per],
                                     sm[m % 2][:, 0:per * n].rearrange("p (h n) -> p h n", h=per),
                                     AX.X, ALU.max).then_inc(sm_read.sem, 1)
                ve.wait_ge(*sm_read(s * NM + NM))
                ch.link(ve.tensor_tensor(mm_[:, :, :], mx[:, 0], mx[:, 1], ALU.max))
                ve.wait_ge(*nm_turned(s))
                part = [nm3[:, :, c * G:c * G + G] for c in range(NMAX)]
                ch.link(ve.tensor_scalar(part[0], mm_[:, :, :], -1.0, None, ALU.mult))
                ve.scalar_tensor_tensor(out=r1[:, :, :], in0=mm_[:, :, :], scalar=-1.0, in1=part[0],
                                        op0=ALU.mult, op1=ALU.subtract).then_inc(chain_v, 1)
                ve.wait_ge(chain_v, s * VC + 1 + 3)
                ve.tensor_copy(part[1], r1[:, :, :]).then_inc(split, 1)
                ve.wait_ge(split, s + 1)
                ve.tensor_tensor(part[2], r1[:, :, :], part[1], ALU.subtract).then_inc(nm_ready.sem, 1)

            max_of(0, 0)
            steps(ve, lambda s, u, more: max_of(s + 1, (u + 1) % NB) if more else None)


def dispatch(nc, xr, xr_t, slot_embeds, gamma, eye, ec_t, slots_t):
    E = 8
    with Phase(nc, "di") as ph:
        ident = ph.sb("ident", [P, P])
        ones = ph.sb("ones", [P, P])
        gam = ph.sb("gam", [P, D])
        emb = ph.sb("emb", [P, E, D])
        sq = ph.sb("sq", [P, D])
        ss = ph.sb("ss", [P, E])
        sn_t = ph.sb("sn_t", [P, 2, E * P])
        xs = [ph.sb(f"xs{u}", [P, TILES, D + 1]) for u in range(2)]
        xt = [ph.sb(f"xt{u}", [P, TILES, 2, P]) for u in range(2)]
        lg = [ph.sb(f"lg{u}", [P, TILES, E * P]) for u in range(2)]
        ec = ph.sb("ec", [P, 2, E, P])
        ect = ph.sb("ect", [P, 2, E, P])
        nmc = ph.sb("nmc", [P, 2])
        run = ph.sb("run", [P, E, P])
        maxd = ph.sb("maxd", [P, E])
        diag = ph.sb("diag", [P, E, P])
        mb = ph.sb("mb", [P, E * P])
        rec = ph.sb("rec", [P, 2])
        nat = ph.sb("nat", [P, 2, D])
        slt = ph.sb("slt", [P, 2, 2, P])
        pl = [ph.ps(f"pl{r}", [P, E, P]) for r in range(2)]
        tp = ph.ps("tp", [P, E, P])
        sl = ph.ps("sl", [P, 2, 512])

        const_in = ph.sem("const_in")
        ones_set = ph.sem("ones_set")
        slots_in = ph.sem("slots_in")
        prep_v = ph.sem("prep_v")
        prep_a = ph.sem("prep_a")
        prep_p = ph.sem("prep_p")
        xt_in = [ph.event(f"xt_in{u}", 16) for u in range(2)]
        xs_in = [ph.event(f"xs_in{u}", 16) for u in range(2)]
        l_done = ph.event("l_done")
        l_copied = ph.event("l_copied")
        nmc_ready = ph.event("nmc_ready")
        run_done = ph.event("run_done")
        ec_done = ph.event("ec_done")
        ec_turned = ph.event("ec_turned")
        ect_copied = ph.event("ect_copied")
        ect_stored = [ph.event(f"ect_stored{r}", 16) for r in range(2)]
        run_turned = ph.event("run_turned")
        maxd_done = ph.event("maxd_done")
        diag_ready = ph.event("diag_ready")
        mb_done = ph.event("mb_done")
        mb_copied = ph.event("mb_copied")
        ld_done = ph.event("ld_done")
        ed_done = ph.event("ed_done")
        slot_done = ph.event("slot_done", credit=E + 1)
        rec_done = ph.event("rec_done")
        nat_done = ph.event("nat_done")
        slt_turned = ph.event("slt_turned")
        slt_copied = ph.event("slt_copied")
        slt_stored = [ph.event(f"slt_stored{r}", 16) for r in range(2)]
        block = ph.block()
        N = TILES

        def steps(eng, step):
            with eng.Fori(0, B // 2 - 1) as k:
                for u in range(2):
                    step(k * 2 + u, k, u, True)
            for u in range(2):
                step(B - 2 + u, B // 2 - 1, u, u == 0)

        @block.sync
        def _(sp):
            sp.dma_start(ident[:, :], eye).then_inc(const_in, 16)
            sp.dma_start(gam[:, :], gamma.unsqueeze(0).broadcast_to((P, D))).then_inc(const_in, 16)
            sp.dma_start(emb[:, :, :], slot_embeds.rearrange("e s d -> s e d")).then_inc(slots_in, 16)
            ph.give_credits(sp)

            def load(b, u):
                sp.dma_start(xt[u][:, :, :, :], xr_t[bass.ds(b * N, N)].rearrange("i p c t -> p i c t")) \
                    .then_inc(xt_in[u].sem, 16)
                sp.dma_start(xs[u][:, :, 0:D], xr[bass.ds(b * N, N)].rearrange("i p d -> p i d")) \
                    .then_inc(xs_in[u].sem, 16)

            def store_ec(b, n):
                sp.wait_ge(*ect_copied(b * N + n + 1))
                sp.dma_start(ec_t[b * N + n], ect[:, n % 2]).then_inc(ect_stored[n % 2].sem, 16)

            load(0, 0)
            load(1, 1)
            for n in range(N):
                store_ec(0, n)

            def step(b, k, u, more):
                if more:
                    for n in range(N):
                        store_ec(b + 1, n)
                for m in range(E):
                    sp.wait_ge(*slt_copied(b * E + m + 1))
                    sp.dma_start(slots_t[m, :, :, b], slt[:, m % 2]).then_inc(slt_stored[m % 2].sem, 16)
                if not isinstance(b, int) or b + 2 < B:
                    load(b + 2, u)

            steps(sp, step)
            for r in range(2):
                sp.wait_ge(*ect_stored[r](B * N // 2))
                sp.wait_ge(*slt_stored[r](B * E // 2))

        @block.gpsimd
        def _(gp):
            gp.memset(ones[:, :], 1.0).then_inc(ones_set, 1)
            for u in range(2):
                gp.memset(xs[u][:, :, D:D + 1], 1.0).then_inc(ones_set, 1)

            def step(b, k, u, more):
                gp.wait_ge(*mb_copied(b + 1))
                for n in range(N):
                    gp.wait_ge(*l_copied(b * N + n + 1))
                    gp.tensor_tensor(lg[u][:, n], lg[u][:, n], mb[:, :], ALU.subtract).then_inc(ld_done.sem, 1)

            steps(gp, step)

        @block.tensor
        def _(pe):
            pe.wait_ge(const_in, 32)
            pe.wait_ge(ones_set, 3)
            for e in range(E):
                pe.wait_ge(prep_v, 2 * E + 3 + e)
                if e:
                    pe.wait_ge(prep_a, e + 1)
                for c in range(2):
                    mm = pe.transpose(tp[:, c], emb[:, e, c * P:c * P + P], ident[:, :])
                mm.then_inc(prep_p, 1)
            pe.wait_ge(prep_a, E + 1)

            def turn_ec(b, n):
                pe.wait_ge(*ec_done(b * N + n + 1))
                pe.wait_ge(*ect_copied(b * N + n))
                for c in range(E):
                    mm = pe.transpose(tp[:, c], ec[:, n % 2, c], ident[:, :])
                mm.then_inc(ec_turned.sem, 1)

            def logits(b, k, u):
                pe.wait_ge(*xt_in[u](k + 1))
                for n in range(N):
                    pe.wait_ge(*l_copied(b * N + n - 1))
                    for c2 in range(2):
                        for c in range(2):
                            mm = pe.matmul(pl[n % 2][:, 4 * c2:4 * c2 + 4], xt[u][:, n, c],
                                           sn_t[:, c, c2 * 512:c2 * 512 + 512], start=c == 0, stop=c == 1)
                    mm.then_inc(l_done.sem, 1)
                    if n:
                        turn_ec(b, n - 1)
                turn_ec(b, N - 1)

            logits(0, 0, 0)

            def step(b, k, u, more):
                pe.wait_ge(*run_done(b * N + N))
                pe.wait_ge(*ect_copied(b * N + N))
                pe.wait_ge(*slt_copied(b * E))
                for c in range(E):
                    mm = pe.transpose(tp[:, c], run[:, c], ident[:, :])
                mm.then_inc(run_turned.sem, 1)
                pe.wait_ge(*diag_ready(b + 1))
                pe.wait_ge(*nat_done(b * E))
                for c in range(2):
                    mm = pe.matmul(sl[:, c, :], ones[:, :], diag[:, 4 * c:4 * c + 4], start=True, stop=True)
                mm.then_inc(mb_done.sem, 1)
                if more:
                    logits(b + 1, k + u, 1 - u)
                pe.wait_ge(*xs_in[u](k + 1))
                pe.wait_ge(*mb_copied(b + 1))
                for m in range(E + 1):
                    if m < E:
                        pe.wait_ge(*nat_done(b * E + m - 1))
                        for n in range(N):
                            if m == 0:
                                pe.wait_ge(*ed_done(b * N + n + 1))
                            mm = pe.matmul(sl[:, m % 2, 0:D + 1], lg[u][:, n, m * P:m * P + P], xs[u][:, n],
                                           start=n == 0, stop=n == N - 1)
                        mm.then_inc(slot_done.sem, 1)
                    if m:
                        pe.wait_ge(*nat_done(b * E + m))
                        pe.wait_ge(*slt_copied(b * E + m - 2))
                        if m == 1:
                            pe.wait_ge(*maxd_done(b + 1))
                            pe.wait_ge(*ect_copied(b * N + N + (N if more else 0)))
                        for c in range(2):
                            at = 4 * ((m - 1) % 2) + c
                            mm = pe.transpose(tp[:, at], nat[:, (m - 1) % 2, c * P:c * P + P], ident[:, :])
                        mm.then_inc(slt_turned.sem, 1)

            steps(pe, step)

        @block.scalar
        def _(ac):
            ac.wait_ge(prep_v, E)
            ac.activation(ss[:, :], ss[:, :], ACT.Sqrt).then_inc(prep_a, 1)
            for e in range(E):
                ac.wait_ge(prep_p, e + 1)
                ac.activation(sn_t[:, :, e * P:e * P + P], tp[:, 0:2], ACT.Copy).then_inc(prep_a, 1)

            def logit_tile(b, u, n):
                ac.wait_ge(*l_done(b * N + n + 1))
                ac.wait_ge(*slot_done(b * E - E))
                ac.activation(lg[u][:, n], pl[n % 2][:, :, :].rearrange("p e s -> p (e s)"), ACT.Copy) \
                    .then_inc(l_copied.sem, 1)
                ac.wait_ge(*nmc_ready(b * N + n + 1))
                ac.wait_ge(*ec_turned(b * N + n - 1))
                ac.activation(ec[:, n % 2], lg[u][:, n].rearrange("p (e s) -> p e s", s=P), ACT.Exp, bias=nmc[:, n % 2:n % 2 + 1]) \
                    .then_inc(ec_done.sem, 1)

            for n in range(N):
                logit_tile(0, 0, n)

            def step(b, k, u, more):
                ac.wait_ge(*mb_done(b + 1))
                ac.wait_ge(*ld_done(b * N))
                ac.activation(mb[:, :], sl[:, :, :].rearrange("p c n -> p (c n)"), ACT.Copy).then_inc(mb_copied.sem, 1)
                for n in range(N):
                    if more:
                        logit_tile(b + 1, 1 - u, n)
                    ac.wait_ge(*ld_done(b * N + n + 1))
                    ac.activation(lg[u][:, n], lg[u][:, n], ACT.Exp).then_inc(ed_done.sem, 1)
                for m in range(E):
                    ac.wait_ge(*slt_turned(b * E + m + 1))
                    ac.wait_ge(*slt_stored[m % 2](b * (E // 2) + m // 2))
                    ac.activation(slt[:, m % 2], tp[:, 4 * (m % 2):4 * (m % 2) + 2], ACT.Copy).then_inc(slt_copied.sem, 1)

            steps(ac, step)

        @block.vector
        def _(ve):
            ve.wait_ge(slots_in, 16)
            ve.wait_ge(const_in, 32)
            for e in range(E):
                if e:
                    ve.wait_ge(prep_v, e)
                ve.tensor_tensor_reduce(sq[:, :], emb[:, e], emb[:, e], 1.0, 0.0, ALU.mult, ALU.add,
                                        ss[:, e:e + 1]).then_inc(prep_v, 1)
            ve.wait_ge(prep_a, 1)
            ve.tensor_scalar(ss[:, :], ss[:, :], 1e-12, None, ALU.max).then_inc(prep_v, 1)
            ve.wait_ge(prep_v, E + 1)
            ve.reciprocal(ss[:, :], ss[:, :]).then_inc(prep_v, 1)
            ve.wait_ge(prep_v, E + 2)
            for e in range(E):
                ve.tensor_scalar(emb[:, e], emb[:, e], ss[:, e:e + 1], float(D) ** 0.5, ALU.mult, ALU.mult) \
                    .then_inc(prep_v, 1)
            for e in range(E):
                ve.wait_ge(prep_v, E + 3 + e)
                ve.tensor_tensor(emb[:, e], emb[:, e], gam[:, :], ALU.mult).then_inc(prep_v, 1)

            def copy_ect(b, n):
                ve.wait_ge(*ec_turned(b * N + n + 1))
                ve.wait_ge(*ect_stored[n % 2](b * (N // 2) + n // 2))
                ve.tensor_copy(ect[:, n % 2], tp[:, :, :]).then_inc(ect_copied.sem, 1)

            def logit_tiles(b, u):
                for n in range(N):
                    ve.wait_ge(*l_copied(b * N + n + 1))
                    tile = lg[u][:, n].rearrange("p (e s) -> p e s", s=P)
                    ve.wait_ge(*ec_done(b * N + n - 1))
                    ve.tensor_reduce(nmc[:, n % 2:n % 2 + 1], lg[u][:, n],
                                     AX.X, ALU.max, negate=True).then_inc(nmc_ready.sem, 1)
                    if n == 0:
                        ve.wait_ge(*run_turned(b))
                        ve.tensor_copy(run[:, :, :], tile).then_inc(run_done.sem, 1)
                    else:
                        ve.wait_ge(*run_done(b * N + n))
                        ve.tensor_tensor(run[:, :, :], tile, run[:, :, :], ALU.max) \
                            .then_inc(run_done.sem, 1)
                        copy_ect(b, n - 1)
                copy_ect(b, N - 1)

            logit_tiles(0, 0)

            def step(b, k, u, more):
                ve.wait_ge(*run_turned(b + 1))
                ve.tensor_reduce(maxd[:, :], tp[:, :, :], AX.X, ALU.max).then_inc(maxd_done.sem, 1)
                ve.wait_ge(*maxd_done(b + 1))
                ve.wait_ge(*mb_done(b))
                ve.tensor_tensor(diag[:, :, :], ident[:, :].unsqueeze(1).broadcast_to((P, E, P)),
                                 maxd[:, :].unsqueeze(2).broadcast_to((P, E, P)), ALU.mult).then_inc(diag_ready.sem, 1)
                if more:
                    logit_tiles(b + 1, 1 - u)
                for m in range(E):
                    ve.wait_ge(*slot_done(b * E + m + 1))
                    ve.reciprocal(rec[:, m % 2:m % 2 + 1], sl[:, m % 2, D:D + 1]).then_inc(rec_done.sem, 1)
                    ve.wait_ge(*rec_done(b * E + m + 1))
                    ve.wait_ge(*slt_turned(b * E + m - 1))
                    ve.tensor_scalar(nat[:, m % 2], sl[:, m % 2, 0:D], rec[:, m % 2:m % 2 + 1], None, ALU.mult) \
                        .then_inc(nat_done.sem, 1)

            steps(ve, step)
def experts(nc, slots_t, w1, b1_t, w2, b2, eo):
    E, HID = 8, 4 * D
    F, BH = HID // P, B // 2
    UNITS, CHUNKS = 2 * F, 4
    with Phase(nc, "ex") as ph:
        raw = ph.sb("raw", [P, 2, CHUNKS, 1024])
        w2s = ph.sb("w2s", [P, 2, F * D])
        b1s = ph.sb("b1s", [P, 2, F])
        b2s = ph.sb("b2s", [P, 2, D])
        xw = ph.sb("xw", [P, 2, CHUNKS, 1024], F32R)
        w2r = ph.sb("w2r", [P, 2, F * D], F32R)
        ht = ph.sb("ht", [P, 4, 512])
        hr = ph.sb("hr", [P, 2, UNITS, 512], F32R)
        eos = ph.sb("eos", [P, 2, D])
        pht = [ph.ps(f"pht{r}", [P, 512]) for r in range(4)]
        peo = [ph.ps(f"peo{r}", [P, 512]) for r in range(2)]
        loaded = [ph.event(f"loaded{u}", 16 * 5) for u in range(2)]
        h_done = ph.event("h_done", credit=UNITS)
        gelu_done = ph.event("gelu_done", credit=4)
        h_hi = ph.event("h_hi", credit=4)
        h_lo = ph.event("h_lo", credit=4)
        xw_hi = ph.event("xw_hi", credit=2 * CHUNKS)
        xw_lo = ph.event("xw_lo", credit=2 * CHUNKS)
        w2_hi = ph.event("w2_hi")
        w2_lo = ph.event("w2_lo")
        eo_done = ph.event("eo_done", credit=2 * BH)
        eo_ready = ph.event("eo_ready", credit=B)
        stored = [ph.event(f"stored{r}", 16) for r in range(2)]
        block = ph.block()
        PARTS = ((0, 0), (0, 1), (1, 0))
        W2_AT = 4

        def loops(eng, body):
            with eng.Fori(0, E // 2 - 1) as k:
                for u in range(2):
                    body(k * 2 + u, k, u, True)
            for u in range(2):
                body(E - 2 + u, E // 2 - 1, u, u == 0)

        @block.sync
        def _(sp):
            ph.give_credits(sp)

            def load(e, k, u):
                sp.wait_ge(*eo_ready((e - 1) * B))
                for dst, src in ((raw[:, u, 0:2], slots_t[e].rearrange("p c b s -> p c (b s)")),
                                 (raw[:, u, 2:4], w1[e].rearrange("(c p) h -> p c h", p=P)),
                                 (w2s[:, u].rearrange("p (f d) -> p f d", d=D), w2[e].rearrange("(f p) d -> p f d", p=P)),
                                 (b1s[:, u], b1_t[e]),
                                 (b2s[:, u], b2[bass.ds(e, 1)].broadcast_to((P, D)))):
                    sp.dma_start(dst, src).then_inc(loaded[u].sem, 16)

            def store(e, k, u):
                for n in range(B):
                    sp.wait_ge(*eo_ready(e * B + n + 1))
                    sp.dma_start(eo[n, e], eos[:, n % 2]).then_inc(stored[n % 2].sem, 16)

            staggered(sp, E, [(2, store), (0, load)])
            for r in range(2):
                sp.wait_ge(*stored[r](E * B // 2))

        @block.tensor
        def _(pe):
            def body(e, k, u, more):
                for c in range(2):
                    for f in range(F):
                        i = c * F + f
                        if i == 0:
                            pe.wait_ge(*xw_lo(e * CHUNKS + CHUNKS))
                        pe.wait_ge(*gelu_done(e * UNITS + i - 3))
                        for n, (a, b) in enumerate(PARTS):
                            for d in range(2):
                                mm = pe.matmul(pht[f % 4][:, :], xw[:, a, 2 + d, f * P:f * P + P],
                                               xw[:, b, d, c * 512:c * 512 + 512],
                                               start=n == 0 and d == 0, stop=n == 2 and d == 1)
                        mm.then_inc(h_done.sem, 1)
                for n in range(B):
                    c = n // BH
                    pe.wait_ge(*h_lo(e * UNITS + (c + 1) * F))
                    pe.wait_ge(*w2_lo(e + 1))
                    pe.wait_ge(*eo_ready(e * B + n - 1))
                    at = (n % BH) * P
                    for f in range(F):
                        for m, (a, b) in enumerate(PARTS):
                            mm = pe.matmul(peo[n % 2][:, 0:D], hr[:, a, c * F + f, at:at + P], w2r[:, b, f * D:f * D + D],
                                           start=f == 0 and m == 0, stop=f == F - 1 and m == 2)
                    mm.then_inc(eo_done.sem, 1)

            loops(pe, body)

        @block.scalar
        def _(ac):
            def split_inputs(e, k, u):
                ac.wait_ge(*loaded[u](k + 1))
                ac.wait_ge(*h_done(e * UNITS))
                for n in range(CHUNKS):
                    ac.activation(xw[:, 0, n], raw[:, u, n], ACT.Copy).then_inc(xw_hi.sem, 1)

            def keep_hi(e, k, i):
                if i == 0:
                    ac.wait_ge(*eo_done(e * B))
                ac.wait_ge(*gelu_done(e * UNITS + i + 1))
                ac.activation(hr[:, 0, i], ht[:, i % 4], ACT.Copy).then_inc(h_hi.sem, 1)

            def body(e, k, u, more):
                for i in range(UNITS):
                    ac.wait_ge(*h_done(e * UNITS + i + 1))
                    ac.wait_ge(*h_lo(e * UNITS + i - 3))
                    ac.activation(ht[:, i % 4], pht[i % 4][:, :], ACT.Gelu,
                                  bias=b1s[:, u, i % F:i % F + 1]).then_inc(gelu_done.sem, 1)
                    if i > 0:
                        keep_hi(e, k, i - 1)
                    if i == W2_AT:
                        ac.wait_ge(*eo_done(e * B))
                        ac.activation(w2r[:, 0], w2s[:, u], ACT.Copy).then_inc(w2_hi.sem, 1)
                keep_hi(e, k, UNITS - 1)
                if more:
                    split_inputs(e + 1, k + u, 1 - u)

            split_inputs(0, 0, 0)
            loops(ac, body)

        @block.vector
        def _(ve):
            def split_input(e, k, u, n):
                ve.wait_ge(*xw_hi(e * CHUNKS + n + 1))
                ve.tensor_tensor(xw[:, 1, n], raw[:, u, n], xw[:, 0, n], ALU.subtract).then_inc(xw_lo.sem, 1)

            def body(e, k, u, more):
                for i in range(UNITS):
                    ve.wait_ge(*h_hi(e * UNITS + i + 1))
                    ve.tensor_tensor(hr[:, 1, i], ht[:, i % 4], hr[:, 0, i], ALU.subtract).then_inc(h_lo.sem, 1)
                    if i == W2_AT:
                        ve.wait_ge(*w2_hi(e + 1))
                        ve.tensor_tensor(w2r[:, 1], w2s[:, u], w2r[:, 0], ALU.subtract).then_inc(w2_lo.sem, 1)
                for n in range(B):
                    if more and n < CHUNKS:
                        split_input(e + 1, k + u, 1 - u, n)
                    ve.wait_ge(*eo_done(e * B + n + 1))
                    ve.wait_ge(*stored[n % 2](e * (B // 2) + n // 2))
                    ve.tensor_tensor(eos[:, n % 2], peo[n % 2][:, 0:D], b2s[:, u], ALU.add).then_inc(eo_ready.sem, 1)

            for n in range(CHUNKS):
                split_input(0, 0, 0, n)
            loops(ve, body)


def mix_and_gate(nc, x, ec_t, eo, o_t, wo_t, eye, x1):
    E = 8
    with Phase(nc, "mx") as ph:
        x_n = x.rearrange("b (i p) d -> (b i) p d", p=P)
        ident = ph.sb("ident", [P, P])
        wo = ph.sb("wo", [P, 2, D])
        eos = ph.sb("eos", [P, 2 * E, D + 1])
        ect = ph.sb("ect", [P, 4, E, P])
        ot = ph.sb("ot", [P, 4, G, P])
        xt = ph.sb("xt", [P, 8, D])
        rden = ph.sb("rden", [P, 2, H])
        on = ph.sb("on", [P, 2, H, DH])
        ont = ph.sb("ont", [P, 2, 2, P])
        rc = ph.sb("rc", [P, 2])
        ff = ph.sb("ff", [P, 2, D])
        sigm = ph.sb("sigm", [P, 2, D])
        gate = ph.sb("gate", [P, D])
        sg = ph.sb("sg", [P, D])
        xo = ph.sb("xo", [P, 4, D])
        pc = [ph.ps(f"pc{r}", [P, 512]) for r in range(2)]
        pt = [ph.ps(f"pt{r}", [P, H, VP]) for r in range(2)]
        pn = [ph.ps(f"pn{r}", [P, 2, P]) for r in range(2)]
        pw = [ph.ps(f"pw{r}", [P, 512]) for r in range(2)]
        const_in = ph.sem("const_in")
        ones_set = ph.sem("ones_set")
        passed = ph.sem("passed")
        sig = lambda name, unit=1: ph.event(name, unit, credit=8)
        eo_in = ph.event("eo_in", 16, credit=0)
        tile_in = [sig(f"tile_in{u}", 16 * 3) for u in range(4)]
        mixed = ph.event("mixed", credit=TILES + 1)
        o_turned = sig("o_turned")
        o_rec = sig("o_rec")
        o_ready = sig("o_ready")
        on_turned = sig("on_turned")
        on_copied = sig("on_copied")
        projected = sig("projected")
        rc_done = sig("rc_done")
        ff_done = sig("ff_done")
        sigmoid_done = sig("sigmoid_done")
        gate_done = sig("gate_done")
        s_done = sig("s_done")
        x_done = sig("x_done")
        stored = [sig(f"stored{u}", 16) for u in range(4)]
        block = ph.block()
        quarter = lambda k, i: k * (TILES // 4) + i // 4

        @block.sync
        def _(sp):
            sp.dma_start(ident[:, :], eye).then_inc(const_in, 16)
            sp.dma_start(wo[:, :, :], wo_t.rearrange("(c p) n -> p c n", p=P)).then_inc(const_in, 16)
            ph.give_credits(sp)

            def load(t, b, i):
                u = i % 4
                sp.wait_ge(*mixed(t - 3))
                sp.dma_start(ect[:, u], ec_t[t]).then_inc(tile_in[u].sem, 16)
                sp.wait_ge(*o_turned(t - 3))
                sp.dma_start(ot[:, u], o_t[b, :, :, i].rearrange("g p t -> p g t")).then_inc(tile_in[u].sem, 16)
                sp.wait_ge(*x_done(t - 7))
                sp.dma_start(xt[:, i], x_n[t]).then_inc(tile_in[u].sem, 16)

            def store(t, b, i):
                sp.wait_ge(*x_done(t + 1))
                sp.dma_start(x1[t], xo[:, i % 4]).then_inc(stored[i % 4].sem, 16)

            staggered(sp, ALL, [(0, load), (5, store)], TILES)
            for u in range(4):
                sp.wait_ge(*stored[u](ALL // 4))

        @block.gpsimd
        def _(gp):
            gp.memset(eos[:, :, D:D + 1], 1.0).then_inc(ones_set, 1)
            for v in range(2):
                gp.dma_start(eos[:, v * E:v * E + E, 0:D], eo[v].rearrange("e p d -> p e d")).then_inc(eo_in.sem, 16)
                gp.wait_ge(*eo_in(v + 1))
            with gp.Fori(0, B // 2 - 1) as pair:
                b = pair * 2
                for v in range(2):
                    gp.wait_ge(*mixed(b * TILES + (v + 1) * TILES))
                    gp.sem_inc(passed, 1)
                    gp.dma_start(eos[:, v * E:v * E + E, 0:D], eo[b + v + 2].rearrange("e p d -> p e d")) \
                        .then_inc(eo_in.sem, 16)
                    gp.wait_ge(*eo_in(b + v + 3))
                    gp.sem_inc(passed, 1)

        @block.tensor
        def _(pe):
            pe.wait_ge(const_in, 32)
            pe.wait_ge(ones_set, 1)

            def turn_and_mix(t, b, i):
                u = i % 2
                pe.wait_ge(*tile_in[i % 4](quarter(b, i) + 1))
                pe.wait_ge(*o_ready(t - 1))
                for g in range(G):
                    mm = pe.transpose(pt[u][:, g * G:g * G + G].rearrange("p h d -> p (h d)"), ot[:, i % 4, g], ident[:, :])
                mm.then_inc(o_turned.sem, 1)
                pe.wait_ge(*eo_in(b + 1))
                pe.wait_ge(*ff_done(t - 1))
                first = (b % 2) * E
                for m in range(E):
                    mm = pe.matmul(pc[u][:, 0:D + 1], ect[:, i % 4, m], eos[:, bass.ds(first + m, 1)].rearrange("p a d -> p (a d)"),
                                   start=m == 0, stop=m == E - 1)
                mm.then_inc(mixed.sem, 1)

            def turn_back(t, b, i):
                u = i % 2
                pe.wait_ge(*o_ready(t + 1))
                pe.wait_ge(*on_copied(t - 1))
                for c in range(2):
                    mm = pe.transpose(pn[u][:, c], on[:, u, 8 * c:8 * c + 8].rearrange("p h d -> p (h d)"), ident[:, :])
                mm.then_inc(on_turned.sem, 1)

            def project(t, b, i):
                u = i % 2
                pe.wait_ge(*on_copied(t + 1))
                pe.wait_ge(*s_done(t - 1))
                for c in range(2):
                    mm = pe.matmul(pw[u][:, 0:D], ont[:, u, c], wo[:, c], start=c == 0, stop=c == 1)
                mm.then_inc(projected.sem, 1)

            staggered(pe, ALL, [(3, project), (2, turn_back), (1, turn_and_mix)], TILES)

        @block.scalar
        def _(ac):
            def copies(t, b, i):
                u = i % 2
                ac.wait_ge(*ff_done(t + 1))
                ac.wait_ge(*gate_done(t - 1))
                ac.activation(sigm[:, u], ff[:, u], ACT.Sigmoid).then_inc(sigmoid_done.sem, 1)
                ac.wait_ge(*on_turned(t + 1))
                ac.wait_ge(*projected(t - 1))
                ac.activation(ont[:, u], pn[u][:, :, :], ACT.Copy).then_inc(on_copied.sem, 1)

            staggered(ac, ALL, [(2, copies)], TILES)

        @block.vector
        def _(ve):
            def divide(t, b, i):
                u = i % 2
                ve.wait_ge(*o_turned(t + 1))
                ve.reciprocal(rden[:, u], pt[u][:, :, DH]).then_inc(o_rec.sem, 1)
                ve.wait_ge(*o_rec(t + 1))
                ve.wait_ge(*on_turned(t - 1))
                ve.tensor_tensor(on[:, u], pt[u][:, :, 0:DH], rden[:, u].unsqueeze(2).broadcast_to((P, H, DH)), ALU.mult) \
                    .then_inc(o_ready.sem, 1)
                ve.wait_ge(*mixed(t + 1))
                ve.reciprocal(rc[:, u:u + 1], pc[u][:, D:D + 1]).then_inc(rc_done.sem, 1)
                ve.wait_ge(*rc_done(t + 1))
                ve.wait_ge(*gate_done(t - 1))
                ve.tensor_scalar(ff[:, u], pc[u][:, 0:D], rc[:, u:u + 1], None, ALU.mult).then_inc(ff_done.sem, 1)

            def gate_step(t, b, i):
                u = i % 2
                ve.wait_ge(*sigmoid_done(t + 1))
                ve.tensor_tensor(gate[:, :], ff[:, u], sigm[:, u], ALU.mult).then_inc(gate_done.sem, 1)
                ve.wait_ge(*gate_done(t + 1))
                ve.wait_ge(*projected(t + 1))
                ve.tensor_tensor(sg[:, :], pw[u][:, 0:D], gate[:, :], ALU.mult).then_inc(s_done.sem, 1)
                ve.wait_ge(*s_done(t + 1))
                ve.wait_ge(*stored[i % 4](quarter(b, i)))
                ve.tensor_tensor(xo[:, i % 4], sg[:, :], xt[:, i], ALU.add).then_inc(x_done.sem, 1)

            staggered(ve, ALL, [(3, gate_step), (1, divide)], TILES)


SEG = 64
W1 = H + 1
ONE = DH + 1


def project_memory(nc, x1, w_qkv, wu_t, wu, wo_norm, seg_avg, run_avg, seg_mask, eye, xn_d, qk_t, pk_d, v_d, gates_d):
    with Phase(nc, "pm") as ph:
        ident = ph.sb("ident", [P, P])
        w_s = ph.sb("w_s", [P, 2, 3 * D])
        wut_s = ph.sb("wut_s", [P, 2, D])
        wu_s = ph.sb("wu_s", [P, 2, D])
        nw = ph.sb("nw", [P, D])
        savg = ph.sb("savg", [P, 2])
        ravg = ph.sb("ravg", [P, P])
        smask = ph.sb("smask", [P, 1])
        half = ph.sb("half", [P, 2])
        xt = ph.sb("xt", [P, 4, D])
        stat = ph.sb("stat", [P, 6])
        mv = ph.sb("mv", [P, 2, 2])
        v2 = ph.sb("v2", [P, 2, 2])
        rs = ph.sb("rs", [P, 2, 2])
        xn = ph.sb("xn", [P, 4, D])
        xm = ph.sb("xm", [P, D])
        xr = ph.sb("xr", [P, 2, D])
        xT = ph.sb("xT", [P, 2, 4, P])
        mt = ph.sb("mt", [P, 2, 2, 2])
        neg = ph.sb("neg", [P, 2 * D])
        eq = ph.sb("eq", [P, 2 * D])
        pqk = ph.sb("pqk", [P, 4, 2 * D])
        qkT = ph.sb("qkT", [P, 4, 4, P])
        vp = ph.sb("vp", [P, 4, H, VP])
        mc = ph.sb("mc", [P, D])
        junk = ph.sb("junk", [P, D])
        gcol = ph.sb("gcol", [P, 2, H])
        gs = ph.sb("gs", [P, 4, W1])
        nm = ph.sb("nm", [P, 1])
        nms = ph.sb("nms", [P, 1])
        ge = ph.sb("ge", [P, W1])
        gsum = ph.sb("gsum", [P, 1])
        grec = ph.sb("grec", [P, 1])
        gate = ph.sb("gate", [P, 4, W1])
        p_t = ph.ps("p_t", [P, 4, P])
        p_m = ph.ps("p_m", [P, 2, 2])
        p_qk = ph.ps("p_qk", [P, 2 * D])
        p_vu = ph.ps("p_vu", [P, 2 * D])
        p_mc = ph.ps("p_mc", [P, D])
        p_g = ph.ps("p_g", [P, 2, 2])
        p_sc = ph.ps("p_sc", [P, H])
        p_tq = ph.ps("p_tq", [P, 4, P])

        const_in = ph.sem("const_in")
        preset = ph.sem("preset")
        passed = ph.sem("passed")
        carried = ph.sem("carried")
        sig = lambda name, unit=1: ph.event(name, unit, credit=6)
        loaded = [sig(f"loaded{u}", 16) for u in range(4)]
        stat_done = sig("stat_done")
        mv_done = sig("mv_done")
        v2_done = sig("v2_done")
        rs_done = sig("rs_done")
        xn_done = sig("xn_done")
        xm_done = sig("xm_done")
        xr_done = sig("xr_done")
        turned = sig("turned")
        turn_copied = sig("turn_copied")
        mt_copied = sig("mt_copied")
        projected = sig("projected")
        g_made = sig("g_made")
        g_copied = sig("g_copied")
        neg_done = sig("neg_done")
        eq_done = sig("eq_done")
        pqk_done = sig("pqk_done")
        v_copied = sig("v_copied")
        mc_copied = sig("mc_copied")
        cur_done = sig("cur_done")
        qk_turned = sig("qk_turned")
        qk_copied = sig("qk_copied")
        sc_done = sig("sc_done")
        gs_copied = sig("gs_copied")
        gs_masked = sig("gs_masked")
        nm_done = sig("nm_done")
        nms_done = sig("nms_done")
        ge_done = sig("ge_done")
        grec_done = sig("grec_done")
        gate_done = sig("gate_done")
        xn_stored = [sig(f"xn_stored{u}", 16) for u in range(4)]
        stored = [sig(f"stored{u}", 16 * 4) for u in range(4)]
        block = ph.block()
        R = TILES
        quarter = lambda k, i: k * (R // 4) + i // 4

        @block.sync
        def _(sp):
            for dst, src in ((ident[:, :], eye), (w_s[:, :, :], w_qkv.rearrange("(c p) n -> p c n", p=P)),
                             (wut_s[:, :, :], wu_t.rearrange("(c p) n -> p c n", p=P)),
                             (wu_s[:, :, :], wu.rearrange("(c p) n -> p c n", p=P)),
                             (nw[:, :], wo_norm.unsqueeze(0).broadcast_to((P, D))),
                             (savg[:, :], seg_avg), (ravg[:, :], run_avg), (smask[:, :], seg_mask)):
                sp.dma_start(dst, src).then_inc(const_in, 16)
            ph.give_credits(sp)

            def load(t, k, i):
                sp.wait_ge(*xm_done(t - 3))
                sp.dma_start(xt[:, i % 4], x1[t]).then_inc(loaded[i % 4].sem, 16)

            def store_xn(t, k, i):
                sp.wait_ge(*xn_done(t + 1))
                sp.dma_start(xn_d[t], xn[:, i % 4]).then_inc(xn_stored[i % 4].sem, 16)

            def store(t, k, i):
                u = i % 4
                sp.wait_ge(*pqk_done(t + 1))
                sp.dma_start(pk_d[t], pqk[:, u, D:2 * D]).then_inc(stored[u].sem, 16)
                sp.wait_ge(*v_copied(t + 1))
                sp.dma_start(v_d[t], vp[:, u].rearrange("p h d -> p (h d)")).then_inc(stored[u].sem, 16)
                sp.wait_ge(*qk_copied(t + 1))
                sp.dma_start(qk_t[t], qkT[:, u].rearrange("p c t -> p (c t)")).then_inc(stored[u].sem, 16)
                sp.wait_ge(*gate_done(t + 1))
                sp.dma_start(gates_d[t], gate[:, u]).then_inc(stored[u].sem, 16)

            staggered(sp, ALL, [(0, load), (6, store), (3, store_xn)], R)
            for u in range(4):
                sp.wait_ge(*xn_stored[u](ALL // 4))
                sp.wait_ge(*stored[u](ALL // 4))

        @block.gpsimd
        def _(gp):
            gp.memset(half[:, :], -0.5).then_inc(preset, 1)
            gp.memset(gate[:, :, :], 0.0).then_inc(preset, 1)
            gp.memset(vp[:, :, :, :], 0.0).then_inc(passed, 1)
            gp.wait_ge(passed, 1)
            gp.memset(vp[:, :, :, DH:DH + 1], 1.0).then_inc(preset, 1)
            gp.wait_ge(preset, 3)
            gp.wait_ge(const_in, 8 * 16)

            def roots(t, k, i):
                u = i % 2
                gp.wait_ge(*v2_done(t + 1))
                gp.wait_ge(*xm_done(t - 1))
                gp.tensor_tensor(rs[:, u], v2[:, u], half[:, :], ALU.pow).then_inc(rs_done.sem, 1)

            def scale(t, k, i):
                u = i % 2
                gp.wait_ge(*xm_done(t + 1))
                gp.wait_ge(*turned(t - 1))
                gp.tensor_tensor(xr[:, u], xm[:, :], nw[:, :], ALU.mult).then_inc(xr_done.sem, 1)

            staggered(gp, ALL, [(2, scale), (1, roots)], R)

        @block.vector
        def _(ve):
            ve.wait_ge(preset, 3)
            ve.wait_ge(const_in, 8 * 16)

            def stats(t, k, i):
                u = i % 2
                ve.wait_ge(*loaded[i % 4](quarter(k, i) + 1))
                ve.bn_stats(stat[:, :], xt[:, i % 4]).then_inc(stat_done.sem, 1)
                ve.wait_ge(*stat_done(t + 1))
                ve.sem_inc(carried, 1)
                ve.bn_aggr(mv[:, u], stat[:, :]).then_inc(mv_done.sem, 1)
                ve.wait_ge(*mv_done(t + 1))
                ve.wait_ge(*rs_done(t - 1))
                ve.tensor_scalar(v2[:, u, 0:1], mv[:, u, 1:2], LN_EPS, None, ALU.add)
                ve.tensor_scalar(v2[:, u, 1:2], mv[:, u, 1:2], 1 + RMS_EPS, RMS_EPS * LN_EPS, ALU.mult, ALU.add) \
                    .then_inc(v2_done.sem, 1)

            def norms(t, k, i):
                u = i % 2
                ve.wait_ge(*rs_done(t + 1))
                ve.wait_ge(*xn_stored[i % 4](quarter(k, i)))
                ve.wait_ge(*projected(t - 3))
                ve.tensor_scalar(xn[:, i % 4], xt[:, i % 4], mv[:, u, 0:1], rs[:, u, 0:1], ALU.subtract, ALU.mult) \
                    .then_inc(xn_done.sem, 1)
                ve.wait_ge(*xr_done(t))
                ve.tensor_scalar(xm[:, :], xt[:, i % 4], mv[:, u, 0:1], rs[:, u, 1:2], ALU.subtract, ALU.mult) \
                    .then_inc(xm_done.sem, 1)

            def elu(t, k, i):
                u = i % 2
                ve.wait_ge(*projected(t + 1))
                ve.wait_ge(*eq_done(t))
                ve.tensor_scalar(neg[:, :], p_qk[:, :], 0.0, None, ALU.min).then_inc(neg_done.sem, 1)
                ve.wait_ge(*mc_copied(t + 1))
                ve.wait_ge(*v_copied(t + 1))
                ve.wait_ge(*gate_done(t - 3))
                ve.tensor_tensor_reduce(junk[:, :], p_vu[:, D:2 * D], mc[:, :], 1.0, 0.0, ALU.mult, ALU.add,
                                        gs[:, i % 4, 2 * i + 1:2 * i + 2]).then_inc(cur_done.sem, 1)
                ve.wait_ge(*eq_done(t + 1))
                ve.wait_ge(*qk_turned(t - 1))
                ve.wait_ge(*stored[i % 4](quarter(k, i)))
                ve.scalar_tensor_tensor(out=pqk[:, i % 4], in0=p_qk[:, :], scalar=0.0, in1=eq[:, :],
                                        op0=ALU.max, op1=ALU.add).then_inc(pqk_done.sem, 1)

            def gates(t, k, i):
                u, n = i % 2, 2 * i + 1
                g = gs[:, i % 4]
                ve.wait_ge(*sc_done(t + 1))
                if i:
                    ve.tensor_copy(g[:, 0:n - 1], p_sc[:, 0:n - 1])
                ve.tensor_scalar(g[:, n - 1:n], p_sc[:, n - 1:n], smask[:, :], None, ALU.add).then_inc(gs_copied.sem, 1)
                ve.wait_ge(*gs_copied(t + 1))
                ve.wait_ge(*cur_done(t + 1))
                ve.tensor_reduce(nm[:, :], g[:, 0:n + 1], AX.X, ALU.max, negate=True).then_inc(nm_done.sem, 1)
                ve.wait_ge(*nm_done(t + 1))
                ve.wait_ge(*ge_done(t))
                ve.tensor_scalar(nms[:, :], nm[:, :], float(D) ** -0.5, None, ALU.mult).then_inc(nms_done.sem, 1)

            def gates_end(t, k, i):
                u, n = i % 2, 2 * i + 1
                ve.wait_ge(*ge_done(t + 1))
                ve.reciprocal(grec[:, :], gsum[:, :]).then_inc(grec_done.sem, 1)
                ve.wait_ge(*grec_done(t + 1))
                ve.wait_ge(*stored[i % 4](quarter(k, i)))
                ve.tensor_scalar(gate[:, i % 4, 1:n + 1], ge[:, 0:n], grec[:, :], None, ALU.mult)
                ve.tensor_scalar(gate[:, i % 4, 0:1], ge[:, n:n + 1], grec[:, :], None, ALU.mult).then_inc(gate_done.sem, 1)

            staggered(ve, ALL, [(5, gates), (2, norms), (1, stats), (4, elu), (5, gates_end)], R)

        @block.scalar
        def _(ac):
            ac.wait_ge(preset, 3)

            def turn(t, k, i):
                u = i % 2
                ac.wait_ge(*turned(t + 1))
                ac.wait_ge(*sc_done(t - 1))
                ac.activation(xT[:, u], p_t[:, :, :], ACT.Copy).then_inc(turn_copied.sem, 1)
                ac.wait_ge(*g_made(t - 1))
                ac.activation(mt[:, u], p_m[:, :, :], ACT.Copy).then_inc(mt_copied.sem, 1)

            def values(t, k, i):
                u = i % 2
                ac.wait_ge(*g_made(t + 1))
                ac.activation(gcol[:, :, 2 * i:2 * i + 2], p_g[:, :, :], ACT.Copy).then_inc(g_copied.sem, 1)
                ac.wait_ge(*projected(t + 1))
                ac.wait_ge(*cur_done(t))
                ac.activation(mc[:, :], p_mc[:, :], ACT.Copy).then_inc(mc_copied.sem, 1)
                ac.wait_ge(*stored[i % 4](quarter(k, i)))
                ac.activation(vp[:, i % 4, :, 0:DH], p_vu[:, 0:D].rearrange("p (h d) -> p h d", d=DH), ACT.Copy) \
                    .then_inc(v_copied.sem, 1)
                ac.wait_ge(*neg_done(t + 1))
                ac.wait_ge(*pqk_done(t))
                ac.activation(eq[:, :], neg[:, :], ACT.Exp).then_inc(eq_done.sem, 1)

            def gates(t, k, i):
                n = 2 * i + 1
                ac.wait_ge(*nms_done(t + 1))
                ac.wait_ge(*gate_done(t))
                ac.activation(ge[:, 0:n + 1], gs[:, i % 4, 0:n + 1], ACT.Exp, bias=nms[:, :], scale=float(D) ** -0.5,
                              accum_out=gsum[:, :]).then_inc(ge_done.sem, 1)

            def qk(t, k, i):
                u = i % 2
                ac.wait_ge(*qk_turned(t + 1))
                ac.wait_ge(*stored[i % 4](quarter(k, i)))
                ac.activation(qkT[:, i % 4], p_tq[:, :, :], ACT.Copy).then_inc(qk_copied.sem, 1)

            staggered(ac, ALL, [(5, gates), (3, turn), (4, values), (5, qk)], R)

        @block.tensor
        def _(pe):
            pe.wait_ge(const_in, 8 * 16)

            def turn(t, k, i):
                u = i % 2
                pe.wait_ge(*xn_done(t + 1))
                pe.wait_ge(*xr_done(t + 1))
                pe.wait_ge(*turn_copied(t))
                for c in range(2):
                    pe.transpose(p_t[:, c], xn[:, i % 4, c * P:c * P + P], ident[:, :])
                for c in range(2):
                    pe.transpose(p_t[:, 2 + c], xr[:, u, c * P:c * P + P], ident[:, :])
                pe.wait_ge(*mt_copied(t))
                for c in range(2):
                    mm = pe.matmul(p_m[:, c], xn[:, i % 4, c * P:c * P + P], savg[:, :], start=True, stop=True)
                mm.then_inc(turned.sem, 1)

            def project(t, k, i):
                u = i % 2
                pe.wait_ge(*mt_copied(t + 1))
                pe.wait_ge(*g_copied(t))
                for ci in range(2):
                    for co in range(2):
                        mm = pe.matmul(p_g[:, ci], wu_s[:, co, ci * P:ci * P + P], mt[:, u, co],
                                       start=co == 0, stop=co == 1)
                mm.then_inc(g_made.sem, 1)
                pe.wait_ge(*turn_copied(t + 1))
                pe.wait_ge(*pqk_done(t))
                for c in range(2):
                    pe.matmul(p_qk[:, :], xT[:, u, 2 + c], w_s[:, c, 0:2 * D], start=c == 0, stop=c == 1)
                pe.wait_ge(*cur_done(t))
                for c in range(2):
                    pe.matmul(p_vu[:, 0:D], xT[:, u, 2 + c], w_s[:, c, 2 * D:3 * D], start=c == 0, stop=c == 1)
                for c in range(2):
                    pe.matmul(p_vu[:, D:2 * D], xT[:, u, c], wut_s[:, c], start=c == 0, stop=c == 1)
                mm = pe.matmul(p_mc[:, :], ravg[:, :], xn[:, i % 4], start=True, stop=True)
                mm.then_inc(projected.sem, 1)

            def scores(t, k, i):
                u = i % 2
                pe.wait_ge(*g_copied(t + 1))
                pe.wait_ge(*gs_copied(t))
                for c in range(2):
                    mm = pe.matmul(p_sc[:, 0:2 * i + 1], xT[:, u, c], gcol[:, c, 0:2 * i + 1], start=c == 0, stop=c == 1)
                mm.then_inc(sc_done.sem, 1)

            def turn_qk(t, k, i):
                pe.wait_ge(*pqk_done(t + 1))
                pe.wait_ge(*qk_copied(t))
                for c in range(4):
                    mm = pe.transpose(p_tq[:, c], pqk[:, i % 4, c * P:c * P + P], ident[:, :])
                mm.then_inc(qk_turned.sem, 1)

            staggered(pe, ALL, [(5, scores), (3, turn), (4, project), (5, turn_qk)], R)


RETRIEVED = [2 * -(-(2 * i + 1) // 4) for i in range(TILES)]
R_BEFORE = [sum(RETRIEVED[:i]) for i in range(TILES)]
R_BATCH = sum(RETRIEVED)
LINKS = sum(2 * i + 1 for i in range(TILES))
LINKS_BEFORE = [sum(2 * j + 1 for j in range(i)) for i in range(TILES)]


def rounds_of(eng, body, lag):
    for i in range(TILES):
        body(0, i)
    with eng.Fori(1, B) as k:
        for i in range(TILES):
            body(k, i)
    for i in range(lag):
        body(B, i)


def behind(k, i, lag):
    i -= lag
    if i < 0:
        k, i = k - 1, i + TILES
    t = k * TILES + i
    if isinstance(k, int) and not 0 <= t < ALL:
        return None
    return t, k, i


def retrieve(nc, xn_d, qk_t, pk_d, v_d, gates_d, wo_t, causal, head_mask, eye, s1):
    with Phase(nc, "rt") as ph:
        ident = ph.sb("ident", [P, P])
        wo = ph.sb("wo", [P, 2, D])
        tri = ph.sb("tri", [P, P])
        hm = ph.sb("hm", [P, H // 2])
        qkT = ph.sb("qkT", [P, 4, 4, P])
        pkz = ph.sb("pkz", [P, 4, 2, D])
        vp = ph.sb("vp", [P, 4, H, VP])
        gt = ph.sb("gt", [P, 4, W1])
        xn = ph.sb("xn", [P, 4, D])
        qx = ph.sb("qx", [P, 2, H, P])
        asb = ph.sb("asb", [P, 2, H, P])
        st = ph.sb("st", [P, 2 * 2 * TILES, 2, H // 2, DH])
        last = ph.sb("last", [P, 2, 2, H // 2, VP])
        oT = ph.sb("oT", [P, 4, P])
        rden = ph.sb("rden", [P, H])
        dn = ph.sb("dn", [P, H])
        on = ph.sb("on", [P, H, DH])
        onT = ph.sb("onT", [P, 2, P])
        acc = ph.sb("acc", [P, 2, 2, P])
        sx = ph.sb("sx", [P, D])
        so = ph.sb("so", [P, 2, D])
        p_a = [ph.ps(f"p_a{r}", [P, 4, P]) for r in range(2)]
        p_r = [ph.ps(f"p_r{r}", [P, 4, P]) for r in range(2)]
        p_o = ph.ps("p_o", [P, 4, P])
        p_on = ph.ps("p_on", [P, H, VP])
        p_s = ph.ps("p_s", [P, 512])
        p_w = ph.ps("p_w", [P, 2, D])

        const_in = ph.sem("const_in")
        preset = ph.sem("preset")
        sig = lambda name, unit=1: ph.event(name, unit, credit=5)
        loaded = [sig(f"loaded{u}", 16 * 6) for u in range(4)]
        stored = [sig(f"stored{u}", 16) for u in range(2)]
        q_spread = sig("q_spread")
        a_made = ph.event("a_made", credit=9)
        a_masked = sig("a_masked")
        s_made = sig("s_made")
        s_copied = sig("s_copied")
        o_made = sig("o_made")
        o_copied = sig("o_copied")
        o_turned = sig("o_turned")
        dn_done = sig("dn_done")
        rden_done = sig("rden_done")
        on_done = sig("on_done")
        on_turned = sig("on_turned")
        on_copied = sig("on_copied")
        projected = sig("projected")
        r_made = sig("r_made")
        acc_link = [sig(f"acc_link{c}") for c in range(2)]
        sx_done = sig("sx_done")
        s_done = sig("s_done")
        block = ph.block()
        quarter = lambda k, i: k * (TILES // 4) + i // 4
        half = lambda k, i: k * (TILES // 2) + i // 2
        state = lambda k, n: st[:, bass.ds((k % 2) * (2 * TILES) + n, 1)].rearrange("p a c h d -> p (a c) h d")

        @block.sync
        def _(sp):
            for dst, src in ((ident[:, :], eye), (wo[:, :, :], wo_t.rearrange("(c p) n -> p c n", p=P)),
                             (tri[:, :], causal), (hm[:, :], head_mask)):
                sp.dma_start(dst, src).then_inc(const_in, 16)
            ph.give_credits(sp)
            sp.wait_ge(preset, 2)

            def body(k, i):
                if at := behind(k, i, 4):
                    t, _, j = at
                    sp.wait_ge(*s_done(t + 1))
                    sp.dma_start(s1[t], so[:, j % 2]).then_inc(stored[j % 2].sem, 16)
                if at := behind(k, i, 0):
                    t, _, j = at
                    u = j % 4
                    sp.wait_ge(*s_done(t - 3))
                    for dst, src in ((qkT[:, u], qk_t[t].rearrange("p (c t) -> p c t", t=P)),
                                     (pkz[0:SEG, u, 0], pk_d[t, 0:SEG]), (pkz[SEG:P, u, 1], pk_d[t, SEG:P]),
                                     (vp[:, u], v_d[t].rearrange("p (h d) -> p h d", d=VP)),
                                     (gt[:, u], gates_d[t]), (xn[:, u], xn_d[t])):
                        sp.dma_start(dst, src).then_inc(loaded[u].sem, 16)

            rounds_of(sp, body, 4)
            for u in range(2):
                sp.wait_ge(*stored[u](ALL // 2))

        @block.gpsimd
        def _(gp):
            gp.memset(pkz[:, :, :, :], 0.0).then_inc(preset, 1)
            gp.memset(last[:, :, :, :, :], 0.0).then_inc(preset, 1)
            gp.wait_ge(const_in, 4 * 16)

            def body(k, i):
                t = k * TILES + i
                gp.wait_ge(*loaded[i % 4](quarter(k, i) + 1))
                gp.wait_ge(*a_made(4 * t - 4))
                for c in range(2):
                    ins = gp.tensor_tensor(qx[:, i % 2, 8 * c:8 * c + 8],
                                           qkT[:, i % 4, c].unsqueeze(1).broadcast_to((P, 8, P)),
                                           hm[:, :].unsqueeze(2).broadcast_to((P, 8, P)), ALU.mult)
                ins.then_inc(q_spread.sem, 1)

            rounds_of(gp, body, 0)

        @block.tensor
        def _(pe):
            pe.wait_ge(const_in, 4 * 16)
            pe.wait_ge(preset, 2)

            def add_state(t, k, i, seg):
                pe.wait_ge(*s_copied(2 * t + seg))
                for c in range(2):
                    mm = pe.matmul(p_s[:, c * 8 * ONE:(c + 1) * 8 * ONE], pkz[:, i % 4, seg, c * P:c * P + P],
                                   vp[:, i % 4, 8 * c:8 * c + 8, 0:ONE], start=i == 0 and seg == 0 and c == 0,
                                   stop=i == TILES - 1 and seg == 1, skip_group_check=True)
                mm.then_inc(s_made.sem, 1)

            def products(t, k, i, m):
                pe.wait_ge(*a_masked(4 * t + m - 1))
                pe.matmul(p_a[m % 2][:, :, :], qkT[:, i % 4, 2 + m // 2], qx[:, i % 2, 4 * m:4 * m + 4],
                          start=True, stop=True).then_inc(a_made.sem, 1)

            def read_states(t, k, i, r):
                jb, c = r // 2, r % 2
                n = min(4, 2 * i + 1 - 4 * jb)
                pe.wait_ge(*acc_link[c](k * LINKS + LINKS_BEFORE[i] + 4 * jb))
                src = st[:, bass.ds((k % 2) * (2 * TILES) + 4 * jb, n), c]
                pe.matmul(p_r[c][:, 0:n], qkT[:, i % 4, c], src, start=True, stop=True).then_inc(r_made.sem, 1)

            def attend_tile(t, k, i):
                pe.wait_ge(*a_masked(4 * t + 4))
                pe.wait_ge(*o_copied(t))
                for g in range(4):
                    if i:
                        pe.matmul(p_o[:, g], last[:, (i - 1) % 2, g // 2, 4 * (g % 2):4 * (g % 2) + 4],
                                  qkT[:, i % 4, g // 2], start=True, stop=False, skip_group_check=True)
                    for h in range(4):
                        mm = pe.matmul(p_o[h * VP:h * VP + VP, g], vp[:, i % 4, 4 * g + h], asb[:, i % 2, 4 * g + h],
                                       start=i == 0, stop=True, skip_group_check=True)
                mm.then_inc(o_made.sem, 1)

            def body(k, i):
                if at := behind(k, i, 3):
                    t, _, j = at
                    pe.wait_ge(*on_copied(t + 1))
                    for c in range(2):
                        mm = pe.matmul(p_w[:, 1], onT[:, c], wo[:, c], start=c == 0, stop=c == 1)
                    mm.then_inc(projected.sem, 1)
                new, old = behind(k, i, 1), behind(k, i, 2)
                if old:
                    attend_tile(*old)
                if new:
                    pe.wait_ge(*q_spread(new[0] + 1))
                for m in range(4):
                    if new:
                        if m == 0:
                            pe.wait_ge(*loaded[new[2] % 4](quarter(*new[1:]) + 1))
                            add_state(*new, 0)
                        products(*new, m)
                        if m == 1:
                            add_state(*new, 1)
                    if old:
                        if m == 0:
                            pe.wait_ge(*o_copied(old[0] + 1))
                            pe.wait_ge(*on_done(old[0]))
                            for g in range(4):
                                mm = pe.transpose(p_on[:, 4 * g:4 * g + 4].rearrange("p h d -> p (h d)"),
                                                  oT[:, g], ident[:, :])
                            mm.then_inc(o_turned.sem, 1)
                        for r in range(2 * m, min(2 * m + 2, RETRIEVED[old[2]])):
                            read_states(*old, r)
                if old:
                    pe.wait_ge(*on_done(old[0] + 1))
                    pe.wait_ge(*sx_done(old[0]))
                    for c in range(2):
                        mm = pe.transpose(p_w[:, 0, c * P:c * P + P],
                                          on[:, 8 * c:8 * c + 8].rearrange("p h d -> p (h d)"), ident[:, :])
                    mm.then_inc(on_turned.sem, 1)

            rounds_of(pe, body, 3)

        @block.scalar
        def _(ac):
            def body(k, i):
                if at := behind(k, i, 2):
                    t, _, j = at
                    ac.wait_ge(*o_made(t + 1))
                    ac.wait_ge(*o_turned(t))
                    ac.activation(oT[:, :, :], p_o[:, :, :], ACT.Copy).then_inc(o_copied.sem, 1)
                    ac.wait_ge(*on_turned(t + 1))
                    ac.wait_ge(*projected(t))
                    ac.activation(onT[:, :, :], p_w[:, 0].rearrange("p (c t) -> p c t", t=P), ACT.Copy) \
                        .then_inc(on_copied.sem, 1)

            rounds_of(ac, body, 2)

        @block.vector
        def _(ve):
            ve.wait_ge(const_in, 4 * 16)
            ve.wait_ge(preset, 2)

            def keep_state(t, k, i, seg):
                ve.wait_ge(*s_made(2 * t + seg + 1))
                sums = p_s[:, 0:2 * 8 * ONE].rearrange("p (c h d) -> p c h d", c=2, d=ONE)
                same = hm[:, :].unsqueeze(1).unsqueeze(3).broadcast_to((P, 2, 8, ONE))
                if seg:
                    ve.wait_ge(*o_made(t))
                    ve.tensor_tensor(last[:, i % 2, :, :, 0:ONE], sums, same, ALU.mult)
                ve.tensor_tensor(state(k, 2 * i + seg), sums[:, :, :, 0:DH], same[:, :, :, 0:DH], ALU.mult) \
                    .then_inc(s_copied.sem, 1)

            def mask(t, k, i, m):
                ve.wait_ge(*a_made(4 * t + m + 1))
                ve.wait_ge(*o_made(t - 1))
                ve.tensor_tensor(asb[:, i % 2, 4 * m:4 * m + 4], p_a[m % 2][:, :, :],
                                 tri[:, :].unsqueeze(1).broadcast_to((P, 4, P)), ALU.mult).then_inc(a_masked.sem, 1)

            def divide(t, k, i):
                ve.wait_ge(*o_turned(t + 1))
                ve.tensor_scalar(dn[:, :], p_on[:, :, DH], RMS_EPS, None, ALU.add).then_inc(dn_done.sem, 1)
                ve.wait_ge(*dn_done(t + 1))
                ve.reciprocal(rden[:, :], dn[:, :]).then_inc(rden_done.sem, 1)
                ve.wait_ge(*rden_done(t + 1))
                ve.wait_ge(*on_turned(t))
                ve.tensor_tensor(on[:, :, :], p_on[:, :, 0:DH], rden[:, :].unsqueeze(2).broadcast_to((P, H, DH)), ALU.mult) \
                    .then_inc(on_done.sem, 1)

            def weigh(t, k, i, r):
                jb, c = r // 2, r % 2
                ve.wait_ge(*r_made(k * R_BATCH + R_BEFORE[i] + r + 1))
                for n in range(4 * jb, min(4 * jb + 4, 2 * i + 1)):
                    src, g = p_r[c][:, n - 4 * jb], gt[:, i % 4, 1 + n:2 + n]
                    if n == 0:
                        ins = ve.tensor_scalar(acc[:, i % 2, c], src, g, None, ALU.mult)
                    else:
                        ve.wait_ge(*acc_link[c](k * LINKS + LINKS_BEFORE[i] + n))
                        ins = ve.scalar_tensor_tensor(out=acc[:, i % 2, c], in0=src, scalar=g, in1=acc[:, i % 2, c],
                                                      op0=ALU.mult, op1=ALU.add)
                    ins.then_inc(acc_link[c].sem, 1)

            def finish(t, k, i):
                ve.wait_ge(*projected(t + 1))
                ve.wait_ge(*s_done(t))
                ve.tensor_tensor(sx[:, :], p_w[:, 1], xn[:, i % 4], ALU.add).then_inc(sx_done.sem, 1)
                ve.wait_ge(*sx_done(t + 1))
                ve.wait_ge(*stored[i % 2](half(k, i)))
                ve.scalar_tensor_tensor(out=so[:, i % 2], in0=sx[:, :], scalar=gt[:, i % 4, 0:1],
                                        in1=acc[:, i % 2].rearrange("p c d -> p (c d)"), op0=ALU.mult, op1=ALU.add) \
                    .then_inc(s_done.sem, 1)

            def body(k, i):
                if at := behind(k, i, 3):
                    finish(*at)
                new, old = behind(k, i, 1), behind(k, i, 2)
                for m in range(4):
                    if new:
                        if m == 0:
                            keep_state(*new, 0)
                        mask(*new, m)
                        if m == 1:
                            keep_state(*new, 1)
                    if old:
                        if m == 0:
                            divide(*old)
                        for r in range(2 * m, min(2 * m + 2, RETRIEVED[old[2]])):
                            weigh(*old, r)

            rounds_of(ve, body, 3)


def switch(nc, x1, xn_d, s1, m1, m2, mb, w1, w2, b2, ramp, eye, out):
    BLK, Y = 16, 64
    F = BLK * Y
    with Phase(nc, "sw") as ph:
        out_n = out.rearrange("b (i p) d -> (b i) p d", p=P)
        ident = ph.sb("ident", [P, P])
        m1s = ph.sb("m1s", [P, 2, Y])
        m2s = ph.sb("m2s", [Y + 1, F])
        w1s = ph.sb("w1s", [P, 2, F])
        w2s = ph.sb("w2s", [P, F // P, D])
        w1r = ph.sb("w1r", [P, 2, 2, F], F32R)
        w2r = ph.sb("w2r", [P, 2, F // P, D], F32R)
        b2s = ph.sb("b2s", [P, D])
        rank = ph.sb("rank", [P, F])
        xn = ph.sb("xn", [P, 2, D])
        xs = ph.sb("xs", [P, 2, D])
        ss = ph.sb("ss", [P, 2, D])
        xnT = ph.sb("xnT", [P, 2, 2, P])
        lrT = ph.sb("lrT", [Y + 1, 2, P])
        mx = ph.sb("mx", [P, BLK])
        top = ph.sb("top", [P, F])
        cand = ph.sb("cand", [P, F])
        mx2 = ph.sb("mx2", [P, BLK])
        pick = ph.sb("pick", [P, F])
        h = ph.sb("h", [P, F])
        hT = ph.sb("hT", [P, 2, F // P, P])
        xnr = ph.sb("xnr", [P, 2, 2, 2, P], F32R)
        hr = ph.sb("hr", [P, 2, 2, F // P, P], F32R)
        f = ph.sb("f", [P, 2, D])
        gf = ph.sb("gf", [P, D])
        sf = ph.sb("sf", [P, D])
        sg = ph.sb("sg", [P, D])
        xo = ph.sb("xo", [P, 2, D])
        p_x = ph.ps("p_x", [P, 4, P])
        p_l = ph.ps("p_l", [P, F])
        p_m = ph.ps("p_m", [P, F])
        p_h = [ph.ps(f"p_h{r}", [P, 4, P]) for r in range(2)]
        p_r = ph.ps("p_r", [P, 512])

        const_in = ph.sem("const_in")
        preset = ph.sem("preset")
        sig = lambda name, unit=1: ph.event(name, unit, credit=6)
        xn_in = [sig(f"xn_in{u}", 16) for u in range(2)]
        xs_in = [sig(f"xs_in{u}", 32) for u in range(2)]
        stored = [sig(f"stored{u}", 16) for u in range(2)]
        turned = sig("turned")
        turn_copied = sig("turn_copied")
        lr_made = sig("lr_made")
        lr_copied = sig("lr_copied")
        logits_made = sig("logits_made")
        mid_made = sig("mid_made")
        mx_done = sig("mx_done")
        top_done = sig("top_done")
        cand_done = sig("cand_done")
        mx2_done = sig("mx2_done")
        pick_done = sig("pick_done")
        h_done = sig("h_done")
        h_turned = sig("h_turned")
        h_copied = sig("h_copied")
        w_hi = ph.sem("w_hi")
        w_lo = ph.sem("w_lo")
        xn_hi = sig("xn_hi")
        xn_lo = sig("xn_lo")
        h_hi = sig("h_hi")
        h_lo = sig("h_lo")
        res_made = sig("res_made")
        f_done = sig("f_done")
        sigmoid_done = sig("sigmoid_done")
        sf_done = sig("sf_done")
        sg_done = sig("sg_done")
        x_done = sig("x_done")
        block = ph.block()
        blocks = lambda a: a.rearrange("p (j y) -> p j y", y=Y)
        spread = lambda a: a.unsqueeze(2).broadcast_to((P, BLK, Y))
        CONSTS = 8
        PARTS = ((0, 0), (0, 1), (1, 0))

        @block.sync
        def _(sp):
            for dst, src in ((ident[:, :], eye), (m1s[:, :, :], m1.rearrange("(c p) n -> p c n", p=P)),
                             (m2s[0:Y, :], m2), (m2s[Y:Y + 1, :], mb),
                             (w1s[:, :, :], w1.rearrange("(c p) n -> p c n", p=P)),
                             (w2s[:, :, :], w2.rearrange("(c p) n -> p c n", p=P)),
                             (b2s[:, :], b2.unsqueeze(0).broadcast_to((P, D))),
                             (rank[:, :], ramp.broadcast_to((P, F)))):
                sp.dma_start(dst, src).then_inc(const_in, 16)
            ph.give_credits(sp)

            def load_xn(t, k, u):
                sp.wait_ge(*turned(t - 1))
                sp.dma_start(xn[:, u], xn_d[t]).then_inc(xn_in[u].sem, 16)

            def load_xs(t, k, u):
                sp.wait_ge(*x_done(t - 1))
                sp.dma_start(xs[:, u], x1[t]).then_inc(xs_in[u].sem, 16)
                sp.dma_start(ss[:, u], s1[t]).then_inc(xs_in[u].sem, 16)

            def store(t, k, u):
                sp.wait_ge(*x_done(t + 1))
                sp.dma_start(out_n[t], xo[:, u]).then_inc(stored[u].sem, 16)

            staggered(sp, ALL, [(6, store), (4, load_xs), (0, load_xn)])
            for u in range(2):
                sp.wait_ge(*stored[u](ALL // 2))

        @block.gpsimd
        def _(gp):
            gp.memset(lrT[Y:Y + 1, :, :], 1.0).then_inc(preset, 1)
            gp.wait_ge(const_in, CONSTS * 16)
            gp.wait_ge(w_hi, 2)
            gp.tensor_tensor(w1r[:, 1], w1s[:, :, :], w1r[:, 0], ALU.subtract).then_inc(w_lo, 1)
            gp.tensor_tensor(w2r[:, 1], w2s[:, :, :], w2r[:, 0], ALU.subtract).then_inc(w_lo, 1)

            def rest_of_xn(t, k, u):
                gp.wait_ge(*xn_hi(t + 1))
                gp.tensor_tensor(xnr[:, u, 1], xnT[:, u], xnr[:, u, 0], ALU.subtract).then_inc(xn_lo.sem, 1)

            def rest_of_h(t, k, u):
                gp.wait_ge(*h_hi(t + 1))
                gp.tensor_tensor(hr[:, u, 1], hT[:, u], hr[:, u, 0], ALU.subtract).then_inc(h_lo.sem, 1)

            def scale(t, k, u):
                gp.wait_ge(*f_done(t + 1))
                gp.wait_ge(*xs_in[u](k + 1))
                gp.wait_ge(*sg_done(t))
                gp.tensor_tensor(sf[:, :], f[:, u], ss[:, u], ALU.mult).then_inc(sf_done.sem, 1)

            def rank_top(t, k, u):
                gp.wait_ge(*top_done(t + 1))
                gp.wait_ge(*pick_done(t))
                gp.tensor_tensor(cand[:, :], top[:, :], rank[:, :], ALU.mult).then_inc(cand_done.sem, 1)

            def add_x(t, k, u):
                gp.wait_ge(*sg_done(t + 1))
                gp.wait_ge(*stored[u](k))
                gp.tensor_tensor(xo[:, u], sg[:, :], xs[:, u], ALU.add).then_inc(x_done.sem, 1)

            staggered(gp, ALL, [(5, scale), (2, rank_top), (1, rest_of_xn), (3, rest_of_h), (5, add_x)])

        @block.tensor
        def _(pe):
            pe.wait_ge(const_in, CONSTS * 16)
            pe.wait_ge(preset, 1)
            pe.wait_ge(w_lo, 2)

            def turn(t, k, u):
                pe.wait_ge(*xn_in[u](k + 1))
                pe.wait_ge(*lr_copied(t))
                for c in range(2):
                    mm = pe.transpose(p_x[:, c], xn[:, u, c * P:c * P + P], ident[:, :])
                mm.then_inc(turned.sem, 1)

            def low_rank(t, k, u):
                pe.wait_ge(*turn_copied(t + 1))
                for c in range(2):
                    mm = pe.matmul(p_x[0:Y, 2], m1s[:, c], xnT[:, u, c], start=c == 0, stop=c == 1)
                mm.then_inc(lr_made.sem, 1)

            def hidden(t, k, u):
                pe.wait_ge(*lr_copied(t + 1))
                pe.wait_ge(*top_done(t))
                for n in range(0, F, 512):
                    mm = pe.matmul(p_l[:, n:n + 512], lrT[:, u], m2s[:, n:n + 512], start=True, stop=True)
                mm.then_inc(logits_made.sem, 1)
                pe.wait_ge(*h_done(t))
                pe.wait_ge(*xn_lo(t + 1))
                for n in range(0, F, 512):
                    for m, (a, b) in enumerate(PARTS):
                        for c in range(2):
                            mm = pe.matmul(p_m[:, n:n + 512], xnr[:, u, a, c], w1r[:, b, c, n:n + 512],
                                           start=m == 0 and c == 0, stop=m == 2 and c == 1)
                mm.then_inc(mid_made.sem, 1)

            def turn_hidden(t, k, u):
                pe.wait_ge(*h_done(t + 1))
                for r in range(2):
                    pe.wait_ge(*h_copied(2 * t + r - 1))
                    for c in range(4):
                        mm = pe.transpose(p_h[r][:, c], h[:, (4 * r + c) * P:(4 * r + c + 1) * P], ident[:, :])
                    mm.then_inc(h_turned.sem, 1)

            def result(t, k, u):
                pe.wait_ge(*h_lo(t + 1))
                pe.wait_ge(*f_done(t))
                for c in range(F // P):
                    for m, (a, b) in enumerate(PARTS):
                        mm = pe.matmul(p_r[:, 0:D], hr[:, u, a, c], w2r[:, b, c],
                                       start=m == 0 and c == 0, stop=m == 2 and c == F // P - 1)
                mm.then_inc(res_made.sem, 1)

            staggered(pe, ALL, [(1, turn), (2, hidden), (1, low_rank), (4, result), (3, turn_hidden)])

        @block.scalar
        def _(ac):
            ac.wait_ge(preset, 1)
            ac.wait_ge(const_in, CONSTS * 16)
            ac.activation(w1r[:, 0], w1s[:, :, :], ACT.Copy).then_inc(w_hi, 1)
            ac.activation(w2r[:, 0], w2s[:, :, :], ACT.Copy).then_inc(w_hi, 1)

            def sigmoid(t, k, u):
                ac.wait_ge(*f_done(t + 1))
                ac.wait_ge(*sg_done(t))
                ac.activation(gf[:, :], f[:, u], ACT.Sigmoid).then_inc(sigmoid_done.sem, 1)

            def copy_turned(t, k, u):
                ac.wait_ge(*turned(t + 1))
                ac.wait_ge(*mid_made(t - 1))
                ac.activation(xnT[:, u], p_x[:, 0:2], ACT.Copy).then_inc(turn_copied.sem, 1)

            def copy_low_rank(t, k, u):
                ac.wait_ge(*lr_made(t + 1))
                ac.activation(lrT[0:Y, u], p_x[0:Y, 2], ACT.Copy).then_inc(lr_copied.sem, 1)
                ac.wait_ge(*turn_copied(t + 1))
                ac.activation(xnr[:, u, 0], xnT[:, u], ACT.Copy).then_inc(xn_hi.sem, 1)

            def copy_hidden(t, k, u):
                ac.wait_ge(*res_made(t - 1))
                for r in range(2):
                    ac.wait_ge(*h_turned(2 * t + r + 1))
                    ac.activation(hT[:, u, 4 * r:4 * r + 4], p_h[r][:, :, :], ACT.Copy).then_inc(h_copied.sem, 1)
                ac.wait_ge(*h_copied(2 * t + 2))
                ac.activation(hr[:, u, 0], hT[:, u], ACT.Copy).then_inc(h_hi.sem, 1)

            staggered(ac, ALL, [(5, sigmoid), (1, copy_turned), (1, copy_low_rank), (3, copy_hidden)])

        @block.vector
        def _(ve):
            ve.wait_ge(const_in, CONSTS * 16)

            def tops(t, k, u):
                ve.wait_ge(*logits_made(t + 1))
                ve.tensor_reduce(mx[:, :], blocks(p_l[:, :]), AX.X, ALU.max).then_inc(mx_done.sem, 1)
                ve.wait_ge(*mx_done(t + 1))
                ve.wait_ge(*cand_done(t))
                ve.tensor_tensor(blocks(top[:, :]), blocks(p_l[:, :]), spread(mx[:, :]), ALU.is_equal) \
                    .then_inc(top_done.sem, 1)

            def pass_chosen(t, k, u):
                ve.wait_ge(*cand_done(t + 1))
                ve.tensor_reduce(mx2[:, :], blocks(cand[:, :]), AX.X, ALU.max).then_inc(mx2_done.sem, 1)
                ve.wait_ge(*mx2_done(t + 1))
                ve.wait_ge(*h_done(t))
                ve.tensor_tensor(blocks(pick[:, :]), blocks(cand[:, :]), spread(mx2[:, :]), ALU.is_equal) \
                    .then_inc(pick_done.sem, 1)
                ve.wait_ge(*pick_done(t + 1))
                ve.wait_ge(*mid_made(t + 1))
                ve.wait_ge(*h_turned(2 * t))
                ve.scalar_tensor_tensor(out=h[:, :], in0=p_m[:, :], scalar=0.0, in1=pick[:, :],
                                        op0=ALU.max, op1=ALU.mult).then_inc(h_done.sem, 1)

            def add_bias(t, k, u):
                ve.wait_ge(*res_made(t + 1))
                ve.wait_ge(*sf_done(t - 1))
                ve.tensor_tensor(f[:, u], p_r[:, 0:D], b2s[:, :], ALU.add).then_inc(f_done.sem, 1)

            def gate(t, k, u):
                ve.wait_ge(*sigmoid_done(t + 1))
                ve.wait_ge(*sf_done(t + 1))
                ve.wait_ge(*x_done(t))
                ve.tensor_tensor(sg[:, :], sf[:, :], gf[:, :], ALU.mult).then_inc(sg_done.sem, 1)

            staggered(ve, ALL, [(2, tops), (5, gate), (2, pass_chosen), (4, add_bias)])


def program(nc, w, out):
    def scratch(name, shape, dt=F32):
        return nc.dram_tensor(f"s_{name}", shape, dt).ap()

    qk_parts = scratch("qk_parts", (2, 3, STEPS * G * DH, T), BF16)
    v_pad = scratch("v_pad", (STEPS, T, G * VP))
    xr = scratch("xr", (ALL, P, D))
    xr_t = scratch("xr_t", (ALL, P, 2, P))
    qk_quads = qk_parts.rearrange("q c (b r) (j t) -> b j q c r t", b=B, j=TILES // 4)
    v_tiles = v_pad.rearrange("(b g) (i p) n -> b i g p n", g=G, p=P)
    project_rope(nc, w["x"], w["w_qkv"], w["gamma"], w["cos_t"], w["sin_t"], w["eye"], w["eye_bf"],
                 qk_quads, v_tiles, xr, xr_t)
    o_t = scratch("o_t", (STEPS, P, T))
    attend(nc, qk_parts, v_pad, w["eye_bf"], w["mask_q"], w["mask_k"], o_t)
    ec_t = scratch("ec_t", (ALL, P, 8, P))
    slots_t = scratch("slots_t", (8, P, 2, B, P))
    dispatch(nc, xr, xr_t, w["slots"], w["slot_gamma"], w["eye"], ec_t, slots_t)
    eo = scratch("eo", (B, 8, P, D))
    experts(nc, slots_t, w["w1"], w["b1_t"], w["w2"], w["b2"], eo)
    x1 = scratch("x1", (ALL, P, D))
    o_tiles = o_t.rearrange("(b g) p (i t) -> b g p i t", g=G, t=P)
    mix_and_gate(nc, w["x"], ec_t, eo, o_tiles, w["wo_t"], w["eye"], x1)

    xn1 = scratch("xn1", (ALL, P, D))
    qk1 = scratch("qk1", (ALL, P, 2 * D))
    pk1 = scratch("pk1", (ALL, P, D))
    v1 = scratch("v1", (ALL, P, H * VP))
    gates1 = scratch("gates1", (ALL, P, W1))
    s1 = scratch("s1", (ALL, P, D))
    project_memory(nc, x1, w["w_qkv1"], w["wu_t"], w["wu"], w["norm_w"], w["seg_avg"], w["run_avg"],
                   w["seg_mask"], w["eye"], xn1, qk1, pk1, v1, gates1)
    retrieve(nc, xn1, qk1, pk1, v1, gates1, w["wo1_t"], w["causal"], w["head_mask"], w["eye"], s1)
    switch(nc, x1, xn1, s1, w["m1"], w["m2"], w["mb"], w["f_w1"], w["f_w2"], w["f_b2"], w["ramp"], w["eye"], out)


def constants():
    import numpy as np
    inv = 1.0 / (np.float32(10000.0) ** (np.arange(0, DH, 2, dtype=np.float32) / np.float32(DH)))
    ang = np.outer(np.arange(T, dtype=np.float32), inv.astype(np.float32)).astype(np.float32)
    cos = np.concatenate([np.cos(ang), np.cos(ang)], 1).astype(np.float32)
    sin = np.concatenate([-np.sin(ang), np.sin(ang)], 1).astype(np.float32)
    eye = np.eye(P, dtype=np.float32)
    later = np.triu(np.ones((P, P), np.float32), 1) * np.float32(NEG)
    bf = mybir.dt.np(BF16)
    p = np.arange(P)
    same = p[:, None] // 64 == p[None, :] // 64
    causal = (p[:, None] <= p[None, :]).astype(np.float32)
    seg_avg = np.zeros((P, 2), np.float32)
    seg_avg[p, p // 64] = 1.0 / 64
    run_avg = np.where(same, causal / (p[None, :] % 64 + 1), 0).astype(np.float32)
    more = {"causal": causal, "seg_avg": seg_avg, "run_avg": run_avg,
            "seg_mask": np.where(p < 64, np.float32(NEG), np.float32(0))[:, None].astype(np.float32),
            "head_mask": (p[:, None] // DH == np.arange(8)[None, :]).astype(np.float32),
            "ramp": np.tile(64 - np.arange(64, dtype=np.float32), 16)[None, :]}
    return {**more, "mask_q": later.astype(bf), "mask_k": np.ascontiguousarray(later.T).astype(bf),
            "cos_t": cos, "sin_t": sin, "eye": eye, "eye_bf": eye.astype(bf)}


def kernel(**inputs):
    import numpy as np
    import concourse.bacc as bacc
    from concourse.bass_utils import run_bass_kernel_spmd

    nc = bacc.Bacc("TRN2", target_bir_lowering=False, num_devices=1)
    laid = {"x": inputs["L0_attn_x"],
            "w_qkv": np.concatenate([inputs[f"L0_attn_W{m}"].T for m in "qkv"], 1),
            "gamma": inputs["L0_ffn_norm_gamma"],
            "slots": inputs["L0_ffn_slot_embeds"], "slot_gamma": inputs["L0_ffn_slot_norm_gamma"]}
    laid.update({"w1": inputs["L0_ffn_w1"], "w2": inputs["L0_ffn_w2"], "b2": inputs["L0_ffn_b2"],
                 "b1_t": np.asarray(inputs["L0_ffn_b1"]).reshape(8, -1, P).transpose(0, 2, 1), "wo_t": inputs["L0_attn_Wo"].T})
    laid.update({"w_qkv1": np.concatenate([inputs[f"L1_attn_W{m}"].T for m in "qkv"], 1),
                 "wu_t": inputs["L1_attn_Wu"].T, "wu": inputs["L1_attn_Wu"], "wo1_t": inputs["L1_attn_Wo"].T,
                 "norm_w": inputs["L1_attn_norm_w"], "m1": inputs["L1_ffn_m1"],
                 "m2": inputs["L1_ffn_m2"].reshape(64, -1), "mb": inputs["L1_ffn_mb"].reshape(1, -1),
                 "f_w1": inputs["L1_ffn_w1"].reshape(D, -1),
                 "f_w2": inputs["L1_ffn_w2"].transpose(1, 0, 2).reshape(-1, D), "f_b2": inputs["L1_ffn_b2"]})
    laid = {n: np.ascontiguousarray(a) for n, a in laid.items()}
    laid.update(constants())
    ins = {n: nc.dram_tensor(f"in_{n}", a.shape, mybir.dt.from_np(a.dtype), kind="ExternalInput").ap()
           for n, a in laid.items()}
    out = nc.dram_tensor("out", (B, T, D), F32, kind="ExternalOutput").ap()
    program(nc, ins, out)
    r = run_bass_kernel_spmd(nc, [{f"in_{n}": a for n, a in laid.items()}], core_ids=[0])
    return r.results[0]["out"]
```
